# Optimizing a Trainium2 kernel written in Bass

```python
import numpy as np
import jax
import jax.numpy as jnp

def _softmax(x, axis=-1):
    return jax.nn.softmax(x, axis=axis)

def _gelu(x):
    return jax.nn.gelu(x, approximate=True)

def _silu(x):
    return jax.nn.silu(x)

def _sigmoid(x):
    return jax.nn.sigmoid(x)

def _layernorm(x, axis=-1, eps=1e-05):
    m = jnp.mean(x, axis=axis, keepdims=True)
    v = jnp.var(x, axis=axis, keepdims=True)
    return (x - m) / jnp.sqrt(v + eps)

def _scatter_add(tgt, idx, src, axis=0):
    return tgt.at[idx].add(src)

def _segment_sum(src, seg, n):
    return jax.ops.segment_sum(src, seg, n)
kernel_name = 'mk_seq_postln_d1_jaxref_r8_9f8425'

def setup_inputs(seed: int=0):
    np.random.seed(seed)
    _w = jnp.asarray

    def _L0_attn_setup():
        import jax, jax.numpy as jnp
        import numpy as np
        H, KV, D = (8, 2, 32)
        RD = D // 4
        ROPE_THETA = 10000.0

        def _rope_cos_sin(seq_len, dtype):
            inv_freq = 1.0 / ROPE_THETA ** (jnp.arange(0, RD, 2, dtype=jnp.float32) / RD)
            pos = jnp.arange(seq_len, dtype=jnp.float32)
            freqs = pos[:, None] * inv_freq[None, :]
            emb = jnp.concatenate([freqs, freqs], axis=-1)
            return (jnp.cos(emb).astype(dtype), jnp.sin(emb).astype(dtype))

        def _apply_partial_rope(x, cos, sin):
            x_rot, x_pass = (x[..., :RD], x[..., RD:])
            half = RD // 2
            rot = jnp.concatenate([-x_rot[..., half:], x_rot[..., :half]], axis=-1)
            x_rot = x_rot * cos[None, None] + rot * sin[None, None]
            return jnp.concatenate([x_rot, x_pass], axis=-1)
        key = jax.random.key(seed)
        ks = jax.random.split(key, 5)
        B, S, hid = (4, 256, 128)
        s = 0.02
        return {'hidden_states': jax.random.normal(ks[0], (B, S, hid), jnp.float32), 'Wq': jax.random.normal(ks[1], (hid, H * D * 2), jnp.float32) * s, 'Wk': jax.random.normal(ks[2], (hid, KV * D), jnp.float32) * s, 'Wv': jax.random.normal(ks[3], (hid, KV * D), jnp.float32) * s, 'Wo': jax.random.normal(ks[4], (H * D, hid), jnp.float32) * s}
    _L0_attn_in = _L0_attn_setup()

    def _L0_ffn_setup():
        import jax, jax.numpy as jnp
        import numpy as np
        DIM = 128
        DEPTH = 2
        HEADS = 8
        DIM_HEAD = 64
        WINDOW = 64
        INNER = HEADS * DIM_HEAD
        HID = int(DIM * 4 * 2 / 3)
        B, N = (2, 1024)
        QK_SCALE = 8.0

        def shift_token(t):
            t1, t2 = jnp.split(t, 2, axis=-1)
            t2 = jnp.pad(t2, ((0, 0), (1, 0), (0, 0)))[:, :-1]
            return jnp.concatenate([t1, t2], axis=-1)

        def l2norm(t):
            return t / jnp.clip(jnp.linalg.norm(t, axis=-1, keepdims=True), 1e-12)

        def rotate_half(x):
            x1, x2 = jnp.split(x, 2, axis=-1)
            return jnp.concatenate([-x2, x1], axis=-1)

        def rotary_xpos(q, k):
            n = q.shape[-2]
            half_idx = jnp.arange(0, DIM_HEAD, 2, dtype=jnp.float32)
            inv_freq = 1.0 / 10000.0 ** (half_idx / DIM_HEAD)
            t = jnp.arange(n, dtype=jnp.float32)
            freqs = t[:, None] * inv_freq[None, :]
            freqs = jnp.concatenate([freqs, freqs], axis=-1)
            base = (half_idx + 0.4 * DIM_HEAD) / (1.4 * DIM_HEAD)
            power = (t - n // 2) / float(WINDOW // 2)
            scale = base[None, :] ** power[:, None]
            scale = jnp.concatenate([scale, scale], axis=-1)
            cos, sin = (jnp.cos(freqs), jnp.sin(freqs))
            q = q * cos * scale + rotate_half(q) * sin * scale
            k = k * cos / scale + rotate_half(k) * sin / scale
            return (q, k)

        def local_attention(q, k, v):
            b, h, n, d = q.shape
            w = n // WINDOW
            bq = q.reshape(b, h, w, WINDOW, d) * QK_SCALE
            bk = k.reshape(b, h, w, WINDOW, d)
            bv = v.reshape(b, h, w, WINDOW, d)

            def look_around(t):
                p = jnp.pad(t, ((0, 0), (0, 0), (1, 0), (0, 0), (0, 0)))
                return jnp.concatenate([p[:, :, :w], p[:, :, 1:]], axis=3)
            bk, bv = (look_around(bk), look_around(bv))
            bt = jnp.arange(n).reshape(w, WINDOW)
            btp = jnp.pad(bt, ((1, 0), (0, 0)), constant_values=-1)
            btk = jnp.concatenate([btp[:w], btp[1:]], axis=1)
            sim = jnp.einsum('bhwid,bhwjd->bhwij', bq, bk)
            i = bt[:, :, None]
            j = btk[:, None, :]
            mask = (i < j) | (i > j + WINDOW) | (j == -1)
            sim = jnp.where(mask, -jnp.finfo(sim.dtype).max, sim)
            attn = jax.nn.softmax(sim, axis=-1)
            out = jnp.einsum('bhwij,bhwjd->bhwid', attn, bv)
            return out.reshape(b, h, n, d)

        def _layer(x, wqkv, qs, ksc, wo, lg, lb, w1, b1, w2, b2):
            b, n, _ = x.shape
            h = shift_token(x)
            qkv = h @ wqkv
            q, k, v = jnp.split(qkv, 3, axis=-1)
            to_heads = lambda t: t.reshape(b, n, HEADS, DIM_HEAD).transpose(0, 2, 1, 3)
            q, k, v = (to_heads(q), to_heads(k), to_heads(v))
            q = l2norm(q) * qs
            k = l2norm(k) * ksc
            q, k = rotary_xpos(q, k)
            o = local_attention(q, k, v)
            o = o.transpose(0, 2, 1, 3).reshape(b, n, INNER)
            x = x + o @ wo
            h = shift_token(x)
            mu = h.mean(-1, keepdims=True)
            var = h.var(-1, keepdims=True)
            h = (h - mu) / jnp.sqrt(var + 1e-05) * lg + lb
            h = h @ w1 + b1
            a, g = jnp.split(h, 2, axis=-1)
            h = a * jax.nn.gelu(g, approximate=False)
            x = x + h @ w2 + b2
            return x
        key = jax.random.key(seed)
        ks = jax.random.split(key, 6)
        return {'x': jax.random.normal(ks[0], (B, N, DIM), jnp.float32), 'wqkv': jax.random.normal(ks[1], (DEPTH, DIM, 3 * INNER), jnp.float32) * 0.02, 'q_scale': jnp.ones((DEPTH, DIM_HEAD), jnp.float32), 'k_scale': jnp.ones((DEPTH, DIM_HEAD), jnp.float32), 'wo': jax.random.normal(ks[2], (DEPTH, INNER, DIM), jnp.float32) * 0.02, 'ln_g': jnp.ones((DEPTH, DIM), jnp.float32), 'ln_b': jnp.zeros((DEPTH, DIM), jnp.float32), 'w1': jax.random.normal(ks[3], (DEPTH, DIM, 2 * HID), jnp.float32) * 0.02, 'b1': jnp.zeros((DEPTH, 2 * HID), jnp.float32), 'w2': jax.random.normal(ks[4], (DEPTH, HID, DIM), jnp.float32) * 0.02, 'b2': jnp.zeros((DEPTH, DIM), jnp.float32)}
    _L0_ffn_in = _L0_ffn_setup()
    _d = {'L0_attn_hidden_states': _L0_attn_in['hidden_states'], 'L0_attn_Wq': _L0_attn_in['Wq'], 'L0_attn_Wk': _L0_attn_in['Wk'], 'L0_attn_Wv': _L0_attn_in['Wv'], 'L0_attn_Wo': _L0_attn_in['Wo'], 'L0_ffn_wqkv': _L0_ffn_in['wqkv'], 'L0_ffn_q_scale': _L0_ffn_in['q_scale'], 'L0_ffn_k_scale': _L0_ffn_in['k_scale'], 'L0_ffn_wo': _L0_ffn_in['wo'], 'L0_ffn_ln_g': _L0_ffn_in['ln_g'], 'L0_ffn_ln_b': _L0_ffn_in['ln_b'], 'L0_ffn_w1': _L0_ffn_in['w1'], 'L0_ffn_b1': _L0_ffn_in['b1'], 'L0_ffn_w2': _L0_ffn_in['w2'], 'L0_ffn_b2': _L0_ffn_in['b2']}
    _x0 = _d['L0_attn_hidden_states']
    _d['L0_attn_hidden_states'] = jax.random.normal(jax.random.fold_in(jax.random.key(seed), 1), (8, 512, 128), dtype=_x0.dtype)
    del _x0
    return _d

def reference(L0_attn_hidden_states, L0_attn_Wq, L0_attn_Wk, L0_attn_Wv, L0_attn_Wo, L0_ffn_wqkv, L0_ffn_q_scale, L0_ffn_k_scale, L0_ffn_wo, L0_ffn_ln_g, L0_ffn_ln_b, L0_ffn_w1, L0_ffn_b1, L0_ffn_w2, L0_ffn_b2):

    def _L0_attn_ref(hidden_states, Wq, Wk, Wv, Wo):
        import jax, jax.numpy as jnp
        import numpy as np
        H, KV, D = (8, 2, 32)
        RD = D // 4
        ROPE_THETA = 10000.0

        def _rope_cos_sin(seq_len, dtype):
            inv_freq = 1.0 / ROPE_THETA ** (jnp.arange(0, RD, 2, dtype=jnp.float32) / RD)
            pos = jnp.arange(seq_len, dtype=jnp.float32)
            freqs = pos[:, None] * inv_freq[None, :]
            emb = jnp.concatenate([freqs, freqs], axis=-1)
            return (jnp.cos(emb).astype(dtype), jnp.sin(emb).astype(dtype))

        def _apply_partial_rope(x, cos, sin):
            x_rot, x_pass = (x[..., :RD], x[..., RD:])
            half = RD // 2
            rot = jnp.concatenate([-x_rot[..., half:], x_rot[..., :half]], axis=-1)
            x_rot = x_rot * cos[None, None] + rot * sin[None, None]
            return jnp.concatenate([x_rot, x_pass], axis=-1)
        B, S, _ = hidden_states.shape
        G = H // KV
        qg = hidden_states @ Wq
        q, gate = (qg[..., :H * D], qg[..., H * D:])
        k = hidden_states @ Wk
        v = hidden_states @ Wv
        q = q.reshape(B, S, H, D).transpose(0, 2, 1, 3)
        k = k.reshape(B, S, KV, D).transpose(0, 2, 1, 3)
        v = v.reshape(B, S, KV, D).transpose(0, 2, 1, 3)
        cos, sin = _rope_cos_sin(S, q.dtype)
        q = _apply_partial_rope(q, cos, sin)
        k = _apply_partial_rope(k, cos, sin)
        qg4 = q.reshape(B, KV, G, S, D)
        scores = jnp.einsum('bkgsd,bktd->bkgst', qg4, k) / jnp.sqrt(jnp.asarray(D, q.dtype))
        attn = jax.nn.softmax(scores, axis=-1)
        out = jnp.einsum('bkgst,bktd->bkgsd', attn, v)
        out = out.reshape(B, H, S, D).transpose(0, 2, 1, 3).reshape(B, S, H * D)
        out = out * jax.nn.silu(gate)
        return out @ Wo

    def _L0_ffn_ref(x, wqkv, q_scale, k_scale, wo, ln_g, ln_b, w1, b1, w2, b2):
        import jax, jax.numpy as jnp
        import numpy as np
        DIM = 128
        DEPTH = 2
        HEADS = 8
        DIM_HEAD = 64
        WINDOW = 64
        INNER = HEADS * DIM_HEAD
        HID = int(DIM * 4 * 2 / 3)
        B, N = (2, 1024)
        QK_SCALE = 8.0

        def shift_token(t):
            t1, t2 = jnp.split(t, 2, axis=-1)
            t2 = jnp.pad(t2, ((0, 0), (1, 0), (0, 0)))[:, :-1]
            return jnp.concatenate([t1, t2], axis=-1)

        def l2norm(t):
            return t / jnp.clip(jnp.linalg.norm(t, axis=-1, keepdims=True), 1e-12)

        def rotate_half(x):
            x1, x2 = jnp.split(x, 2, axis=-1)
            return jnp.concatenate([-x2, x1], axis=-1)

        def rotary_xpos(q, k):
            n = q.shape[-2]
            half_idx = jnp.arange(0, DIM_HEAD, 2, dtype=jnp.float32)
            inv_freq = 1.0 / 10000.0 ** (half_idx / DIM_HEAD)
            t = jnp.arange(n, dtype=jnp.float32)
            freqs = t[:, None] * inv_freq[None, :]
            freqs = jnp.concatenate([freqs, freqs], axis=-1)
            base = (half_idx + 0.4 * DIM_HEAD) / (1.4 * DIM_HEAD)
            power = (t - n // 2) / float(WINDOW // 2)
            scale = base[None, :] ** power[:, None]
            scale = jnp.concatenate([scale, scale], axis=-1)
            cos, sin = (jnp.cos(freqs), jnp.sin(freqs))
            q = q * cos * scale + rotate_half(q) * sin * scale
            k = k * cos / scale + rotate_half(k) * sin / scale
            return (q, k)

        def local_attention(q, k, v):
            b, h, n, d = q.shape
            w = n // WINDOW
            bq = q.reshape(b, h, w, WINDOW, d) * QK_SCALE
            bk = k.reshape(b, h, w, WINDOW, d)
            bv = v.reshape(b, h, w, WINDOW, d)

            def look_around(t):
                p = jnp.pad(t, ((0, 0), (0, 0), (1, 0), (0, 0), (0, 0)))
                return jnp.concatenate([p[:, :, :w], p[:, :, 1:]], axis=3)
            bk, bv = (look_around(bk), look_around(bv))
            bt = jnp.arange(n).reshape(w, WINDOW)
            btp = jnp.pad(bt, ((1, 0), (0, 0)), constant_values=-1)
            btk = jnp.concatenate([btp[:w], btp[1:]], axis=1)
            sim = jnp.einsum('bhwid,bhwjd->bhwij', bq, bk)
            i = bt[:, :, None]
            j = btk[:, None, :]
            mask = (i < j) | (i > j + WINDOW) | (j == -1)
            sim = jnp.where(mask, -jnp.finfo(sim.dtype).max, sim)
            attn = jax.nn.softmax(sim, axis=-1)
            out = jnp.einsum('bhwij,bhwjd->bhwid', attn, bv)
            return out.reshape(b, h, n, d)

        def _layer(x, wqkv, qs, ksc, wo, lg, lb, w1, b1, w2, b2):
            b, n, _ = x.shape
            h = shift_token(x)
            qkv = h @ wqkv
            q, k, v = jnp.split(qkv, 3, axis=-1)
            to_heads = lambda t: t.reshape(b, n, HEADS, DIM_HEAD).transpose(0, 2, 1, 3)
            q, k, v = (to_heads(q), to_heads(k), to_heads(v))
            q = l2norm(q) * qs
            k = l2norm(k) * ksc
            q, k = rotary_xpos(q, k)
            o = local_attention(q, k, v)
            o = o.transpose(0, 2, 1, 3).reshape(b, n, INNER)
            x = x + o @ wo
            h = shift_token(x)
            mu = h.mean(-1, keepdims=True)
            var = h.var(-1, keepdims=True)
            h = (h - mu) / jnp.sqrt(var + 1e-05) * lg + lb
            h = h @ w1 + b1
            a, g = jnp.split(h, 2, axis=-1)
            h = a * jax.nn.gelu(g, approximate=False)
            x = x + h @ w2 + b2
            return x
        for l in range(DEPTH):
            x = _layer(x, wqkv[l], q_scale[l], k_scale[l], wo[l], ln_g[l], ln_b[l], w1[l], b1[l], w2[l], b2[l])
        return x
    x = L0_attn_hidden_states
    x = _layernorm(x + _L0_attn_ref(x, L0_attn_Wq, L0_attn_Wk, L0_attn_Wv, L0_attn_Wo), axis=-1)
    x = _layernorm(x + _L0_ffn_ref(x, L0_ffn_wqkv, L0_ffn_q_scale, L0_ffn_k_scale, L0_ffn_wo, L0_ffn_ln_g, L0_ffn_ln_b, L0_ffn_w1, L0_ffn_b1, L0_ffn_w2, L0_ffn_b2), axis=-1)
    return x

_drawn_inputs = setup_inputs


def setup_inputs(seed=0):
    import zlib

    import numpy as np

    out = dict(_drawn_inputs(seed))
    spreads = {'L0_ffn_q_scale': (1.0, 0.6),
     'L0_ffn_k_scale': (1.0, 0.6),
     'L0_ffn_ln_g': (1.0, 0.6),
     'L0_ffn_ln_b': (0.0, 0.8),
     'L0_ffn_b1': (0.0, 0.8),
     'L0_ffn_b2': (0.0, 0.422)}
    factors = {'L0_attn_Wq': 8.0,
     'L0_attn_Wk': 8.0,
     'L0_attn_Wv': 8.0,
     'L0_attn_Wo': 8.0,
     'L0_ffn_wqkv': 3.78,
     'L0_ffn_wo': 3.773,
     'L0_ffn_w1': 6.213,
     'L0_ffn_w2': 6.124}
    for name, (base, spread) in spreads.items():
        noise = np.random.default_rng([zlib.crc32(name.encode()), seed]).standard_normal(out[name].shape)
        drawn = base * np.exp(spread * noise) if base else spread * noise
        out[name] = jnp.asarray(drawn.astype(out[name].dtype))
    for name, factor in factors.items():
        out[name] = (out[name] * factor).astype(out[name].dtype)
    return out
```

```python
from contextlib import ExitStack

import concourse.bass as bass
from concourse import mybir

ALU = mybir.AluOpType
ACT = mybir.ActivationFunctionType
F32 = mybir.dt.float32
F32R = mybir.dt.float32r
BF16 = mybir.dt.bfloat16
I32 = mybir.dt.int32
AX_X = mybir.AxisListType.X

P = 128
B, S, C = 8, 512, 128
TT = S // P
LN_EPS = 1e-5

H, KV, D = 8, 2, 32
G = H // KV
NQK = (H + KV) * D
NQKV = NQK + KV * D
RD = D // 4
SPLIT = 3 * D
SM_SCALE = float(D) ** -0.5

LAYERS, LH, LD, W = 2, 8, 64, 64
INNER = LH * LD
PAIRS = LH // 2
KW = W + P
QK_SCALE = 8.0
MASKED = -1e38
HID = 341
HT = (HID + P - 1) // P
HSIZE = [min(P, HID - P * i) for i in range(HT)]
B1A, B1G, LNG, LNB, B2, NCOLS = 0, HT, 2 * HT, 2 * HT + 1, 2 * HT + 2, 2 * HT + 3
XW = S + 2


class Signal:

    def __init__(self, sem, per, lead=1, unit=1):
        self.sem, self.per, self.lead, self.unit = sem, per, lead, unit

    def at(self, n, k):
        return n * (self.per * self.unit) + (self.lead * self.per + k) * self.unit

    def past(self, n, k, back=1):
        return n * (self.per * self.unit) + ((self.lead - back) * self.per + k) * self.unit


class Chain:

    def __init__(self, engine, sig, n, passed=None):
        self.engine, self.sig, self.n, self.count, self.passed = engine, sig, n, 0, passed

    def add(self, instruction):
        self.count += 1
        instruction.then_inc(self.sig.sem, 1)

    def settle(self):
        self.engine.wait_ge(self.sig.sem, self.sig.at(self.n, self.count))

    def settle_apart(self):
        self.settle()
        self.engine.sem_inc(self.passed, 1)

    def __call__(self, instruction):
        self.add(instruction)
        self.settle()


def rsqrt_steps(dve, link, out, x, tmp, least):
    half, y, z = tmp
    link(dve.tensor_scalar(half, x, least, None, ALU.max))
    link(dve.tensor_scalar(y.bitcast(I32), half.bitcast(I32), 1, None, ALU.logical_shift_right))
    link(dve.tensor_scalar(z.bitcast(I32), y.bitcast(I32), -1.0, 1597463007.0, ALU.mult, ALU.add))
    link(dve.tensor_scalar(half, half, -0.5, None, ALU.mult))
    src = z
    for i in range(3):
        a, b = (y, out)
        link(dve.tensor_tensor(a, src, src, ALU.mult))
        link(dve.tensor_tensor(a, a, half, ALU.mult))
        dst = out if i == 2 else z
        link(dve.scalar_tensor_tensor(out=dst, in0=a, scalar=1.5, in1=src, op0=ALU.add, op1=ALU.mult))
        src = dst


RSQRT_LINKS = 13


def layernorm_steps(dve, link, src, out, stats, mv, rstd, tmp):
    for t in range(TT):
        link.add(dve.bn_stats(stats[:, t, :], src[:, t, :]))
    link.settle_apart()
    for t in range(TT):
        link.add(dve.bn_aggr(mv[:, t, :], stats[:, t, :]))
    link.settle()
    link(dve.tensor_scalar(rstd[:, 0, :], mv[:, :, 1], LN_EPS, None, ALU.add))
    rsqrt_steps(dve, link, rstd[:, 1, :], rstd[:, 0, :], tmp, 1e-30)
    for t in range(TT):
        link.add(dve.tensor_scalar(out[:, t, :], src[:, t, :], mv[:, t, 0:1], rstd[:, 1, t:t + 1],
                                   ALU.subtract, ALU.mult))
    link.settle_apart()


LAYERNORM_LINKS = 3 * TT + 1 + RSQRT_LINKS


def global_attention_block(nc, io, xtok, xs, ident):
    with ExitStack() as ctx:
        def sb(name, shape, dt=F32):
            return ctx.enter_context(nc.sbuf_tensor(name, shape, dt))

        signals = []

        def signal(name, per, lead=1, unit=1):
            s = Signal(ctx.enter_context(nc.semaphore(name)), per, lead, unit)
            signals.append(s)
            return s

        ps = ctx.enter_context(nc.psum_tensor("ps_a", [P, 8, 512], F32))
        S_BANK, ST_BANK, GATE_BANKS, O_BANK, DEN_BANK, MISC = 0, 2, (4, 7), 5, 6, 7
        NST = 3

        wqkv = sb("a_wqkv", [P, NQKV])
        wgate = sb("a_wgate", [P, H * D])
        wo = sb("a_wo", [P, KV, C])
        rope = sb("a_rope", [P, TT, 2, RD])
        ones32 = sb("a_ones32", [P, D])
        xstage = sb("a_xstage", [P, TT, C])
        xT = sb("a_xT", [P, S])
        qkv = sb("a_qkv", [P, TT, NQKV])
        rot = sb("a_rot", [P, 2, TT, H + KV, RD])
        q3 = sb("a_q3", [P, TT, H + KV, SPLIT])
        qT = sb("a_qT", [P, H, S], F32R)
        kT = sb("a_kT", [P, KV, S], F32R)
        onesrow = sb("a_onesrow", [1, KV, S])
        nmax = sb("a_nmax", [P, H, TT])
        probs = sb("a_probs", [P, KV, G, TT, S])
        gate = sb("a_gate", [P, KV, S])
        tanh = sb("a_tanh", [P, KV, S])
        rden = sb("a_rden", [P, S])
        og = sb("a_og", [P, KV, S])
        y = sb("a_y", [P, TT, C])
        stats = sb("a_stats", [P, TT, 6])
        mv = sb("a_mv", [P, TT, 2])
        rstd = sb("a_rstd", [P, 2, TT])
        small = [sb(f"a_small{i}", [P, TT])[:] for i in range(3)]

        consts_in = ctx.enter_context(nc.semaphore("consts_in"))
        xtok_in = ctx.enter_context(nc.semaphore("xtok_in"))
        consts_set = ctx.enter_context(nc.semaphore("consts_set"))
        passed = ctx.enter_context(nc.semaphore("passed"))
        x_loaded = signal("x_loaded", 1, unit=16)
        xT_done = signal("xT_done", 1)
        xT_ready = signal("xT_ready", 1)
        qkv_done = signal("qkv_done", TT)
        qkv_ready = signal("qkv_ready", TT)
        gate_done = signal("gate_done", KV)
        tanh_ready = signal("tanh_ready", KV)
        gate_ready = signal("gate_ready", KV)
        NH = H + KV
        split_link = signal("split_link", 9)
        turned = signal("turned", NH)
        turned_act = signal("turned_act", NH // 2)
        turned_dve = signal("turned_dve", NH // 2)
        s_done = signal("s_done", 2 * H)
        max_ready = signal("max_ready", 2 * H)
        mrow_done = signal("mrow_done", H)
        mrow_ready = signal("mrow_ready", H)
        st_done = signal("st_done", H * TT)
        exp_ready = signal("exp_ready", H * TT)
        pv_done = signal("pv_done", KV * TT)
        og_link = signal("og_link", 3 * KV)
        wo_done = signal("wo_done", 1)
        norm_link = signal("norm_link", 1 + LAYERNORM_LINKS)
        xn_turned = signal("xn_turned", 1)
        xs_ready = signal("xs_ready", 2)

        block = ctx.enter_context(nc.Block())

        @block.sync
        def _(sp):
            for s in signals:
                sp.sem_inc(s.sem, s.lead * s.per * s.unit)
            x_dram = io["x"].rearrange("b (t p) c -> b p t c", p=P)
            sp.dma_start(ident[:], io["ident"]).then_inc(consts_in, 16)
            sp.dma_start(wqkv[:, 0:H * D], io["wq"][:, 0:H * D]).then_inc(consts_in, 16)
            sp.dma_start(wqkv[:, H * D:NQK], io["wk"]).then_inc(consts_in, 16)
            sp.dma_start(wqkv[:, NQK:NQKV], io["wv"]).then_inc(consts_in, 16)
            sp.dma_start(wgate[:], io["wq"][:, H * D:2 * H * D]).then_inc(consts_in, 16)
            sp.dma_start(wo[:], io["wo"].rearrange("(g p) c -> p g c", p=P)).then_inc(consts_in, 16)
            sp.dma_start(rope[:], io["rope"].rearrange("(t p) a r -> p t a r", p=P)).then_inc(consts_in, 16)
            sp.dma_start(xtok[:], io["x"].rearrange("b (t p) c -> p (b t) c", p=P)).then_inc(xtok_in, 16)
            with sp.Fori(0, B) as n:
                sp.wait_ge(xT_done.sem, xT_done.past(n, 1))
                sp.dma_start(xstage[:], x_dram[n]).then_inc(x_loaded.sem, 16)

        CONSTS = 7 * 16
        TURN_ORDER = [H, H + 1] + list(range(H))

        def turned_target(h):
            return kT[0:SPLIT, h - H, :] if h >= H else qT[0:SPLIT, h, :]


        @block.gpsimd
        def _(pool):
            pool.memset(ones32[:], 1.0).then_inc(consts_set, 1)
            pool.memset(onesrow[:], 1.0).then_inc(consts_set, 1)
            pool.memset(xs[:], 0.0).then_inc(consts_set, 1)

        SETS = 3

        def products(pe, out, lhsT, rhs):
            return pe.matmul(out, lhsT, rhs, start=True, stop=True)

        @block.tensor
        def _(pe):
            pe.wait_ge(consts_in, CONSTS)
            pe.wait_ge(consts_set, SETS)

            def project(n):
                pe.wait_ge(x_loaded.sem, x_loaded.at(n, 1))
                pe.wait_ge(xs_ready.sem, xs_ready.past(n, 2))
                for t in range(TT):
                    last = pe.transpose(ps[:, MISC, t * P:(t + 1) * P], xstage[:, t, :], ident[:])
                last.then_inc(xT_done.sem, 1)
                pe.wait_ge(xT_ready.sem, xT_ready.at(n, 1))
                pe.wait_ge(exp_ready.sem, exp_ready.past(n, H * TT))
                pe.wait_ge(max_ready.sem, max_ready.past(n, 2 * H))
                for t in range(TT):
                    products(pe, ps[:, t, 0:NQKV], xT[:, t * P:(t + 1) * P], wqkv[:]).then_inc(qkv_done.sem, 1)
                for g in range(KV):
                    products(pe, ps[:, GATE_BANKS[g], :], wgate[:, g * P:(g + 1) * P], xT[:]).then_inc(gate_done.sem, 1)

            def turn(n):
                pe.wait_ge(split_link.sem, split_link.at(n, split_link.per))
                for i, h in enumerate(TURN_ORDER):
                    if i < 4:
                        pe.wait_ge(qkv_ready.sem, qkv_ready.at(n, i + 1))
                    elif i % 2:
                        pe.wait_ge(turned_dve.sem, turned_dve.at(n, (i - 4) // 2 + 1))
                    else:
                        pe.wait_ge(turned_act.sem, turned_act.at(n, (i - 4) // 2 + 1))
                    for t in range(TT):
                        last = pe.transpose(ps[0:SPLIT, i % 4, t * P:(t + 1) * P], q3[:, t, h, :], ident[:])
                    last.then_inc(turned.sem, 1)

            def scores(n, h, half):
                if h == 0 and half == 0:
                    pe.wait_ge(turned_act.sem, turned_act.at(n, NH // 2))
                    pe.wait_ge(turned_dve.sem, turned_dve.at(n, NH // 2))
                else:
                    pe.wait_ge(max_ready.sem, max_ready.at(n, 2 * h + half))
                for t in range(2):
                    q = (2 * half + t) * P
                    last = pe.matmul(ps[:, S_BANK + t, :], qT[0:SPLIT, h, q:q + P], kT[0:SPLIT, h // G, :],
                                     start=True, stop=True)
                last.then_inc(s_done.sem, 1)

            def max_row(n, h):
                pe.wait_ge(max_ready.sem, max_ready.at(n, 2 * h + 2))
                if h == 0:
                    pe.wait_ge(gate_ready.sem, gate_ready.at(n, KV))
                else:
                    pe.wait_ge(mrow_ready.sem, mrow_ready.at(n, h))
                for t in range(TT):
                    last = pe.transpose(ps[0:1, MISC, t * P:(t + 1) * P], nmax[:, h, t:t + 1], ident[:])
                last.then_inc(mrow_done.sem, 1)

            def scores_t(n, h, tiles):
                if tiles[0] == 0:
                    pe.wait_ge(mrow_ready.sem, mrow_ready.at(n, h + 1))
                for t in tiles:
                    i = h * TT + t
                    if i >= NST:
                        pe.wait_ge(exp_ready.sem, exp_ready.at(n, i - NST + 1))
                    elif i == 2:
                        pe.wait_ge(gate_ready.sem, gate_ready.at(n, 1))
                    pe.matmul(ps[:, ST_BANK + i % NST, :], kT[0:SPLIT + 1, h // G, t * P:(t + 1) * P],
                              qT[0:SPLIT + 1, h, :], start=True, stop=True).then_inc(st_done.sem, 1)

            def weighted(n, g, t):
                if t == 0:
                    pe.wait_ge(exp_ready.sem, exp_ready.at(n, (g + 1) * G * TT))
                    if g == 0:
                        pe.wait_ge(og_link.sem, og_link.past(n, 3 * KV))
                    else:
                        pe.wait_ge(og_link.sem, og_link.at(n, 3))
                for j in range(G):
                    pe.matmul(ps[D * j:D * (j + 1), O_BANK, :], qkv[:, t, NQK + g * D:NQK + (g + 1) * D],
                              probs[:, g, j, t, :], start=(t == 0), stop=(t == TT - 1))
                for j in range(G):
                    last = pe.matmul(ps[D * j:D * (j + 1), DEN_BANK, :], ones32[:],
                                     probs[:, g, j, t, :], start=(t == 0), stop=(t == TT - 1))
                last.then_inc(pv_done.sem, 1)

            def out_project(n):
                pe.wait_ge(og_link.sem, og_link.at(n, 3 * KV))
                for t in range(TT):
                    for g in range(KV):
                        last = pe.matmul(ps[:, MISC, t * C:(t + 1) * C], og[:, g, t * P:(t + 1) * P], wo[:, g, :],
                                         start=(g == 0), stop=(g == KV - 1))
                last.then_inc(wo_done.sem, 1)
                pe.wait_ge(norm_link.sem, norm_link.at(n, norm_link.per))
                for t in range(TT):
                    last = pe.transpose(ps[:, MISC, t * P:(t + 1) * P], y[:, t, :], ident[:])
                last.then_inc(xn_turned.sem, 1)

            with pe.Fori(0, B) as n:
                project(n)
                turn(n)
                for h in range(H + 1):
                    if h < H:
                        scores(n, h, 0)
                    if h >= 1:
                        max_row(n, h - 1)
                    for t in {5: [0], 6: [1], 7: [2, 3]}.get(h, []):
                        weighted(n, 0, t)
                    if h >= 1:
                        scores_t(n, h - 1, [0, 1])
                    if h < H:
                        scores(n, h, 1)
                    if h >= 1:
                        scores_t(n, h - 1, [2, 3])
                for t in range(TT):
                    weighted(n, 1, t)
                out_project(n)

        @block.scalar
        def _(act):
            act.wait_ge(consts_set, SETS)
            act.copy(kT[SPLIT:SPLIT + 1, :, :], onesrow[:]).then_inc(consts_set, 1)
            with act.Fori(0, B) as n:
                act.wait_ge(xT_done.sem, xT_done.at(n, 1))
                act.wait_ge(gate_done.sem, gate_done.past(n, KV))
                act.copy(xT[:], ps[:, MISC, :]).then_inc(xT_ready.sem, 1)
                for t in range(TT):
                    act.wait_ge(qkv_done.sem, qkv_done.at(n, t + 1))
                    if t == 0:
                        act.wait_ge(pv_done.sem, pv_done.past(n, KV * TT))
                        act.wait_ge(split_link.sem, split_link.past(n, split_link.per))
                    act.copy(qkv[:, t, :], ps[:, t, 0:NQKV]).then_inc(qkv_ready.sem, 1)
                for g in range(KV):
                    act.wait_ge(gate_done.sem, gate_done.at(n, g + 1))
                    act.wait_ge(gate_ready.sem, gate_ready.past(n, g + 1))
                    act.activation(tanh[:, g, :], ps[:, GATE_BANKS[g], :], ACT.Tanh, scale=0.5).then_inc(tanh_ready.sem, 1)
                for i in range(0, NH, 2):
                    act.wait_ge(turned.sem, turned.at(n, i + 1))
                    act.copy(turned_target(TURN_ORDER[i]), ps[0:SPLIT, i % 4, :]).then_inc(turned_act.sem, 1)
                for h in range(H):
                    act.wait_ge(mrow_done.sem, mrow_done.at(n, h + 1))
                    act.copy(qT[SPLIT:SPLIT + 1, h, :], ps[0:1, MISC, :]).then_inc(mrow_ready.sem, 1)
                    for t in range(TT):
                        i = h * TT + t
                        act.wait_ge(st_done.sem, st_done.at(n, i + 1))
                        if h % G == 0 and t == 0:
                            act.wait_ge(pv_done.sem, pv_done.past(n, (h // G + 1) * TT))
                        act.activation(probs[:, h // G, h % G, t, :], ps[:, ST_BANK + i % NST, :], ACT.Exp,
                                       scale=SM_SCALE).then_inc(exp_ready.sem, 1)
                act.wait_ge(xn_turned.sem, xn_turned.at(n, 1))
                act.copy(xs[0:64, n, 0:S], ps[0:64, MISC, :]).then_inc(xs_ready.sem, 1)
                act.copy(xs[64:P, n, 1:S + 1], ps[64:P, MISC, :]).then_inc(xs_ready.sem, 1)

        @block.vector
        def _(dve):
            dve.wait_ge(consts_in, CONSTS)
            dve.wait_ge(xtok_in, 16)
            dve.wait_ge(consts_set, SETS + 1)
            with dve.Fori(0, B) as n:
                split, outs, norm = (Chain(dve, sig, n, passed) for sig in (split_link, og_link, norm_link))
                dve.wait_ge(qkv_ready.sem, qkv_ready.at(n, TT))
                heads = qkv[:, :, 0:NQK].rearrange("p t (h d) -> p t h d", d=D)
                cos = rope[:, :, 0:1, :].to_broadcast([P, TT, NH, RD])
                sin = rope[:, :, 1:2, :].to_broadcast([P, TT, NH, RD])
                hr = RD // 2
                split(dve.tensor_tensor(rot[:, 0], heads[:, :, :, 0:RD], cos, ALU.mult))
                split(dve.tensor_tensor(rot[:, 1, :, :, 0:hr], heads[:, :, :, hr:RD], sin[:, :, :, 0:hr], ALU.mult))
                split(dve.tensor_tensor(rot[:, 1, :, :, hr:RD], heads[:, :, :, 0:hr], sin[:, :, :, hr:RD], ALU.mult))
                split(dve.tensor_tensor(heads[:, :, :, 0:RD], rot[:, 0], rot[:, 1], ALU.add))
                dve.wait_ge(turned.sem, turned.past(n, NH))
                hi = q3[:, :, :, 0:D]
                split(dve.tensor_copy(hi.bitcast(F32R), heads))
                split(dve.tensor_copy(q3[:, :, 0:H, D:2 * D], q3[:, :, 0:H, 0:D]))
                split(dve.tensor_tensor(q3[:, :, 0:H, 2 * D:].bitcast(F32R), heads[:, :, 0:H, :], q3[:, :, 0:H, 0:D], ALU.subtract))
                split(dve.tensor_copy(q3[:, :, H:NH, 2 * D:], q3[:, :, H:NH, 0:D]))
                split(dve.tensor_tensor(q3[:, :, H:NH, D:2 * D].bitcast(F32R), heads[:, :, H:NH, :], q3[:, :, H:NH, 0:D], ALU.subtract))
                for g in range(KV):
                    dve.wait_ge(tanh_ready.sem, tanh_ready.at(n, g + 1))
                    dve.wait_ge(og_link.sem, og_link.past(n, 3 * KV))
                    dve.scalar_tensor_tensor(out=gate[:, g, :], in0=tanh[:, g, :], scalar=1.0,
                                             in1=ps[:, GATE_BANKS[g], :], op0=ALU.add,
                                             op1=ALU.mult).then_inc(gate_ready.sem, 1)
                for i in range(1, NH, 2):
                    dve.wait_ge(turned.sem, turned.at(n, i + 1))
                    dve.tensor_copy(turned_target(TURN_ORDER[i]), ps[0:SPLIT, i % 4, :]).then_inc(turned_dve.sem, 1)
                for h in range(H):
                    for half in range(2):
                        dve.wait_ge(s_done.sem, s_done.at(n, 2 * h + half + 1))
                        if h == 0 and half == 0:
                            dve.wait_ge(mrow_done.sem, mrow_done.past(n, H))
                        dve.tensor_reduce(nmax[:, h, 2 * half:2 * half + 2], ps[:, S_BANK:S_BANK + 2, :], AX_X,
                                          ALU.max, negate=True).then_inc(max_ready.sem, 1)
                for g in range(KV):
                    dve.wait_ge(pv_done.sem, pv_done.at(n, (g + 1) * TT))
                    outs(dve.reciprocal(rden[:], ps[:, DEN_BANK, :]))
                    outs(dve.tensor_tensor(rden[:], rden[:], gate[:, g, :], ALU.mult))
                    if g == 0:
                        dve.wait_ge(wo_done.sem, wo_done.past(n, 1))
                    outs(dve.scalar_tensor_tensor(out=og[:, g, :], in0=ps[:, O_BANK, :], scalar=0.5, in1=rden[:],
                                                  op0=ALU.mult, op1=ALU.mult))
                dve.wait_ge(wo_done.sem, wo_done.at(n, 1))
                dve.wait_ge(xn_turned.sem, xn_turned.past(n, 1))
                x_n = xtok[:, bass.ds(n * TT, TT), :]
                norm(dve.tensor_tensor(y[:], ps[:, MISC, :].rearrange("p (t c) -> p t c", c=C), x_n, ALU.add))
                layernorm_steps(dve, norm, y, y, stats, mv, rstd, small)
                dve.tensor_copy(x_n, y[:])


def ffn_block(nc, io, xtok, xs, ident):
    with ExitStack() as ctx:
        def sb(name, shape, dt=F32):
            return ctx.enter_context(nc.sbuf_tensor(name, shape, dt))

        signals = []

        def signal(name, per, lead=1, unit=1):
            s = Signal(ctx.enter_context(nc.semaphore(name)), per, lead, unit)
            signals.append(s)
            return s

        ps = ctx.enter_context(nc.psum_tensor("ps_b", [P, 8, 512], F32))

        wqkv = sb("b_wqkv", [P, 3 * INNER])
        wo = sb("b_wo", [P, PAIRS, C])
        w1 = sb("c_w1", [P, 2 * HID])
        w2 = sb("c_w2", [P, HT, C])
        cols = sb("c_cols", [P, NCOLS])
        qs = sb("b_qs", [P, 2, LD])
        xpos = sb("b_xpos", [P, TT, 2, 2, LD])
        tab = sb("b_tab", [P, TT, 2, 2, LD])
        mask = sb("b_mask", [P, 2, KW])
        maskb = sb("b_maskb", [P, 2, KW], BF16)
        identb = sb("b_identb", [P, P], BF16)

        hT = sb("b_hT", [P, S])
        qk = sb("b_qk", [P, TT, 2, INNER])
        rot = sb("b_rot", [P, TT, 2, INNER])
        v = sb("b_v", [P, TT + 1, INNER])
        sq = sb("b_sq", [P, 2, INNER])
        ss = sb("b_ss", [P, TT, 2, LH])
        rn = sb("b_rn", [P, TT, 2, LH])
        small = [sb(f"b_small{i}", [P, TT * 2 * LH])[:] for i in range(3)]
        qT = sb("b_qT", [P, PAIRS, S])
        kT = sb("b_kT", [P, PAIRS, W + S])
        NPB = 2
        NU = 2 * LH
        nmax = sb("b_nmax", [P, NU, 2])
        bias = sb("b_bias", [P, NU, 2])
        probs = sb("b_probs", [P, NPB, 2, 2 * P])
        den = sb("b_den", [P, NU, 2])
        rden = sb("b_rden", [P, NU, 2])
        pT = sb("b_pT", [P, NPB, 2, 2, P])
        oT = sb("b_oT", [P, PAIRS, S])

        hc = sb("c_hT", [P, S])
        hn = sb("c_hn", [P, TT, C])
        hg = sb("c_hg", [P, S])
        gelu = sb("c_gelu", [P, HT, S])
        mid = sb("c_mid", [P, HT, S])
        stats = sb("c_stats", [P, TT, 6])
        mv = sb("c_mv", [P, TT, 2])
        rstd = sb("c_rstd", [P, 2, TT])
        lnsmall = [sb(f"c_small{i}", [P, TT])[:] for i in range(3)]

        BW, CW = 4, 4
        consts_in = ctx.enter_context(nc.semaphore("b_consts_in"))
        consts_set = ctx.enter_context(nc.semaphore("b_consts_set"))
        passed = ctx.enter_context(nc.semaphore("b_passed"))
        consts_cast = ctx.enter_context(nc.semaphore("b_consts_cast"))
        bw_loaded = signal("bw_loaded", BW, unit=16)
        cw_loaded = signal("cw_loaded", CW, unit=16)
        tab_ready = signal("tab_ready", 6)
        h_ready = signal("h_ready", 1)
        proj_done = signal("proj_done", 3 * TT)
        proj_copied = signal("proj_copied", 3 * TT)
        sq_ready = signal("sq_ready", 2 * TT)
        ss_ready = signal("ss_ready", 2 * TT)
        rn_link = signal("rn_link", RSQRT_LINKS)
        rot_link = signal("rot_link", 9)
        scale_ready = signal("scale_ready", 1)
        turned = signal("b_turned", 2 * PAIRS)
        turned_act = signal("b_turned_act", PAIRS)
        turned_dve = signal("b_turned_dve", PAIRS)
        s_done = signal("b_s_done", NU)
        max_ready = signal("b_max_ready", NU)
        bias_ready = signal("b_bias_ready", NU)
        exp_ready = signal("b_exp_ready", 2 * NU)
        rden_ready = signal("b_rden_ready", NU)
        norm_ready = signal("b_norm_ready", 2 * NU)
        p_turned = signal("b_p_turned", NU)
        pT_ready = signal("b_pT_ready", NU)
        pv_done = signal("b_pv_done", NU)
        oT_ready = signal("b_oT_ready", PAIRS)
        wo_done = signal("b_wo_done", 1)
        x_added = signal("b_x_added", 2)
        hc_ready = signal("c_h_ready", 1)
        hc_turned = signal("c_h_turned", 1)
        ln_link = signal("c_ln_link", LAYERNORM_LINKS)
        hn_turned = signal("c_hn_turned", 1)
        hg_ready = signal("c_hg_ready", 1)
        up_done = signal("c_up_done", 2 * HT)
        gelu_ready = signal("c_gelu_ready", HT)
        mid_ready = signal("c_mid_ready", HT)
        down_done = signal("c_down_done", 1)
        x_out = signal("c_x_out", 2, lead=B)
        f_copied = signal("f_copied", 2)
        f_turned = signal("f_turned", 1)
        f_link = signal("f_link", 1 + LAYERNORM_LINKS)
        f_stored = signal("f_stored", 1, unit=16)

        block = ctx.enter_context(nc.Block())

        @block.sync
        def _(sp):
            for s in signals:
                sp.sem_inc(s.sem, s.lead * s.per * s.unit)
            sp.dma_start(xpos[:], io["xpos"].rearrange("(t p) a b d -> p t a b d", p=P)).then_inc(consts_in, 16)
            sp.dma_start(mask[:], io["mask"]).then_inc(consts_in, 16)
            with sp.Fori(0, LAYERS) as l:
                n_end = l * B - 1
                sp.wait_ge(wo_done.sem, wo_done.at(n_end, 1))
                sp.wait_ge(tab_ready.sem, tab_ready.past(l, 6))
                sp.dma_start(wqkv[:], io["wqkv"][l]).then_inc(bw_loaded.sem, 16)
                sp.dma_start(wo[:], io["lwo"][l].rearrange("(a p) c -> p a c", p=P)).then_inc(bw_loaded.sem, 16)
                sp.dma_start(qs[:, 0, :], io["qs"][bass.ds(l, 1), :].to_broadcast([P, LD])).then_inc(bw_loaded.sem, 16)
                sp.dma_start(qs[:, 1, :], io["ks"][bass.ds(l, 1), :].to_broadcast([P, LD])).then_inc(bw_loaded.sem, 16)
                sp.wait_ge(x_out.sem, x_out.past(n_end, 2, 0))
                sp.dma_start(w1[:], io["w1"][l]).then_inc(cw_loaded.sem, 16)
                sp.dma_start(w2[:, 0:2, :], io["w2"][l, 0:2 * P].rearrange("(a p) c -> p a c", p=P)).then_inc(cw_loaded.sem, 16)
                sp.dma_start(w2[0:HSIZE[2], 2, :], io["w2"][l, 2 * P:HID]).then_inc(cw_loaded.sem, 16)
                sp.dma_start(cols[:], io["cols"][l]).then_inc(cw_loaded.sem, 16)
            out = io["out"].rearrange("b (t p) c -> b p t c", p=P)
            with sp.Fori(0, B) as n:
                sp.wait_ge(f_link.sem, f_link.at(n, f_link.per))
                sp.dma_start(out[n], hn[:]).then_inc(f_stored.sem, 16)
            sp.wait_ge(f_stored.sem, f_stored.at(B - 1, 1))

        @block.gpsimd
        def _(pool):
            pool.memset(v[:, 0, :], 0.0).then_inc(consts_set, 1)
            pool.memset(kT[:, :, 0:W], 0.0).then_inc(consts_set, 1)
            pool.memset(probs[:], 0.0).then_inc(consts_set, 1)
            pool.wait_ge(consts_in, 32)
            pool.tensor_copy(maskb[:], mask[:]).then_inc(consts_cast, 1)
            pool.tensor_copy(identb[:], ident[:]).then_inc(consts_cast, 1)
            with pool.Fori(0, LAYERS) as l:
                pool.wait_ge(bw_loaded.sem, bw_loaded.at(l, BW))
                pool.wait_ge(rot_link.sem, rot_link.at(l * B - 1, rot_link.per))
                hd = LD // 2
                for j in range(2):
                    s = qs[:, j:j + 1, :].to_broadcast([P, TT, LD])
                    pool.tensor_tensor(tab[:, :, j, 0, :], xpos[:, :, j, 0, :], s, ALU.mult).then_inc(tab_ready.sem, 1)
                    pool.tensor_tensor(tab[:, :, j, 1, 0:hd], xpos[:, :, j, 1, 0:hd], s[:, :, hd:LD], ALU.mult).then_inc(tab_ready.sem, 1)
                    pool.tensor_tensor(tab[:, :, j, 1, hd:LD], xpos[:, :, j, 1, hd:LD], s[:, :, 0:hd], ALU.mult).then_inc(tab_ready.sem, 1)
                with pool.Fori(0, B) as b:
                    n = l * B + b
                    if True:
                        pool.wait_ge(tab_ready.sem, tab_ready.at(l, 6))
                    for u in range(NU):
                        pool.wait_ge(rden_ready.sem, rden_ready.at(n, u + 1))
                        pool.sem_inc(passed, 1)
                        for k in range(2):
                            p_u = probs[:, u % NPB, k, W:W + KW]
                            pool.tensor_scalar(p_u, p_u, rden[:, u, k:k + 1], None, ALU.mult).then_inc(norm_ready.sem, 1)

        @block.tensor
        def _(pe):
            pe.wait_ge(consts_cast, 2)
            pe.wait_ge(consts_set, 3)

            def s_bank(u):
                return u % 2

            def project(n):
                pe.wait_ge(h_ready.sem, h_ready.at(n, 1))
                for t in range(TT):
                    for j in range(3):
                        i = 3 * t + j
                        if i >= 4:
                            pe.wait_ge(proj_copied.sem, proj_copied.at(n, i - 3))
                            k = i - 4
                            if k % 3 < 2:
                                pe.wait_ge(sq_ready.sem, sq_ready.at(n, 2 * (k // 3) + k % 3 + 1))
                        elif i == 0:
                            pe.wait_ge(x_added.sem, x_added.past(n, 2))
                            pe.wait_ge(exp_ready.sem, exp_ready.past(n, 2 * NU))
                        pe.matmul(ps[:, i % 4, :], hT[:, t * P:(t + 1) * P], wqkv[:, j * INNER:(j + 1) * INNER],
                                  start=True, stop=True).then_inc(proj_done.sem, 1)

            def turn(n):
                for i in range(2 * PAIRS):
                    j, a = 1 - i // PAIRS, i % PAIRS
                    if i == 0:
                        pe.wait_ge(rot_link.sem, rot_link.at(n, rot_link.per))
                        pe.wait_ge(proj_copied.sem, proj_copied.at(n, 3 * TT))
                    if i == PAIRS:
                        pass
                    if i >= 4:
                        if i % 2:
                            pe.wait_ge(turned_dve.sem, turned_dve.at(n, (i - 4) // 2 + 1))
                        else:
                            pe.wait_ge(turned_act.sem, turned_act.at(n, (i - 4) // 2 + 1))
                    for t in range(TT):
                        last = pe.transpose(ps[:, i % 4, t * P:(t + 1) * P], qk[:, t, j, a * P:(a + 1) * P], ident[:])
                    last.then_inc(turned.sem, 1)

            def scores(n, u):
                h, tt = u // 2, 2 * (u % 2)
                a, r = h // 2, 64 * (h % 2)
                if u == 0:
                    pe.wait_ge(turned_act.sem, turned_act.at(n, PAIRS))
                    pe.wait_ge(turned_dve.sem, turned_dve.at(n, PAIRS))
                if u >= 2:
                    pe.wait_ge(exp_ready.sem, exp_ready.at(n, 2 * (u - 2) + 2))
                for k in range(2):
                    t = tt + k
                    out = ps[:, s_bank(u), k * KW:(k + 1) * KW]
                    pe.matmul(out, qT[r:r + LD, a, t * P:(t + 1) * P], kT[r:r + LD, a, t * P:t * P + KW],
                              start=True, stop=False)
                    last = pe.matmul(out, identb[:], maskb[:, 0 if t == 0 else 1, :], start=False, stop=True)
                last.then_inc(s_done.sem, 1)

            def turn_probs(n, u):
                pe.wait_ge(norm_ready.sem, norm_ready.at(n, 2 * u + 2))
                if u >= 2:
                    pe.wait_ge(pT_ready.sem, pT_ready.at(n, u - 1))
                for k in range(2):
                    for m in range(2):
                        last = pe.transpose(ps[:, 2 + u % 2, (2 * k + m) * P:(2 * k + m + 1) * P],
                                            probs[:, u % NPB, k, m * P:(m + 1) * P], ident[:])
                last.then_inc(p_turned.sem, 1)

            def weighted(n, u):
                h, tt = u // 2, 2 * (u % 2)
                a, r = h // 2, 64 * (h % 2)
                pe.wait_ge(pT_ready.sem, pT_ready.at(n, u + 1))
                if u % 4 == 0:
                    if a >= 2:
                        pe.wait_ge(oT_ready.sem, oT_ready.at(n, a - 1))
                    else:
                        pe.wait_ge(oT_ready.sem, oT_ready.past(n, PAIRS))
                for k in range(2):
                    t = tt + k
                    out = ps[r:r + LD, 4 + a % 2, t * P:(t + 1) * P]
                    pe.matmul(out, v[:, t + 1, h * LD:(h + 1) * LD], pT[:, u % NPB, k, 1, :], start=True, stop=False)
                    last = pe.matmul(out, v[64:P, t, h * LD:(h + 1) * LD], pT[64:P, u % NPB, k, 0, :],
                                     start=False, stop=True)
                last.then_inc(pv_done.sem, 1)

            def out_project(n):
                pe.wait_ge(oT_ready.sem, oT_ready.at(n, PAIRS))
                pe.wait_ge(x_added.sem, x_added.past(n, 2))
                for a in range(PAIRS):
                    last = pe.matmul(ps[:, 6, :], wo[:, a, :], oT[:, a, :], start=(a == 0), stop=(a == PAIRS - 1))
                last.then_inc(wo_done.sem, 1)

            def feed_forward(n):
                pe.wait_ge(hc_ready.sem, hc_ready.at(n, 1))
                pe.wait_ge(hg_ready.sem, hg_ready.past(n, 1))
                pe.wait_ge(ln_link.sem, ln_link.past(n, ln_link.per))
                for t in range(TT):
                    last = pe.transpose(ps[:, 0, t * P:(t + 1) * P], hc[:, t * P:(t + 1) * P], ident[:])
                last.then_inc(hc_turned.sem, 1)
                pe.wait_ge(ln_link.sem, ln_link.at(n, ln_link.per))
                for t in range(TT):
                    last = pe.transpose(ps[:, 0, t * P:(t + 1) * P], hn[:, t, :], ident[:])
                last.then_inc(hn_turned.sem, 1)
                pe.wait_ge(hg_ready.sem, hg_ready.at(n, 1))
                for i in range(HT):
                    m = HSIZE[i]
                    for a in (1, 0):
                        bank = 1 + 2 * i + a
                        pe.wait_ge(mid_ready.sem, mid_ready.past(n, i + 1))
                        pe.matmul(ps[0:m, bank, :], w1[:, a * HID + i * P:a * HID + i * P + m], hg[:],
                                  start=True, stop=True).then_inc(up_done.sem, 1)
                for i in range(HT):
                    m = HSIZE[i]
                    pe.wait_ge(mid_ready.sem, mid_ready.at(n, i + 1))
                    if i == 0:
                        pe.wait_ge(x_out.sem, x_out.past(n, 2))
                    last = pe.matmul(ps[:, 7, :], w2[0:m, i, :], mid[0:m, i, :], start=(i == 0), stop=(i == HT - 1))
                last.then_inc(down_done.sem, 1)

            with pe.Fori(0, LAYERS) as l:
                pe.wait_ge(bw_loaded.sem, bw_loaded.at(l, BW))
                pe.wait_ge(mid_ready.sem, mid_ready.at(l * B - 1, HT))
                pe.wait_ge(hg_ready.sem, hg_ready.at(l * B - 1, 1))
                pe.sem_inc(passed, 1)
                with pe.Fori(0, B) as b:
                    n = l * B + b
                    project(n)
                    turn(n)
                    for i in range(NU + 3):
                        if i < NU:
                            scores(n, i)
                        if 2 <= i < NU + 2:
                            turn_probs(n, i - 2)
                        if i >= 3:
                            weighted(n, i - 3)
                    out_project(n)
                pe.wait_ge(cw_loaded.sem, cw_loaded.at(l, CW))
                pe.wait_ge(x_added.sem, x_added.at(l * B + B - 1, 2))
                pe.wait_ge(exp_ready.sem, exp_ready.at(l * B + B - 1, 2 * NU))
                pe.sem_inc(passed, 1)
                with pe.Fori(0, B) as b:
                    feed_forward(l * B + b)
            pe.wait_ge(mid_ready.sem, mid_ready.at(LAYERS * B - 1, HT))
            with pe.Fori(0, B) as n:
                pe.wait_ge(f_copied.sem, f_copied.at(n, 2))
                pe.wait_ge(f_link.sem, f_link.past(n, f_link.per))
                for t in range(TT):
                    last = pe.transpose(ps[:, 0, t * P:(t + 1) * P], hc[:, t * P:(t + 1) * P], ident[:])
                last.then_inc(f_turned.sem, 1)

        @block.scalar
        def _(act):
            act.wait_ge(consts_set, 3)
            with act.Fori(0, LAYERS) as l:
                with act.Fori(0, B) as b:
                    n = l * B + b
                    act.wait_ge(x_out.sem, x_out.past(n, 2, B))
                    act.wait_ge(proj_done.sem, proj_done.past(n, 3 * TT))
                    act.copy(hT[:], xs[:, b, 0:S]).then_inc(h_ready.sem, 1)
                    for t in range(TT):
                        for j in range(3):
                            i = 3 * t + j
                            act.wait_ge(proj_done.sem, proj_done.at(n, i + 1))
                            if i == 0:
                                act.wait_ge(pv_done.sem, pv_done.past(n, NU))
                                act.wait_ge(turned.sem, turned.past(n, 2 * PAIRS))
                            if j < 2:
                                k = 2 * t + j
                                if k >= 2:
                                    act.wait_ge(ss_ready.sem, ss_ready.at(n, k - 1))
                                else:
                                    act.wait_ge(ss_ready.sem, ss_ready.past(n, 2 * TT))
                                act.activation(sq[:, j, :], ps[:, i % 4, :], ACT.Square).then_inc(sq_ready.sem, 1)
                                act.copy(qk[:, t, j, :], ps[:, i % 4, :]).then_inc(proj_copied.sem, 1)
                            else:
                                act.copy(v[:, t + 1, :], ps[:, i % 4, :]).then_inc(proj_copied.sem, 1)
                    for i in range(0, 2 * PAIRS, 2):
                        j, a = 1 - i // PAIRS, i % PAIRS
                        act.wait_ge(turned.sem, turned.at(n, i + 1))
                        target = kT[:, a, W:] if j else qT[:, a, :]
                        act.copy(target, ps[:, i % 4, :]).then_inc(turned_act.sem, 1)
                    for u in range(NU + 2):
                        if u < NU:
                            h, tt = u // 2, 2 * (u % 2)
                            act.wait_ge(bias_ready.sem, bias_ready.at(n, u + 1))
                            if u >= NPB:
                                act.wait_ge(p_turned.sem, p_turned.at(n, u - NPB + 1))
                            for k in range(2):
                                act.activation(probs[:, u % NPB, k, W:W + KW], ps[:, u % 2, k * KW:(k + 1) * KW],
                                               ACT.Exp, scale=rn[:, tt + k, 0, h:h + 1], bias=bias[:, u, k:k + 1],
                                               accum_out=den[:, u, k:k + 1]).then_inc(exp_ready.sem, 1)
                        if u >= 2:
                            w = u - 2
                            act.wait_ge(p_turned.sem, p_turned.at(n, w + 1))
                            if w >= NPB:
                                act.wait_ge(pv_done.sem, pv_done.at(n, w - NPB + 1))
                            act.copy(pT[:, w % NPB].rearrange("p k m q -> p (k m q)"), ps[:, 2 + w % 2, :]).then_inc(pT_ready.sem, 1)
                            if w % 4 == 3:
                                pass
                with act.Fori(0, B) as b:
                    n = l * B + b
                    act.wait_ge(x_added.sem, x_added.at(n, 2))
                    act.wait_ge(hc_turned.sem, hc_turned.past(n, 1))
                    act.copy(hc[:], xs[:, b, 0:S]).then_inc(hc_ready.sem, 1)
                    act.wait_ge(hn_turned.sem, hn_turned.at(n, 1))
                    act.wait_ge(up_done.sem, up_done.past(n, 2 * HT))
                    act.wait_ge(cw_loaded.sem, cw_loaded.at(l, CW))
                    act.activation(hg[:], ps[:, 0, :], ACT.Identity, scale=cols[:, LNG:LNG + 1],
                                   bias=cols[:, LNB:LNB + 1]).then_inc(hg_ready.sem, 1)
                    for i in range(HT):
                        m = HSIZE[i]
                        act.wait_ge(up_done.sem, up_done.at(n, 2 * i + 1))
                        act.wait_ge(mid_ready.sem, mid_ready.past(n, i + 1))
                        act.activation(gelu[0:m, i, :], ps[0:m, 2 + 2 * i, :], ACT.Gelu,
                                       bias=cols[0:m, B1G + i:B1G + i + 1]).then_inc(gelu_ready.sem, 1)
            with act.Fori(0, B) as n:
                act.wait_ge(x_out.sem, x_out.at(n + (LAYERS - 1) * B, 2))
                act.wait_ge(f_turned.sem, f_turned.past(n, 1))
                act.copy(hc[0:64, :], xs[0:64, n, 0:S]).then_inc(f_copied.sem, 1)
                act.copy(hc[64:P, :], xs[64:P, n, 1:S + 1]).then_inc(f_copied.sem, 1)

        @block.vector
        def _(dve):
            dve.wait_ge(consts_set, 3)

            def linker(sig, n):
                return Chain(dve, sig, n, passed)

            with dve.Fori(0, LAYERS) as l:
                dve.wait_ge(tab_ready.sem, tab_ready.at(l, 6))
                dve.sem_inc(passed, 1)
                with dve.Fori(0, B) as b:
                    n = l * B + b
                    for k in range(2 * TT):
                        t, j = k // 2, k % 2
                        dve.wait_ge(sq_ready.sem, sq_ready.at(n, k + 1))
                        dve.tensor_reduce(ss[:, t, j, :], sq[:, j, :].rearrange("p (h d) -> p h d", d=LD), AX_X,
                                          ALU.add).then_inc(ss_ready.sem, 1)
                    dve.wait_ge(ss_ready.sem, ss_ready.at(n, 2 * TT))
                    dve.wait_ge(exp_ready.sem, exp_ready.past(n, 2 * NU))
                    link = linker(rn_link, n)
                    rsqrt_steps(dve, link, rn[:].rearrange("p t j h -> p (t j h)"),
                                ss[:].rearrange("p t j h -> p (t j h)"), small, 1e-24)
                    dve.wait_ge(proj_copied.sem, proj_copied.at(n, 3 * TT))
                    link = linker(rot_link, n)
                    hd = LD // 2
                    for j in range(2):
                        x = qk[:, :, j, :].rearrange("p t (h d) -> p t h d", d=LD)
                        r = rot[:, :, j, :].rearrange("p t (h d) -> p t h d", d=LD)
                        cos = tab[:, :, j, 0:1, :].to_broadcast([P, TT, LH, LD])
                        sin = tab[:, :, j, 1:2, :].to_broadcast([P, TT, LH, LD])
                        link(dve.tensor_tensor(r[:, :, :, 0:hd], x[:, :, :, hd:LD], sin[:, :, :, 0:hd], ALU.mult))
                        link(dve.tensor_tensor(r[:, :, :, hd:LD], x[:, :, :, 0:hd], sin[:, :, :, hd:LD], ALU.mult))
                        link(dve.tensor_tensor(x, x, cos, ALU.mult))
                        link(dve.tensor_tensor(x, x, r, ALU.add))
                        if j:
                            nrm = rn[:, :, 1, :].rearrange("p t (h o) -> p t h o", o=1).to_broadcast([P, TT, LH, LD])
                            link(dve.tensor_tensor(x, x, nrm, ALU.mult))
                    for i in range(1, 2 * PAIRS, 2):
                        j, a = 1 - i // PAIRS, i % PAIRS
                        dve.wait_ge(turned.sem, turned.at(n, i + 1))
                        target = kT[:, a, W:] if j else qT[:, a, :]
                        dve.tensor_copy(target, ps[:, i % 4, :]).then_inc(turned_dve.sem, 1)
                    dve.tensor_scalar(rn[:, :, 0, :], rn[:, :, 0, :], QK_SCALE, None, ALU.mult).then_inc(scale_ready.sem, 1)
                    dve.wait_ge(scale_ready.sem, scale_ready.at(n, 1))
                    for u in range(NU + 4):
                        if u < NU:
                            h, tt = u // 2, 2 * (u % 2)
                            dve.wait_ge(s_done.sem, s_done.at(n, u + 1))
                            dve.tensor_reduce(nmax[:, u, :], ps[:, u % 2, 0:2 * KW].rearrange("p (k c) -> p k c", k=2),
                                              AX_X, ALU.max, negate=True).then_inc(max_ready.sem, 1)
                            dve.wait_ge(max_ready.sem, max_ready.at(n, u + 1))
                            dve.tensor_tensor(bias[:, u, :], nmax[:, u, :], rn[:, tt:tt + 2, 0, h], ALU.mult).then_inc(bias_ready.sem, 1)
                        if 1 <= u < NU + 1:
                            w = u - 1
                            dve.wait_ge(exp_ready.sem, exp_ready.at(n, 2 * w + 2))
                            if w == 0:
                                dve.wait_ge(norm_ready.sem, norm_ready.past(n, 2 * NU))
                            dve.reciprocal(rden[:, w, :], den[:, w, :]).then_inc(rden_ready.sem, 1)
                        w = u - 4
                        if w >= 0 and w % 4 == 3:
                            a = w // 4
                            dve.wait_ge(pv_done.sem, pv_done.at(n, w + 1))
                            if a == 0:
                                dve.wait_ge(wo_done.sem, wo_done.past(n, 1))
                            dve.tensor_copy(oT[:, a, :], ps[:, 4 + a % 2, :]).then_inc(oT_ready.sem, 1)
                    dve.wait_ge(wo_done.sem, wo_done.at(n, 1))
                    for r in range(2):
                        x = xs[64 * r:64 * r + 64, b, r:r + S]
                        dve.tensor_tensor(x, ps[64 * r:64 * r + 64, 6, :], x, ALU.add).then_inc(x_added.sem, 1)
                with dve.Fori(0, B) as b:
                    n = l * B + b
                    dve.wait_ge(hc_turned.sem, hc_turned.at(n, 1))
                    dve.wait_ge(hn_turned.sem, hn_turned.past(n, 1))
                    layernorm_steps(dve, linker(ln_link, n), ps[:, 0, :].rearrange("p (t c) -> p t c", c=C), hn, stats,
                                    mv, rstd, lnsmall)
                    for i in range(HT):
                        m = HSIZE[i]
                        dve.wait_ge(gelu_ready.sem, gelu_ready.at(n, i + 1))
                        dve.wait_ge(up_done.sem, up_done.at(n, 2 * i + 2))
                        dve.wait_ge(down_done.sem, down_done.past(n, 1))
                        dve.scalar_tensor_tensor(out=mid[0:m, i, :], in0=ps[0:m, 1 + 2 * i, :], scalar=cols[0:m, B1A + i:B1A + i + 1],
                                                 in1=gelu[0:m, i, :], op0=ALU.add, op1=ALU.mult).then_inc(mid_ready.sem, 1)
                    dve.wait_ge(down_done.sem, down_done.at(n, 1))
                    dve.wait_ge(hc_ready.sem, hc_ready.at(n, 1))
                    for r in range(2):
                        rows = slice(64 * r, 64 * r + 64)
                        x = xs[rows, b, r:r + S]
                        dve.scalar_tensor_tensor(out=x, in0=ps[rows, 7, :], scalar=cols[rows, B2:B2 + 1], in1=x,
                                                 op0=ALU.add, op1=ALU.add).then_inc(x_out.sem, 1)
            with dve.Fori(0, B) as n:
                dve.wait_ge(f_turned.sem, f_turned.at(n, 1))
                dve.wait_ge(f_stored.sem, f_stored.past(n, 1))
                link = linker(f_link, n)
                link(dve.tensor_tensor(hn[:], ps[:, 0, :].rearrange("p (t c) -> p t c", c=C),
                                       xtok[:, bass.ds(n * TT, TT), :], ALU.add))
                layernorm_steps(dve, link, hn, hn, stats, mv, rstd, lnsmall)


def build(nc, io):
    with ExitStack() as ctx:
        ident = ctx.enter_context(nc.sbuf_tensor("ident_sb", [P, P], F32))
        xtok = ctx.enter_context(nc.sbuf_tensor("xtok", [P, B * TT, C], F32))
        xs = ctx.enter_context(nc.sbuf_tensor("xs", [P, B, XW], F32))
        global_attention_block(nc, io, xtok, xs, ident)
        ffn_block(nc, io, xtok, xs, ident)


def shape_constants():
    import numpy as np
    f = np.float32
    inv = (f(1.0) / f(10000.0) ** (np.arange(0, RD, 2, dtype=f) / f(RD))).astype(f)
    fr = np.arange(S, dtype=f)[:, None] * inv[None, :]
    c, s = np.cos(fr), np.sin(fr)
    rope = np.stack([np.concatenate([c, c], 1), np.concatenate([-s, s], 1)], 1).astype(f)
    half = np.arange(0, LD, 2, dtype=f)
    inv = (f(1.0) / f(10000.0) ** (half / f(LD))).astype(f)
    t = np.arange(S, dtype=f)
    fr = t[:, None] * inv[None, :]
    base = (half + f(0.4 * LD)) / f(1.4 * LD)
    power = (t - f(S // 2)) / f(W // 2)
    scale = (base[None, :] ** power[:, None]).astype(f)
    c, s = np.cos(fr), np.sin(fr)
    two = lambda a, b: np.concatenate([a, b], 1)
    q = np.stack([two(c * scale, c * scale), two(-s * scale, s * scale)], 1)
    k = np.stack([two(c / scale, c / scale), two(-s / scale, s / scale)], 1)
    xpos = np.stack([q, k], 1).astype(f)
    i, j = np.arange(P)[:, None], np.arange(KW)[None, :] - W
    seen = (j <= i) & (j >= i - W)
    mask = np.stack([np.where(seen & (j >= 0), 0, MASKED), np.where(seen, 0, MASKED)], 1).astype(f)
    return {"rope": rope, "xpos": xpos, "mask": mask, "ident": np.eye(P, dtype=f)}


def kernel(**inputs):
    import numpy as np
    import concourse.bacc as bacc
    from concourse.bass_utils import run_bass_kernel_spmd

    names = {
        "x": "L0_attn_hidden_states", "wq": "L0_attn_Wq", "wk": "L0_attn_Wk", "wv": "L0_attn_Wv", "wo": "L0_attn_Wo",
        "wqkv": "L0_ffn_wqkv", "qs": "L0_ffn_q_scale", "ks": "L0_ffn_k_scale", "lwo": "L0_ffn_wo",
        "w1": "L0_ffn_w1", "w2": "L0_ffn_w2",
    }
    arrays = {short: np.ascontiguousarray(inputs[name]) for short, name in names.items()}
    cols = np.zeros((LAYERS, P, NCOLS), np.float32)
    b1 = np.asarray(inputs["L0_ffn_b1"])
    for first, offset in ((B1A, 0), (B1G, HID)):
        for i, m in enumerate(HSIZE):
            cols[:, 0:m, first + i] = b1[:, offset + P * i:offset + P * i + m]
    for at, name in ((LNG, "L0_ffn_ln_g"), (LNB, "L0_ffn_ln_b"), (B2, "L0_ffn_b2")):
        cols[:, :, at] = np.asarray(inputs[name])
    arrays["cols"] = cols
    arrays.update(shape_constants())
    nc = bacc.Bacc("TRN2", target_bir_lowering=False, num_devices=1)
    io = {k: nc.dram_tensor("in_" + k, a.shape, mybir.dt.from_np(a.dtype), kind="ExternalInput").ap()
          for k, a in arrays.items()}
    io["out"] = nc.dram_tensor("out_x", (B, S, C), F32, kind="ExternalOutput").ap()
    build(nc, io)
    r = run_bass_kernel_spmd(nc, [{"in_" + k: a for k, a in arrays.items()}], core_ids=[0])
    return r.results[0]["out_x"]
```

```python
from contextlib import ExitStack

import concourse.bass as bass
from concourse import mybir

ALU = mybir.AluOpType
ACT = mybir.ActivationFunctionType
F32 = mybir.dt.float32
F32R = mybir.dt.float32r
BF16 = mybir.dt.bfloat16
I32 = mybir.dt.int32
AX_X = mybir.AxisListType.X

P = 128
B, S, C = 8, 512, 128
TT = S // P
LN_EPS = 1e-5

H, KV, D = 8, 2, 32
G = H // KV
NQK = (H + KV) * D
NQKV = NQK + KV * D
RD = D // 4
SPLIT = 3 * D
SM_SCALE = float(D) ** -0.5

LAYERS, LH, LD, W = 2, 8, 64, 64
INNER = LH * LD
PAIRS = LH // 2
KW = W + P
QK_SCALE = 8.0
MASKED = -1e38
HID = 341
HT = (HID + P - 1) // P
HSIZE = [min(P, HID - P * i) for i in range(HT)]
B1A, B1G, LNG, LNB, B2, NCOLS = 0, HT, 2 * HT, 2 * HT + 1, 2 * HT + 2, 2 * HT + 3
XW = S + 2


class Signal:

    def __init__(self, sem, per, lead=1, unit=1):
        self.sem, self.per, self.lead, self.unit = sem, per, lead, unit

    def at(self, n, k):
        return n * (self.per * self.unit) + (self.lead * self.per + k) * self.unit

    def past(self, n, k, back=1):
        return n * (self.per * self.unit) + ((self.lead - back) * self.per + k) * self.unit


class Chain:

    def __init__(self, engine, sig, n, passed=None):
        self.engine, self.sig, self.n, self.count, self.passed = engine, sig, n, 0, passed

    def add(self, instruction):
        self.count += 1
        instruction.then_inc(self.sig.sem, 1)

    def settle(self):
        self.engine.wait_ge(self.sig.sem, self.sig.at(self.n, self.count))

    def settle_apart(self):
        self.settle()
        self.engine.sem_inc(self.passed, 1)

    def __call__(self, instruction):
        self.add(instruction)
        self.settle()


def rsqrt_step(dve, chain, k, out, x, tmp, least):
    half, y, z = tmp
    chain.settle()
    if k == 0:
        step = dve.tensor_scalar(half, x, least, None, ALU.max)
    elif k == 1:
        step = dve.tensor_scalar(y.bitcast(I32), half.bitcast(I32), 1, None, ALU.logical_shift_right)
    elif k == 2:
        step = dve.tensor_scalar(z.bitcast(I32), y.bitcast(I32), -1.0, 1597463007.0, ALU.mult, ALU.add)
    elif k == 3:
        step = dve.tensor_scalar(half, half, -0.5, None, ALU.mult)
    elif (k - 4) % 3 == 0:
        step = dve.tensor_tensor(y, z, z, ALU.mult)
    elif (k - 4) % 3 == 1:
        step = dve.tensor_tensor(y, y, half, ALU.mult)
    else:
        step = dve.scalar_tensor_tensor(out=out if k == RSQRT_LINKS - 1 else z, in0=y, scalar=1.5, in1=z,
                                        op0=ALU.add, op1=ALU.mult)
    chain.add(step)


def rsqrt_steps(dve, chain, out, x, tmp, least):
    for k in range(RSQRT_LINKS):
        rsqrt_step(dve, chain, k, out, x, tmp, least)
    chain.settle()


RSQRT_LINKS = 4 + 3 * 3


def layernorm_parts(dve, link, src, out, stats, mv, rstd, tmp):
    def statistics():
        for t in range(TT):
            link.add(dve.bn_stats(stats[:, t, :], src[:, t, :]))
        link.settle_apart()
        for t in range(TT):
            link.add(dve.bn_aggr(mv[:, t, :], stats[:, t, :]))

    def deviation():
        link.settle()
        link(dve.tensor_scalar(rstd[:, 0, :], mv[:, :, 1], LN_EPS, None, ALU.add))
        rsqrt_steps(dve, link, rstd[:, 1, :], rstd[:, 0, :], tmp, 1e-30)

    def result():
        for t in range(TT):
            link.add(dve.tensor_scalar(out[:, t, :], src[:, t, :], mv[:, t, 0:1], rstd[:, 1, t:t + 1],
                                       ALU.subtract, ALU.mult))
        link.settle_apart()

    return statistics, deviation, result


def layernorm_steps(*args):
    for part in layernorm_parts(*args):
        part()


LAYERNORM_LINKS = 3 * TT + 1 + RSQRT_LINKS


def global_attention_block(nc, io, xtok, xs, ident):
    with ExitStack() as ctx:
        def sb(name, shape, dt=F32):
            return ctx.enter_context(nc.sbuf_tensor(name, shape, dt))

        signals = []

        def signal(name, per, lead=1, unit=1):
            s = Signal(ctx.enter_context(nc.semaphore(name)), per, lead, unit)
            signals.append(s)
            return s

        ps = ctx.enter_context(nc.psum_tensor("ps_a", [P, 8, 512], F32))
        S_BANK, ST_BANK, HEAD_BANK, O_BANK, DEN_BANK, TAIL_BANK = 0, 2, 4, 5, 6, 7
        NST = 2
        NH = H + KV

        HEAD = [("xT", 0)] + [("qkv", t) for t in range(TT)] + [("gate", g) for g in range(KV)]
        HEAD += [("turn", H + g) for g in range(KV)] + [("turn", h) for h in range(H)]
        NP = len(HEAD)
        PIECE = {piece: k for k, piece in enumerate(HEAD)}
        FIRST_TURN = PIECE["turn", H]
        SLOTS = {
            0: [(0, ("turn", 6)), None, (0, ("turn", 7))],
            1: [(1, ("xT", 0)), (1, ("qkv", 0)), (1, ("qkv", 1))],
            2: [(1, ("qkv", 2)), (1, ("qkv", 3)), None],
            3: [(1, ("gate", 0)), None, None],
            4: [(1, ("gate", 1)), None, None],
            5: [(1, ("turn", H)), (1, ("turn", H + 1)), (1, ("turn", 0))],
            6: [(1, ("turn", 1)), (1, ("turn", 2)), (1, ("turn", 3))],
            7: [(1, ("turn", 4)), (1, ("turn", 5)), None],
        }
        WEIGHTED = {5: (0, 0, [0]), 6: (0, 0, [1]), 7: (0, 0, [2]), 0: (1, 0, [3]),
                    1: (1, 1, [0, 1]), 2: (1, 1, [2]), 3: (1, 1, [3])}
        OUT_COPY = {0: 0, 3: 1}

        wqkv = sb("a_wqkv", [P, NQKV])
        wgate = sb("a_wgate", [P, H * D])
        wo = sb("a_wo", [P, KV, C])
        rope = sb("a_rope", [P, TT, 2, RD])
        ones32 = sb("a_ones32", [P, D])
        xstage = sb("a_xstage", [P, TT, C])
        xT = [sb(f"a_xT{p}", [P, S]) for p in range(2)]
        qkv = [sb(f"a_qkv{p}", [P, TT, NQKV]) for p in range(2)]
        rot = sb("a_rot", [P, 2, TT, NH, RD])
        q3 = sb("a_q3", [P, TT, NH, SPLIT])
        qT = sb("a_qT", [P, H, S], F32R)
        kT = [sb(f"a_kT{p}", [P, KV, S], F32R) for p in range(2)]
        v = sb("a_v", [P, KV, TT, D])
        nmax = sb("a_nmax", [P, H, TT])
        probs = sb("a_probs", [P, KV, G, TT, S])
        gate = [sb(f"a_gate{p}", [P, KV, S]) for p in range(2)]
        tanh = sb("a_tanh", [P, S])
        outs = sb("a_outs", [P, S])
        dens = sb("a_dens", [P, S])
        rden = sb("a_rden", [P, S])
        og = sb("a_og", [P, KV, S])
        y = sb("a_y", [P, TT, C])
        stats = sb("a_stats", [P, TT, 6])
        mv = sb("a_mv", [P, TT, 2])
        rstd = sb("a_rstd", [P, 2, TT])
        small = [sb(f"a_small{i}", [P, TT])[:] for i in range(3)]

        consts_in = ctx.enter_context(nc.semaphore("consts_in"))
        xtok_in = ctx.enter_context(nc.semaphore("xtok_in"))
        consts_set = ctx.enter_context(nc.semaphore("consts_set"))
        passed = ctx.enter_context(nc.semaphore("passed"))
        x_loaded = signal("x_loaded", 1, unit=16)
        head_done = signal("head_done", NP)
        head_read = signal("head_read", NP)
        gate_ready = signal("gate_ready", KV)
        split_link = signal("split_link", 7)
        dup_ready = signal("dup_ready", 2)
        s_done = signal("s_done", 2 * H)
        max_ready = signal("max_ready", 2 * H)
        mrow_done = signal("mrow_done", H)
        mrow_ready = signal("mrow_ready", H)
        st_done = signal("st_done", H * TT)
        exp_ready = signal("exp_ready", H * TT)
        pv_done = signal("pv_done", KV * TT)
        outs_ready = signal("outs_ready", 2 * KV)
        rden_link = signal("rden_link", 3 * KV, lead=2)
        v_ready = signal("v_ready", KV, lead=2)
        og_ready = signal("og_ready", KV)
        wo_done = signal("wo_done", 1)
        norm_link = signal("norm_link", 2 + LAYERNORM_LINKS)
        xn_turned = signal("xn_turned", 1)
        xs_ready = signal("xs_ready", 2)

        def over_batches(engine, head, batch, drain):
            head(0, 0)
            batch(0, 0, cur=True, nxt=True, prev=False)
            with engine.Fori(0, (B - 2) // 2) as m:
                for i in range(2):
                    batch(m * 2 + (i + 1), 1 - i, cur=True, nxt=True, prev=True)
            batch(B - 1, 1, cur=True, nxt=False, prev=True)
            drain(B, 0, cur=False, nxt=False, prev=True)

        def before(n, p, j, cur, prev):
            return (n, p, j - 1, cur) if j else (n - 1, 1 - p, H - 1, prev)

        def slot_piece(n, p, j, slot, cur, nxt):
            if SLOTS[j][slot] is None:
                return None
            ahead, piece = SLOTS[j][slot]
            if not (nxt if ahead else cur):
                return None
            return n + ahead, (p + ahead) % 2, piece

        def first_pieces():
            return [x for x in HEAD if x not in (("turn", 6), ("turn", 7))]

        block = ctx.enter_context(nc.Block())

        @block.sync
        def _(sp):
            for s in signals:
                sp.sem_inc(s.sem, s.lead * s.per * s.unit)
            x_dram = io["x"].rearrange("b (t p) c -> b p t c", p=P)
            sp.dma_start(xstage[:], x_dram[0]).then_inc(x_loaded.sem, 16)
            sp.dma_start(ident[:], io["ident"]).then_inc(consts_in, 16)
            sp.dma_start(wqkv[:, 0:H * D], io["wq"][:, 0:H * D]).then_inc(consts_in, 16)
            sp.dma_start(wqkv[:, H * D:NQK], io["wk"]).then_inc(consts_in, 16)
            sp.dma_start(wqkv[:, NQK:NQKV], io["wv"]).then_inc(consts_in, 16)
            sp.dma_start(wgate[:], io["wq"][:, H * D:2 * H * D]).then_inc(consts_in, 16)
            sp.dma_start(rope[:], io["rope"].rearrange("(t p) a r -> p t a r", p=P)).then_inc(consts_in, 16)
            sp.dma_start(wo[:], io["wo"].rearrange("(g p) c -> p g c", p=P)).then_inc(consts_in, 16)
            sp.dma_start(xtok[:], io["x"].rearrange("b (t p) c -> p (b t) c", p=P)).then_inc(xtok_in, 16)
            with sp.Fori(0, B - 1) as m:
                sp.wait_ge(head_done.sem, head_done.at(m, 1))
                sp.dma_start(xstage[:], x_dram[m + 1]).then_inc(x_loaded.sem, 16)

        CONSTS = 7 * 16
        SETS = 4

        @block.gpsimd
        def _(pool):
            pool.memset(ones32[:], 1.0).then_inc(consts_set, 1)
            for p in range(2):
                pool.wait_ge(consts_set, p + 1)
                pool.memset(kT[p][SPLIT:SPLIT + 1, :, :].bitcast(F32), 1.0).then_inc(consts_set, 1)
            pool.wait_ge(consts_set, SETS - 1)
            pool.memset(xs[:], 0.0).then_inc(consts_set, 1)

            def duplicate(n):
                pool.wait_ge(split_link.sem, split_link.at(n, 5))
                pool.sem_inc(passed, 1)
                pool.tensor_copy(q3[:, :, 0:H, D:2 * D], q3[:, :, 0:H, 0:D]).then_inc(dup_ready.sem, 1)
                pool.tensor_copy(q3[:, :, H:NH, 2 * D:], q3[:, :, H:NH, 0:D]).then_inc(dup_ready.sem, 1)

            def gated(n, g):
                pool.wait_ge(rden_link.sem, rden_link.at(n, 3 * g + 3))
                pool.wait_ge(wo_done.sem, wo_done.past(n, 1))
                pool.tensor_tensor(og[:, g, :], outs[:], rden[:], ALU.mult).then_inc(og_ready.sem, 1)

            def keep_v(n, p, g):
                pool.wait_ge(pv_done.sem, pv_done.past(n, (g + 1) * TT))
                pool.wait_ge(head_read.sem, head_read.at(n, PIECE["qkv", TT - 1] + 1))
                pool.sem_inc(passed, 1)
                pool.tensor_copy(v[:, g], qkv[p][:, :, NQK + g * D:NQK + (g + 1) * D]).then_inc(v_ready.sem, 1)

            def batch(n, p, cur, nxt, prev):
                if prev:
                    gated(n - 1, 0)
                if cur:
                    keep_v(n, p, 0)
                if nxt:
                    duplicate(n + 1)
                if prev:
                    gated(n - 1, 1)
                if cur:
                    keep_v(n, p, 1)

            over_batches(pool, lambda n, p: duplicate(n), batch, batch)

        @block.tensor
        def _(pe):
            pe.wait_ge(consts_in, CONSTS)
            pe.wait_ge(consts_set, SETS)

            def piece(n, p, name):
                kind, i = name
                k = PIECE[name]
                bank = ps[:, HEAD_BANK, :]
                if k:
                    pe.wait_ge(head_read.sem, head_read.at(n, k))
                    if HEAD[k - 1][0] == "gate":
                        pe.wait_ge(gate_ready.sem, gate_ready.at(n, HEAD[k - 1][1] + 1))
                else:
                    pe.wait_ge(head_read.sem, head_read.past(n, NP))
                if kind == "xT":
                    pe.wait_ge(x_loaded.sem, x_loaded.at(n, 1))
                    for t in range(TT):
                        last = pe.transpose(bank[:, t * P:(t + 1) * P], xstage[:, t, :], ident[:])
                elif kind == "qkv":
                    last = pe.matmul(bank[:, 0:NQKV], xT[p][:, i * P:(i + 1) * P], wqkv[:], start=True, stop=True)
                elif kind == "gate":
                    last = pe.matmul(bank, wgate[:, i * P:(i + 1) * P], xT[p][:], start=True, stop=True)
                else:
                    if k == FIRST_TURN:
                        pe.wait_ge(split_link.sem, split_link.at(n, split_link.per))
                        pe.wait_ge(dup_ready.sem, dup_ready.at(n, 2))
                    for t in range(TT):
                        last = pe.transpose(ps[0:SPLIT, HEAD_BANK, t * P:(t + 1) * P], q3[:, t, i, :], ident[:])
                last.then_inc(head_done.sem, 1)

            def scores(n, p, h, half):
                if h == 0 and half == 0:
                    pe.wait_ge(head_read.sem, head_read.at(n, PIECE["turn", 5] + 1))
                    pe.wait_ge(max_ready.sem, max_ready.past(n, 2 * H))
                else:
                    pe.wait_ge(max_ready.sem, max_ready.at(n, 2 * h + half))
                if h >= 6 and half == 0:
                    pe.wait_ge(head_read.sem, head_read.at(n, PIECE["turn", h] + 1))
                for t in range(2):
                    q = (2 * half + t) * P
                    last = pe.matmul(ps[:, S_BANK + t, :], qT[0:SPLIT, h, q:q + P], kT[p][0:SPLIT, h // G, :],
                                     start=True, stop=True)
                last.then_inc(s_done.sem, 1)

            def max_row(n, h):
                pe.wait_ge(max_ready.sem, max_ready.at(n, 2 * h + 2))
                pe.wait_ge(mrow_ready.sem, mrow_ready.at(n, h))
                if h == 5:
                    pe.wait_ge(norm_link.sem, norm_link.past(n, 1))
                if h == 7:
                    pe.wait_ge(xs_ready.sem, xs_ready.past(n, 2))
                for t in range(TT):
                    last = pe.transpose(ps[0:1, TAIL_BANK, t * P:(t + 1) * P], nmax[:, h, t:t + 1], ident[:])
                last.then_inc(mrow_done.sem, 1)

            def scores_t(n, p, h, tiles):
                if tiles[0] == 0:
                    pe.wait_ge(mrow_ready.sem, mrow_ready.at(n, h + 1))
                for t in tiles:
                    i = h * TT + t
                    pe.wait_ge(exp_ready.sem, exp_ready.at(n, i - NST + 1))
                    pe.matmul(ps[:, ST_BANK + i % NST, :], kT[p][0:SPLIT + 1, h // G, t * P:(t + 1) * P],
                              qT[0:SPLIT + 1, h, :], start=True, stop=True).then_inc(st_done.sem, 1)

            def weighted(n, p, g, t):
                if t == 0:
                    pe.wait_ge(exp_ready.sem, exp_ready.at(n, (g + 1) * G * TT))
                    pe.wait_ge(outs_ready.sem, outs_ready.at(n, 2 * g))
                    pe.wait_ge(v_ready.sem, v_ready.at(n, g + 1))
                for j in range(G):
                    pe.matmul(ps[D * j:D * (j + 1), O_BANK, :], v[:, g, t, :],
                              probs[:, g, j, t, :], start=(t == 0), stop=(t == TT - 1))
                for j in range(G):
                    last = pe.matmul(ps[D * j:D * (j + 1), DEN_BANK, :], ones32[:],
                                     probs[:, g, j, t, :], start=(t == 0), stop=(t == TT - 1))
                last.then_inc(pv_done.sem, 1)

            def out_project(n):
                pe.wait_ge(og_ready.sem, og_ready.at(n, KV))
                pe.wait_ge(mrow_ready.sem, mrow_ready.at(n + 1, 5) if n_has_next(n) else mrow_ready.at(n, H))
                for t in range(TT):
                    for g in range(KV):
                        last = pe.matmul(ps[:, TAIL_BANK, t * C:(t + 1) * C], og[:, g, t * P:(t + 1) * P], wo[:, g, :],
                                         start=(g == 0), stop=(g == KV - 1))
                last.then_inc(wo_done.sem, 1)

            def n_has_next(n):
                return not (isinstance(n, int) and n == B - 1)

            def turn_result(n):
                pe.wait_ge(norm_link.sem, norm_link.at(n, norm_link.per - 1))
                pe.wait_ge(mrow_ready.sem, mrow_ready.at(n + 1, 7) if n_has_next(n) else mrow_ready.at(n, H))
                for t in range(TT):
                    last = pe.transpose(ps[:, TAIL_BANK, t * P:(t + 1) * P], y[:, t, :], ident[:])
                last.then_inc(xn_turned.sem, 1)

            def batch(n, p, cur, nxt, prev):
                for j in range(H):
                    bn, bp, bh, has_before = before(n, p, j, cur, prev)

                    def slot(i):
                        if x := slot_piece(n, p, j, i, cur, nxt):
                            piece(*x)

                    if cur:
                        scores(n, p, j, 0)
                    if has_before:
                        max_row(bn, bh)
                    slot(0)
                    if j in WEIGHTED:
                        back, g, tiles = WEIGHTED[j]
                        if prev if back else cur:
                            for t in tiles:
                                weighted(n - back, (p + back) % 2, g, t)
                    if has_before:
                        scores_t(bn, bp, bh, [0, 1])
                    if cur:
                        scores(n, p, j, 1)
                    slot(1)
                    if has_before:
                        scores_t(bn, bp, bh, [2, 3])
                    slot(2)
                    if j == 5 and prev:
                        out_project(n - 1)
                    if j == 7 and prev:
                        turn_result(n - 1)

            def head(n, p):
                for name in first_pieces():
                    piece(n, p, name)

            over_batches(pe, head, batch, batch)

        @block.scalar
        def _(act):
            def read_piece(n, p, name):
                kind, i = name
                k = PIECE[name]
                act.wait_ge(head_done.sem, head_done.at(n, k + 1))
                bank = ps[:, HEAD_BANK, :]
                if kind == "xT":
                    out = act.copy(xT[p][:], bank)
                elif kind == "qkv":
                    act.wait_ge(v_ready.sem, v_ready.past(n, KV, 2))
                    out = act.copy(qkv[p][:, i, :], bank[:, 0:NQKV])
                elif kind == "gate":
                    act.wait_ge(gate_ready.sem, gate_ready.at(n, i))
                    out = act.activation(tanh[:], bank, ACT.Tanh, scale=0.5)
                elif i >= H:
                    out = act.copy(kT[p][0:SPLIT, i - H, :], ps[0:SPLIT, HEAD_BANK, :])
                else:
                    act.wait_ge(st_done.sem, st_done.past(n, (i + 1) * TT))
                    out = act.copy(qT[0:SPLIT, i, :], ps[0:SPLIT, HEAD_BANK, :])
                out.then_inc(head_read.sem, 1)

            def exponentials(n, h, tiles):
                for t in tiles:
                    i = h * TT + t
                    act.wait_ge(st_done.sem, st_done.at(n, i + 1))
                    if h % G == 0 and t == 0:
                        act.wait_ge(pv_done.sem, pv_done.past(n, (h // G + 1) * TT))
                    act.activation(probs[:, h // G, h % G, t, :], ps[:, ST_BANK + i % NST, :], ACT.Exp,
                                   scale=SM_SCALE).then_inc(exp_ready.sem, 1)

            def batch(n, p, cur, nxt, prev):
                for j in range(H):
                    bn, bp, bh, has_before = before(n, p, j, cur, prev)

                    def slot(i):
                        if x := slot_piece(n, p, j, i, cur, nxt):
                            read_piece(*x)

                    if has_before:
                        act.wait_ge(mrow_done.sem, mrow_done.at(bn, bh + 1))
                        act.copy(qT[SPLIT:SPLIT + 1, bh, :], ps[0:1, TAIL_BANK, :]).then_inc(mrow_ready.sem, 1)
                    slot(0)
                    if j in OUT_COPY and prev:
                        g = OUT_COPY[j]
                        act.wait_ge(pv_done.sem, pv_done.at(n - 1, (g + 1) * TT))
                        act.wait_ge(og_ready.sem, og_ready.at(n - 1, g))
                        act.copy(outs[:], ps[:, O_BANK, :]).then_inc(outs_ready.sem, 1)
                        act.copy(dens[:], ps[:, DEN_BANK, :]).then_inc(outs_ready.sem, 1)
                    if has_before:
                        exponentials(bn, bh, [0, 1])
                    slot(1)
                    if has_before:
                        exponentials(bn, bh, [2, 3])
                    slot(2)
                    if j == 7 and prev:
                        act.wait_ge(xn_turned.sem, xn_turned.at(n - 1, 1))
                        act.copy(xs[0:64, n - 1, 0:S], ps[0:64, TAIL_BANK, :]).then_inc(xs_ready.sem, 1)
                        act.copy(xs[64:P, n - 1, 1:S + 1], ps[64:P, TAIL_BANK, :]).then_inc(xs_ready.sem, 1)

            def head(n, p):
                for name in first_pieces():
                    read_piece(n, p, name)

            act.wait_ge(consts_set, SETS)
            over_batches(act, head, batch, batch)

        @block.vector
        def _(dve):
            dve.wait_ge(consts_in, CONSTS)
            dve.wait_ge(xtok_in, 16)
            dve.wait_ge(consts_set, SETS)

            def maxima(n, h, half):
                dve.wait_ge(s_done.sem, s_done.at(n, 2 * h + half + 1))
                if half == 0:
                    dve.wait_ge(mrow_done.sem, mrow_done.past(n, h + 1))
                dve.tensor_reduce(nmax[:, h, 2 * half:2 * half + 2], ps[:, S_BANK:S_BANK + 2, :], AX_X,
                                  ALU.max, negate=True).then_inc(max_ready.sem, 1)

            def rotate(n, p, split):
                dve.wait_ge(head_read.sem, head_read.at(n, PIECE["qkv", TT - 1] + 1))
                heads = qkv[p][:, :, 0:NQK].rearrange("p t (h d) -> p t h d", d=D)
                cos = rope[:, :, 0:1, :].to_broadcast([P, TT, NH, RD])
                sin = rope[:, :, 1:2, :].to_broadcast([P, TT, NH, RD])
                hr = RD // 2
                split.add(dve.tensor_tensor(rot[:, 0], heads[:, :, :, 0:RD], cos, ALU.mult))
                split.add(dve.tensor_tensor(rot[:, 1, :, :, 0:hr], heads[:, :, :, hr:RD], sin[:, :, :, 0:hr], ALU.mult))
                split(dve.tensor_tensor(rot[:, 1, :, :, hr:RD], heads[:, :, :, 0:hr], sin[:, :, :, hr:RD], ALU.mult))
                split(dve.tensor_tensor(heads[:, :, :, 0:RD], rot[:, 0], rot[:, 1], ALU.add))

            def split_parts(n, p, split):
                heads = qkv[p][:, :, 0:NQK].rearrange("p t (h d) -> p t h d", d=D)
                dve.wait_ge(head_done.sem, head_done.past(n, NP))
                split(dve.tensor_copy(q3[:, :, :, 0:D].bitcast(F32R), heads))
                split.add(dve.tensor_tensor(q3[:, :, 0:H, 2 * D:].bitcast(F32R), heads[:, :, 0:H, :],
                                            q3[:, :, 0:H, 0:D], ALU.subtract))
                split.add(dve.tensor_tensor(q3[:, :, H:NH, D:2 * D].bitcast(F32R), heads[:, :, H:NH, :],
                                            q3[:, :, H:NH, 0:D], ALU.subtract))

            def silu(n, p, g):
                dve.wait_ge(head_read.sem, head_read.at(n, PIECE["gate", g] + 1))
                dve.wait_ge(rden_link.sem, rden_link.past(n, 3 * g + 3, 2))
                dve.scalar_tensor_tensor(out=gate[p][:, g, :], in0=tanh[:], scalar=1.0,
                                         in1=ps[:, HEAD_BANK, :], op0=ALU.add, op1=ALU.mult).then_inc(gate_ready.sem, 1)

            def reciprocals(n, chain, g, half):
                cols = slice(half * S // 2, (half + 1) * S // 2)
                if half == 0:
                    dve.wait_ge(outs_ready.sem, outs_ready.at(n, 2 * g + 2))
                    dve.wait_ge(og_ready.sem, og_ready.at(n, g))
                chain.add(dve.reciprocal(rden[:, cols], dens[:, cols]))

            def gates(n, p, chain, g):
                chain.settle()
                chain.add(dve.scalar_tensor_tensor(out=rden[:], in0=rden[:], scalar=0.5, in1=gate[p][:, g, :],
                                                   op0=ALU.mult, op1=ALU.mult))

            def residual(n, norm):
                dve.wait_ge(wo_done.sem, wo_done.at(n, 1))
                dve.wait_ge(xn_turned.sem, xn_turned.past(n, 1))
                dve.wait_ge(norm_link.sem, norm_link.past(n, norm_link.per))
                norm(dve.tensor_tensor(y[:], ps[:, TAIL_BANK, :].rearrange("p (t c) -> p t c", c=C),
                                       xtok[:, bass.ds(n * TT, TT), :], ALU.add))

            def batch(n, p, cur, nxt, prev):
                split = Chain(dve, split_link, n + 1, passed)
                rden_chain = Chain(dve, rden_link, n - 1, passed)
                norm = Chain(dve, norm_link, n - 1, passed)
                statistics, deviation, result = layernorm_parts(dve, norm, y, y, stats, mv, rstd, small)
                for j in range(H):
                    for half in range(2):
                        if cur:
                            maxima(n, j, half)
                        if j in (1, 4) and prev:
                            g = (j - 1) // 3
                            reciprocals(n - 1, rden_chain, g, half)
                            if half:
                                gates(n - 1, 1 - p, rden_chain, g)
                        if nxt:
                            if (j, half) == (3, 0):
                                rotate(n + 1, 1 - p, split)
                            if (j, half) == (3, 1):
                                silu(n + 1, 1 - p, 0)
                                split_parts(n + 1, 1 - p, split)
                            if (j, half) == (4, 1):
                                silu(n + 1, 1 - p, 1)
                        if prev:
                            if (j, half) == (5, 1):
                                residual(n - 1, norm)
                                statistics()
                            if (j, half) == (6, 0):
                                deviation()
                            if (j, half) == (6, 1):
                                result()
                                norm.add(dve.tensor_copy(xtok[:, bass.ds((n - 1) * TT, TT), :], y[:]))

            def head(n, p):
                split = Chain(dve, split_link, n, passed)
                rotate(n, p, split)
                split_parts(n, p, split)
                for g in range(KV):
                    silu(n, p, g)

            over_batches(dve, head, batch, batch)


def ffn_block(nc, io, xtok, xs, ident):
    with ExitStack() as ctx:
        def sb(name, shape, dt=F32):
            return ctx.enter_context(nc.sbuf_tensor(name, shape, dt))

        signals = []

        def signal(name, per, lead=1, unit=1):
            s = Signal(ctx.enter_context(nc.semaphore(name)), per, lead, unit)
            signals.append(s)
            return s

        ps = ctx.enter_context(nc.psum_tensor("ps_b", [P, 8, 512], F32))
        PT_BANK, O_BANK, HEAD_BANK = 4, 6, 7
        NU = PAIRS * TT

        HEAD = [("proj", t, j) for t in range(TT) for j in range(2)] + [("proj", t, 2) for t in range(TT)]
        HEAD += [("turn", j, a) for a in range(PAIRS) for j in (1, 0)]
        NP = len(HEAD)
        PIECE = {piece: k for k, piece in enumerate(HEAD)}
        FIRST_TURN = PIECE["turn", 1, 0]
        LATE = [("turn", 1, PAIRS - 1), ("turn", 0, PAIRS - 1)]
        SLOTS = {0: [(0, x) for x in LATE]}
        for step, pieces in ((1, [0, 1]), (2, [2]), (3, [3, 4]), (4, [5]), (5, [6, 7]), (6, [8]), (7, [9]), (8, [10]), (9, [11])):
            SLOTS[step] = [(1, HEAD[i]) for i in pieces]
        SLOTS |= {13 + a: [(1, ("turn", 1, a)), (1, ("turn", 0, a))] for a in range(PAIRS - 1)}
        OUT_STEP = 4
        T_LAG, O_LAG = 3, 4
        COS_STEP, NORM_STEP, ROT_STEP, NORMS = 3, 6, 4, 4
        ROTATED = [3 * (k + 1) for k in range(TT)] + [3 * TT + 4 * (k + 1) for k in range(TT)]

        wqkv = sb("b_wqkv", [P, 3 * INNER])
        wo = sb("b_wo", [P, PAIRS, C])
        w1 = sb("c_w1", [P, 2 * HID])
        w2 = sb("c_w2", [P, HT, C])
        cols = sb("c_cols", [P, NCOLS])
        qs = sb("b_qs", [P, 2, LD])
        xpos = sb("b_xpos", [P, TT, 2, 2, LD])
        tab = sb("b_tab", [P, TT, 2, 2, LD])
        mask = sb("b_mask", [P, 2, KW])
        maskb = sb("b_maskb", [P, 2, KW], BF16)
        identb = sb("b_identb", [P, P], BF16)

        hT = sb("b_hT", [P, S])
        qk = sb("b_qk", [P, TT, 2, INNER])
        rot = sb("b_rot", [P, TT, 2, INNER])
        v = [sb(f"b_v{p}", [P, TT + 1, INNER]) for p in range(2)]
        part = sb("b_part", [P, INNER])
        sq = sb("b_sq", [P, 2, INNER])
        ss = sb("b_ss", [P, TT, 2, LH])
        rn = [sb(f"b_rn{p}", [P, TT, 2, LH]) for p in range(2)]
        small = [sb(f"b_small{i}", [P, TT * 2 * LH])[:] for i in range(3)]
        qT = sb("b_qT", [P, PAIRS, S])
        kT = sb("b_kT", [P, PAIRS, W + S])
        NPB = 4
        nmax = sb("b_nmax", [P, NU, 2])
        bias = sb("b_bias", [P, NU, 2])
        probs = sb("b_probs", [P, NPB, 2, 2 * P])
        den = sb("b_den", [P, NU, 2])
        rden = sb("b_rden", [P, NU, 2])
        pT = sb("b_pT", [P, 2, 2, 2, P])
        oT = sb("b_oT", [P, PAIRS, S])

        hc = [sb(f"c_hT{p}", [P, S]) for p in range(2)]
        hn = [sb(f"c_hn{p}", [P, TT, C]) for p in range(2)]
        hg = sb("c_hg", [P, S])
        gelu = sb("c_gelu", [P, HT, S])
        mid = sb("c_mid", [P, HT, S])
        stats = sb("c_stats", [P, TT, 6])
        mv = sb("c_mv", [P, TT, 2])
        rstd = sb("c_rstd", [P, 2, TT])
        lnsmall = [sb(f"c_small{i}", [P, TT])[:] for i in range(3)]

        BW, CW = 4, 4
        consts_in = ctx.enter_context(nc.semaphore("b_consts_in"))
        consts_set = ctx.enter_context(nc.semaphore("b_consts_set"))
        consts_cast = ctx.enter_context(nc.semaphore("b_consts_cast"))
        passed = ctx.enter_context(nc.semaphore("b_passed"))
        bw_loaded = signal("bw_loaded", BW, unit=16)
        cw_loaded = signal("cw_loaded", CW, unit=16)
        tab_ready = signal("tab_ready", 6)
        h_ready = signal("h_ready", 1)
        head_done = signal("b_head_done", NP)
        proj_read = signal("b_proj_read", 3 * TT)
        sq_ready = signal("sq_ready", 2 * TT)
        ss_ready = signal("ss_ready", 2 * TT)
        rn_link = signal("rn_link", RSQRT_LINKS + 1)
        cos_ready = signal("cos_ready", 2 * TT)
        rot_link = signal("rot_link", 7 * TT)
        kT_ready = signal("b_kT_ready", PAIRS)
        qT_ready = signal("b_qT_ready", PAIRS)
        s_done = signal("b_s_done", NU)
        max_ready = signal("b_max_ready", NU)
        bias_ready = signal("b_bias_ready", NU)
        exp_ready = signal("b_exp_ready", 2 * NU)
        rden_ready = signal("b_rden_ready", NU)
        norm_ready = signal("b_norm_ready", 2 * NU)
        p_turned = signal("b_p_turned", NU)
        pT_ready = signal("b_pT_ready", NU)
        pv_done = signal("b_pv_done", NU, lead=2)
        oT_ready = signal("b_oT_ready", PAIRS)
        wo_done = signal("b_wo_done", 1)
        x_added = signal("b_x_added", 2, lead=2)
        hc_ready = signal("c_h_ready", 1)
        hc_turned = signal("c_h_turned", 1)
        ln_link = signal("c_ln_link", LAYERNORM_LINKS)
        hn_turned = signal("c_hn_turned", 1)
        hg_ready = signal("c_hg_ready", 1)
        up_done = signal("c_up_done", 2 * HT)
        gelu_ready = signal("c_gelu_ready", HT)
        mid_ready = signal("c_mid_ready", HT)
        down_done = signal("c_down_done", 1)
        x_out = signal("c_x_out", 2, lead=B)
        f_copied = signal("f_copied", 2, lead=2)
        f_turned = signal("f_turned", 1, lead=2)
        f_link = signal("f_link", 1 + LAYERNORM_LINKS, lead=2)
        f_stored = [signal(f"f_stored{p}", 1, unit=16) for p in range(2)]

        def over_batches(engine, l, head, batch, drain):
            n0 = l * B
            head(n0, 0, 0)
            batch(n0, 0, 0, cur=True, nxt=True, prev=False)
            with engine.Fori(0, (B - 2) // 2) as m:
                for i in range(2):
                    b = m * 2 + (i + 1)
                    batch(n0 + b, b, 1 - i, cur=True, nxt=True, prev=True)
            batch(n0 + B - 1, B - 1, 1, cur=True, nxt=False, prev=True)
            drain(n0 + B, B, 0, cur=False, nxt=False, prev=True)

        def lagged(n, p, u, lag, cur, prev):
            return (n, p, u - lag, cur) if u >= lag else (n - 1, 1 - p, u - lag + NU, prev)

        def slot_pieces(n, p, u, cur, nxt):
            return [(n + ahead, (p + ahead) % 2, piece) for ahead, piece in SLOTS.get(u, [])
                    if (nxt if ahead else cur)]

        early = [x for x in HEAD if x not in LATE]

        def over_ffn(engine, l, first, batch):
            n0 = l * B
            first(n0, 0)
            with engine.Fori(0, B - 1) as b:
                batch(n0 + b, b, True)
            batch(n0 + (B - 1), B - 1, False)

        block = ctx.enter_context(nc.Block())

        @block.sync
        def _(sp):
            for s in signals:
                sp.sem_inc(s.sem, s.lead * s.per * s.unit)
            sp.dma_start(xpos[:], io["xpos"].rearrange("(t p) a b d -> p t a b d", p=P)).then_inc(consts_in, 16)
            sp.dma_start(mask[:], io["mask"]).then_inc(consts_in, 16)
            with sp.Fori(0, LAYERS) as l:
                sp.wait_ge(wo_done.sem, wo_done.at(l * B - 1, 1))
                sp.wait_ge(tab_ready.sem, tab_ready.past(l, 6))
                sp.dma_start(wqkv[:], io["wqkv"][l]).then_inc(bw_loaded.sem, 16)
                sp.dma_start(wo[:], io["lwo"][l].rearrange("(a p) c -> p a c", p=P)).then_inc(bw_loaded.sem, 16)
                sp.dma_start(qs[:, 0, :], io["qs"][bass.ds(l, 1), :].to_broadcast([P, LD])).then_inc(bw_loaded.sem, 16)
                sp.dma_start(qs[:, 1, :], io["ks"][bass.ds(l, 1), :].to_broadcast([P, LD])).then_inc(bw_loaded.sem, 16)
                sp.wait_ge(x_out.sem, x_out.at(l * B - 1, 2))
                sp.dma_start(w1[:], io["w1"][l]).then_inc(cw_loaded.sem, 16)
                sp.dma_start(w2[:, 0:2, :], io["w2"][l, 0:2 * P].rearrange("(a p) c -> p a c", p=P)).then_inc(cw_loaded.sem, 16)
                sp.dma_start(w2[0:HSIZE[2], 2, :], io["w2"][l, 2 * P:HID]).then_inc(cw_loaded.sem, 16)
                sp.dma_start(cols[:], io["cols"][l]).then_inc(cw_loaded.sem, 16)
            out = io["out"].rearrange("b (t p) c -> b p t c", p=P)
            with sp.Fori(0, B // 2) as m:
                for p in range(2):
                    n = m * 2 + p
                    sp.wait_ge(f_link.sem, f_link.at(n, f_link.per))
                    sp.dma_start(out[n], hn[p][:]).then_inc(f_stored[p].sem, 16)
            for p in range(2):
                sp.wait_ge(f_stored[p].sem, f_stored[p].at(B // 2 - 1, 1))

        @block.gpsimd
        def _(pool):
            for p in range(2):
                pool.memset(v[p][:, 0, :], 0.0).then_inc(consts_set, 1)
            pool.memset(kT[:, :, 0:W], 0.0).then_inc(consts_set, 1)
            pool.memset(probs[:], 0.0).then_inc(consts_set, 1)
            pool.wait_ge(consts_in, 32)
            pool.tensor_copy(maskb[:], mask[:]).then_inc(consts_cast, 1)
            pool.tensor_copy(identb[:], ident[:]).then_inc(consts_cast, 1)

            def head_start(n, b):
                pool.wait_ge(head_done.sem, head_done.past(n, 3 * TT))
                pool.wait_ge(x_out.sem, x_out.past(n, 2, B))
                pool.sem_inc(passed, 1)
                pool.tensor_copy(hT[:], xs[:, b, 0:S]).then_inc(h_ready.sem, 1)

            def cosines(n, k):
                j, t = k // TT, k % TT
                pool.wait_ge(proj_read.sem, proj_read.at(n, PIECE["proj", t, j] + 1))
                x, r = (a[:, t, j, :].rearrange("p (h d) -> p h d", d=LD) for a in (qk, rot))
                pool.wait_ge(rot_link.sem, rot_link.past(n, ROTATED[k]))
                pool.tensor_tensor(r, x, tab[:, t, j, 0:1, :].to_broadcast([P, LH, LD]),
                                   ALU.mult).then_inc(cos_ready.sem, 1)

            def normalise(n, u):
                pool.wait_ge(rden_ready.sem, rden_ready.at(n, u + 1))
                pool.sem_inc(passed, 1)
                for r in range(2):
                    p_u = probs[:, u % NPB, r, W:W + KW]
                    pool.tensor_scalar(p_u, p_u, rden[:, u, r:r + 1], None, ALU.mult).then_inc(norm_ready.sem, 1)

            def batch(n, b, p, cur, nxt, prev):
                for u in range(NU):
                    if nxt and u == 0:
                        head_start(n + 1, b + 1)
                    if nxt and COS_STEP <= u < COS_STEP + 2 * TT:
                        cosines(n + 1, u - COS_STEP)
                    ln, lp, lu, there = lagged(n, p, u, 1, cur, prev)
                    if there:
                        normalise(ln, lu)

            def head(n, b, p):
                head_start(n, b)
                for k in range(2 * TT):
                    cosines(n, k)

            def drain(n, b, p, cur, nxt, prev):
                normalise(n - 1, NU - 1)

            def copy_h(n, b):
                pool.wait_ge(x_added.sem, x_added.at(n, 2))
                pool.wait_ge(hc_turned.sem, hc_turned.past(n, 1))
                pool.sem_inc(passed, 1)
                pool.tensor_copy(hc[0][:], xs[:, b, 0:S]).then_inc(hc_ready.sem, 1)

            with pool.Fori(0, LAYERS) as l:
                pool.wait_ge(bw_loaded.sem, bw_loaded.at(l, BW))
                pool.wait_ge(rot_link.sem, rot_link.at(l * B - 1, rot_link.per))
                hd = LD // 2
                for j in range(2):
                    s = qs[:, j:j + 1, :].to_broadcast([P, TT, LD])
                    pool.tensor_tensor(tab[:, :, j, 0, :], xpos[:, :, j, 0, :], s, ALU.mult).then_inc(tab_ready.sem, 1)
                    pool.tensor_tensor(tab[:, :, j, 1, 0:hd], xpos[:, :, j, 1, 0:hd], s[:, :, hd:LD], ALU.mult).then_inc(tab_ready.sem, 1)
                    pool.tensor_tensor(tab[:, :, j, 1, hd:LD], xpos[:, :, j, 1, hd:LD], s[:, :, 0:hd], ALU.mult).then_inc(tab_ready.sem, 1)
                pool.wait_ge(tab_ready.sem, tab_ready.at(l, 6))
                pool.sem_inc(passed, 1)
                over_batches(pool, l, head, batch, drain)
                with pool.Fori(0, B) as b:
                    copy_h(l * B + b, b)
            pool.wait_ge(hc_turned.sem, hc_turned.at(LAYERS * B - 1, 1))
            pool.sem_inc(passed, 1)
            with pool.Fori(0, B // 2) as m:
                for p in range(2):
                    n = m * 2 + p
                    pool.wait_ge(x_out.sem, x_out.at(n + (LAYERS - 1) * B, 2))
                    pool.wait_ge(f_turned.sem, f_turned.past(n, 1, 2))
                    pool.sem_inc(passed, 1)
                    pool.tensor_copy(hc[p][0:64, :], xs[0:64, n, 0:S]).then_inc(f_copied.sem, 1)
                    pool.tensor_copy(hc[p][64:P, :], xs[64:P, n, 1:S + 1]).then_inc(f_copied.sem, 1)

        SETS = 4

        @block.tensor
        def _(pe):
            pe.wait_ge(consts_cast, 2)
            pe.wait_ge(consts_set, SETS)

            def head_bank_free(n, k):
                kind, i, j = HEAD[k - 1]
                if kind == "proj":
                    pe.wait_ge(proj_read.sem, proj_read.at(n, k))
                elif i:
                    pe.wait_ge(kT_ready.sem, kT_ready.at(n, j + 1))
                else:
                    pe.wait_ge(qT_ready.sem, qT_ready.at(n, j + 1))

            def piece(n, p, name):
                kind, i, j = name
                k = PIECE[name]
                bank = ps[:, HEAD_BANK, :]
                if k:
                    head_bank_free(n, k)
                else:
                    pe.wait_ge(h_ready.sem, h_ready.at(n, 1))
                    pe.wait_ge(qT_ready.sem, qT_ready.past(n, PAIRS))
                if kind == "proj":
                    if name in FIRST_AFTER_OUT:
                        pe.wait_ge(x_added.sem, x_added.past(n, 2, 2))
                    last = pe.matmul(bank, hT[:, i * P:(i + 1) * P], wqkv[:, j * INNER:(j + 1) * INNER],
                                     start=True, stop=True)
                else:
                    if k == FIRST_TURN:
                        pe.wait_ge(rot_link.sem, rot_link.at(n, rot_link.per))
                    for t in range(TT):
                        last = pe.transpose(bank[:, t * P:(t + 1) * P], qk[:, t, i, j * P:(j + 1) * P], ident[:])
                last.then_inc(head_done.sem, 1)

            def scores(n, p, u):
                a, t = u // TT, u % TT
                if t == 0:
                    pe.wait_ge(kT_ready.sem, kT_ready.at(n, a + 1))
                    pe.wait_ge(qT_ready.sem, qT_ready.at(n, a + 1))
                if u >= 2:
                    pe.wait_ge(exp_ready.sem, exp_ready.at(n, 2 * (u - 2) + 2))
                else:
                    pe.wait_ge(exp_ready.sem, exp_ready.past(n, 2 * (u - 2 + NU) + 2))
                for r in range(2):
                    rows = slice(LD * r, LD * r + LD)
                    pe.matmul(ps[:, 2 * (u % 2) + r, 0:KW], qT[rows, a, t * P:(t + 1) * P], kT[rows, a, t * P:t * P + KW],
                              start=True, stop=False)
                for r in range(2):
                    last = pe.matmul(ps[:, 2 * (u % 2) + r, 0:KW], identb[:], maskb[:, 0 if t == 0 else 1, :],
                                     start=False, stop=True)
                last.then_inc(s_done.sem, 1)

            def turn_probs(n, u):
                pe.wait_ge(norm_ready.sem, norm_ready.at(n, 2 * u + 2))
                if u >= 2:
                    pe.wait_ge(pT_ready.sem, pT_ready.at(n, u - 1))
                else:
                    pe.wait_ge(pT_ready.sem, pT_ready.past(n, u - 1 + NU))
                for r in range(2):
                    for m in range(2):
                        last = pe.transpose(ps[:, PT_BANK + u % 2, (2 * r + m) * P:(2 * r + m + 1) * P],
                                            probs[:, u % NPB, r, m * P:(m + 1) * P], ident[:])
                last.then_inc(p_turned.sem, 1)

            def weighted(n, p, u):
                a, t = u // TT, u % TT
                pe.wait_ge(pT_ready.sem, pT_ready.at(n, u + 1))
                if t == 0:
                    pe.wait_ge(oT_ready.sem, oT_ready.at(n, a))
                for r in range(2):
                    h = 2 * a + r
                    pe.matmul(ps[LD * r:LD * r + LD, O_BANK, t * P:(t + 1) * P], v[p][:, t + 1, h * LD:(h + 1) * LD],
                              pT[:, u % 2, r, 1, :], start=True, stop=False)
                for r in range(2):
                    h = 2 * a + r
                    last = pe.matmul(ps[LD * r:LD * r + LD, O_BANK, t * P:(t + 1) * P], v[p][W:P, t, h * LD:(h + 1) * LD],
                                     pT[W:P, u % 2, r, 0, :], start=False, stop=True)
                last.then_inc(pv_done.sem, 1)

            def out_project(n, after):
                pe.wait_ge(oT_ready.sem, oT_ready.at(n, PAIRS))
                if after is not None:
                    head_bank_free(n + 2, after)
                else:
                    pe.wait_ge(qT_ready.sem, qT_ready.at(n, PAIRS))
                for a in range(PAIRS):
                    last = pe.matmul(ps[:, HEAD_BANK, :], wo[:, a, :], oT[:, a, :], start=(a == 0), stop=(a == PAIRS - 1))
                last.then_inc(wo_done.sem, 1)

            FIRST_AFTER_OUT = [SLOTS[OUT_STEP + 1][0][1]]

            def batch(n, b, p, cur, nxt, prev):
                for u in range(NU):
                    pieces = slot_pieces(n, p, u, cur, nxt)
                    if cur:
                        scores(n, p, u)
                    for x in pieces[:1]:
                        piece(*x)
                    ln, lp, lu, there = lagged(n, p, u, T_LAG, cur, prev)
                    if there:
                        turn_probs(ln, lu)
                    for x in pieces[1:]:
                        piece(*x)
                    ln, lp, lu, there = lagged(n, p, u, O_LAG, cur, prev)
                    if there:
                        weighted(ln, lp, lu)
                    if u == OUT_STEP and prev:
                        out_project(n - 1, PIECE[SLOTS[OUT_STEP][-1][1]] + 1 if nxt else None)

            def head(n, b, p):
                for x in early:
                    piece(n, p, x)

            def drain(n, b, p, cur, nxt, prev):
                for u in range(OUT_STEP + 1):
                    if u < T_LAG:
                        turn_probs(n - 1, u - T_LAG + NU)
                    if u < O_LAG:
                        weighted(n - 1, 1 - p, u - O_LAG + NU)
                out_project(n - 1, None)

            def turn_h(n):
                pe.wait_ge(hc_ready.sem, hc_ready.at(n, 1))
                pe.wait_ge(hg_ready.sem, hg_ready.past(n, 1))
                for t in range(TT):
                    last = pe.transpose(ps[:, 0, t * P:(t + 1) * P], hc[0][:, t * P:(t + 1) * P], ident[:])
                last.then_inc(hc_turned.sem, 1)

            def turn_hn(n):
                pe.wait_ge(ln_link.sem, ln_link.at(n, ln_link.per))
                for t in range(TT):
                    last = pe.transpose(ps[:, 0, t * P:(t + 1) * P], hn[0][:, t, :], ident[:])
                last.then_inc(hn_turned.sem, 1)

            def up(n):
                pe.wait_ge(hg_ready.sem, hg_ready.at(n, 1))
                for i in range(HT):
                    m = HSIZE[i]
                    for a in (1, 0):
                        bank = 1 + 2 * i + a
                        pe.wait_ge(mid_ready.sem, mid_ready.past(n, i + 1))
                        pe.matmul(ps[0:m, bank, :], w1[:, a * HID + i * P:a * HID + i * P + m], hg[:],
                                  start=True, stop=True).then_inc(up_done.sem, 1)

            def down(n):
                for i in range(HT):
                    m = HSIZE[i]
                    pe.wait_ge(mid_ready.sem, mid_ready.at(n, i + 1))
                    if i == 0:
                        pe.wait_ge(x_out.sem, x_out.past(n, 2))
                    last = pe.matmul(ps[:, 7, :], w2[0:m, i, :], mid[0:m, i, :], start=(i == 0), stop=(i == HT - 1))
                last.then_inc(down_done.sem, 1)

            def ffn_first(n, b):
                turn_h(n)
                turn_hn(n)

            def ffn(n, b, nxt):
                if nxt:
                    turn_h(n + 1)
                up(n)
                if nxt:
                    turn_hn(n + 1)
                down(n)

            with pe.Fori(0, LAYERS) as l:
                pe.wait_ge(bw_loaded.sem, bw_loaded.at(l, BW))
                pe.wait_ge(mid_ready.sem, mid_ready.at(l * B - 1, HT))
                pe.wait_ge(hg_ready.sem, hg_ready.at(l * B - 1, 1))
                pe.wait_ge(x_out.sem, x_out.at(l * B - 1, 2))
                pe.sem_inc(passed, 1)
                over_batches(pe, l, head, batch, drain)
                pe.wait_ge(cw_loaded.sem, cw_loaded.at(l, CW))
                pe.wait_ge(x_added.sem, x_added.at(l * B + B - 1, 2))
                pe.wait_ge(exp_ready.sem, exp_ready.at(l * B + B - 1, 2 * NU))
                pe.wait_ge(pT_ready.sem, pT_ready.at(l * B + B - 1, NU))
                pe.wait_ge(oT_ready.sem, oT_ready.at(l * B + B - 1, PAIRS))
                pe.sem_inc(passed, 1)
                over_ffn(pe, l, ffn_first, ffn)
            pe.wait_ge(mid_ready.sem, mid_ready.at(LAYERS * B - 1, HT))
            pe.wait_ge(hg_ready.sem, hg_ready.at(LAYERS * B - 1, 1))
            pe.sem_inc(passed, 1)
            with pe.Fori(0, B // 2) as m:
                for p in range(2):
                    n = m * 2 + p
                    pe.wait_ge(f_copied.sem, f_copied.at(n, 2))
                    pe.wait_ge(f_link.sem, f_link.past(n, 1, 2))
                    for t in range(TT):
                        last = pe.transpose(ps[:, p, t * P:(t + 1) * P], hc[p][:, t * P:(t + 1) * P], ident[:])
                    last.then_inc(f_turned.sem, 1)

        @block.scalar
        def _(act):
            act.wait_ge(consts_set, SETS)

            def read_piece(n, p, name):
                kind, i, j = name
                if kind == "turn":
                    if i:
                        act.wait_ge(head_done.sem, head_done.at(n, PIECE[name] + 1))
                        act.wait_ge(s_done.sem, s_done.past(n, (j + 1) * TT))
                        act.copy(kT[:, j, W:], ps[:, HEAD_BANK, :]).then_inc(kT_ready.sem, 1)
                    return
                act.wait_ge(head_done.sem, head_done.at(n, PIECE[name] + 1))
                if j < 2:
                    k = 2 * i + j
                    act.wait_ge(ss_ready.sem, ss_ready.at(n, k - 1))
                    act.copy(qk[:, i, j, :], ps[:, HEAD_BANK, :]).then_inc(proj_read.sem, 1)
                    act.wait_ge(proj_read.sem, proj_read.at(n, k + 1))
                    act.activation(sq[:, j, :], qk[:, i, j, :], ACT.Square).then_inc(sq_ready.sem, 1)
                else:
                    act.wait_ge(pv_done.sem, pv_done.past(n, NU, 2))
                    act.copy(v[p][:, i + 1, :], ps[:, HEAD_BANK, :]).then_inc(proj_read.sem, 1)

            def exponentials(n, p, u):
                a, t = u // TT, u % TT
                act.wait_ge(bias_ready.sem, bias_ready.at(n, u + 1))
                if u >= NPB:
                    act.wait_ge(p_turned.sem, p_turned.at(n, u - NPB + 1))
                else:
                    act.wait_ge(p_turned.sem, p_turned.past(n, u - NPB + 1 + NU))
                for r in range(2):
                    h = 2 * a + r
                    act.activation(probs[:, u % NPB, r, W:W + KW], ps[:, 2 * (u % 2) + r, 0:KW],
                                   ACT.Exp, scale=rn[p][:, t, 0, h:h + 1], bias=bias[:, u, r:r + 1],
                                   accum_out=den[:, u, r:r + 1]).then_inc(exp_ready.sem, 1)

            def copy_pT(n, u):
                act.wait_ge(p_turned.sem, p_turned.at(n, u + 1))
                if u >= 2:
                    act.wait_ge(pv_done.sem, pv_done.at(n, u - 1))
                else:
                    act.wait_ge(pv_done.sem, pv_done.past(n, u - 1 + NU))
                act.copy(pT[:, u % 2].rearrange("p r m q -> p (r m q)"), ps[:, PT_BANK + u % 2, :]).then_inc(pT_ready.sem, 1)

            def copy_oT(n, a):
                act.wait_ge(pv_done.sem, pv_done.at(n, (a + 1) * TT))
                act.wait_ge(wo_done.sem, wo_done.past(n, 1))
                act.copy(oT[:, a, :], ps[:, O_BANK, :]).then_inc(oT_ready.sem, 1)

            def step_tail(n, p, u, cur, prev):
                ln, lp, lu, there = lagged(n, p, u, T_LAG, cur, prev)
                if there:
                    copy_pT(ln, lu)
                ln, lp, lu, there = lagged(n, p, u, O_LAG, cur, prev)
                if there and lu % TT == TT - 1:
                    copy_oT(ln, lu // TT)

            def batch(n, b, p, cur, nxt, prev):
                for u in range(NU):
                    pieces = slot_pieces(n, p, u, cur, nxt)
                    for x in pieces[:1]:
                        read_piece(*x)
                    if cur:
                        exponentials(n, p, u)
                    for x in pieces[1:]:
                        read_piece(*x)
                    step_tail(n, p, u, cur, prev)

            def head(n, b, p):
                for x in early:
                    read_piece(n, p, x)

            def drain(n, b, p, cur, nxt, prev):
                for u in range(O_LAG):
                    if u < T_LAG:
                        copy_pT(n - 1, u - T_LAG + NU)
                copy_oT(n - 1, PAIRS - 1)

            def scale_h(n):
                act.wait_ge(hn_turned.sem, hn_turned.at(n, 1))
                act.wait_ge(up_done.sem, up_done.past(n, 2 * HT))
                act.activation(hg[:], ps[:, 0, :], ACT.Identity, scale=cols[:, LNG:LNG + 1],
                               bias=cols[:, LNB:LNB + 1]).then_inc(hg_ready.sem, 1)

            def ffn(n, b, nxt):
                for i in range(HT):
                    m = HSIZE[i]
                    act.wait_ge(up_done.sem, up_done.at(n, 2 * i + 1))
                    act.wait_ge(mid_ready.sem, mid_ready.past(n, i + 1))
                    act.activation(gelu[0:m, i, :], ps[0:m, 2 + 2 * i, :], ACT.Gelu,
                                   bias=cols[0:m, B1G + i:B1G + i + 1]).then_inc(gelu_ready.sem, 1)
                if nxt:
                    scale_h(n + 1)

            with act.Fori(0, LAYERS) as l:
                over_batches(act, l, head, batch, drain)
                act.wait_ge(cw_loaded.sem, cw_loaded.at(l, CW))
                over_ffn(act, l, lambda n, b: scale_h(n), ffn)

        @block.vector
        def _(dve):
            dve.wait_ge(consts_set, SETS)

            def linker(sig, n):
                return Chain(dve, sig, n, passed)

            def squares(n, k):
                t, j = k // 2, k % 2
                dve.wait_ge(sq_ready.sem, sq_ready.at(n, k + 1))
                dve.tensor_reduce(ss[:, t, j, :], sq[:, j, :].rearrange("p (h d) -> p h d", d=LD), AX_X,
                                  ALU.add).then_inc(ss_ready.sem, 1)

            def norms(n, p, link, k):
                if k == 0:
                    dve.wait_ge(ss_ready.sem, ss_ready.at(n, 2 * TT))
                if k < RSQRT_LINKS:
                    rsqrt_step(dve, link, k, rn[p][:].rearrange("p t j h -> p (t j h)"),
                               ss[:].rearrange("p t j h -> p (t j h)"), small, 1e-24)
                elif k == RSQRT_LINKS:
                    link.settle()
                    link.add(dve.tensor_scalar(rn[p][:, :, 0, :], rn[p][:, :, 0, :], QK_SCALE, None, ALU.mult))

            def rotate(n, link, k, between):
                j, t = k // TT, k % TT
                x, r, a = (z.rearrange("p (h d) -> p h d", d=LD) for z in (qk[:, t, j, :], rot[:, t, j, :], part[:]))
                hd = LD // 2
                sin = tab[:, t, j, 1:2, :].to_broadcast([P, LH, LD])
                link.settle()
                dve.wait_ge(proj_read.sem, proj_read.at(n, PIECE["proj", t, j] + 1))
                link.add(dve.tensor_tensor(a[:, :, 0:hd], x[:, :, hd:LD], sin[:, :, 0:hd], ALU.mult))
                link.add(dve.tensor_tensor(a[:, :, hd:LD], x[:, :, 0:hd], sin[:, :, hd:LD], ALU.mult))
                between()
                link.settle()
                dve.wait_ge(cos_ready.sem, cos_ready.at(n, k + 1))
                link.add(dve.tensor_tensor(x, r, a, ALU.add))

            def scale_keys(n, p, link, k):
                t = k - TT
                x = qk[:, t, 1, :].rearrange("p (h d) -> p h d", d=LD)
                nrm = rn[p][:, t, 1, :].rearrange("p (h o) -> p h o", o=1).to_broadcast([P, LH, LD])
                dve.wait_ge(rn_link.sem, rn_link.at(n, RSQRT_LINKS))
                link.settle()
                link.add(dve.tensor_tensor(x, x, nrm, ALU.mult))

            def maxima(n, u):
                dve.wait_ge(s_done.sem, s_done.at(n, u + 1))
                b2 = 2 * (u % 2)
                dve.tensor_reduce(nmax[:, u, :], ps[:, b2:b2 + 2, 0:KW], AX_X, ALU.max, negate=True).then_inc(max_ready.sem, 1)

            def biases(n, p, u):
                a, t = u // TT, u % TT
                dve.wait_ge(max_ready.sem, max_ready.at(n, u + 1))
                dve.wait_ge(rn_link.sem, rn_link.at(n, rn_link.per))
                dve.tensor_tensor(bias[:, u, :], nmax[:, u, :], rn[p][:, t, 0, 2 * a:2 * a + 2], ALU.mult).then_inc(bias_ready.sem, 1)

            def denominators(n, u):
                dve.wait_ge(exp_ready.sem, exp_ready.at(n, 2 * u + 2))
                dve.wait_ge(norm_ready.sem, norm_ready.past(n, 2 * u + 2))
                dve.reciprocal(rden[:, u, :], den[:, u, :]).then_inc(rden_ready.sem, 1)

            def copy_qT(n, a):
                dve.wait_ge(head_done.sem, head_done.at(n, PIECE["turn", 0, a] + 1))
                dve.wait_ge(s_done.sem, s_done.past(n, (a + 1) * TT))
                dve.tensor_copy(qT[:, a, :], ps[:, HEAD_BANK, :]).then_inc(qT_ready.sem, 1)

            def add_x(n, b):
                dve.wait_ge(wo_done.sem, wo_done.at(n, 1))
                for r in range(2):
                    x = xs[64 * r:64 * r + 64, b, r:r + S]
                    dve.tensor_tensor(x, ps[64 * r:64 * r + 64, HEAD_BANK, :], x, ALU.add).then_inc(x_added.sem, 1)

            def batch(n, b, p, cur, nxt, prev):
                rn_chain, rot_chain = linker(rn_link, n + 1), linker(rot_link, n + 1)
                for u in range(NU):
                    def norm_step(i):
                        k = (u - NORM_STEP) * NORMS + i
                        if nxt and 0 <= k <= RSQRT_LINKS:
                            norms(n + 1, 1 - p, rn_chain, k)

                    if cur:
                        maxima(n, u)
                    norm_step(0)
                    if cur:
                        biases(n, p, u)
                    norm_step(1)
                    ln, lp, lu, there = lagged(n, p, u, 1, cur, prev)
                    if there:
                        denominators(ln, lu)
                    k = u - ROT_STEP
                    if nxt and TT < k <= 2 * TT:
                        scale_keys(n + 1, 1 - p, rot_chain, k - 1)
                    for xn, xp, (kind, i, j) in slot_pieces(n, p, u, cur, nxt):
                        if kind == "proj" and j < 2:
                            squares(xn, 2 * i + j)
                        if kind == "turn" and not i:
                            copy_qT(xn, j)
                    if u == OUT_STEP and prev:
                        add_x(n - 1, b - 1)
                    if nxt and 0 <= k < 2 * TT:
                        rotate(n + 1, rot_chain, k, lambda: norm_step(2))
                    else:
                        norm_step(2)
                    norm_step(3)

            def head(n, b, p):
                for k in range(2 * TT):
                    squares(n, k)
                chain = linker(rn_link, n)
                for k in range(RSQRT_LINKS + 1):
                    norms(n, p, chain, k)
                chain = linker(rot_link, n)
                for k in range(2 * TT):
                    rotate(n, chain, k, lambda: None)
                    if k >= TT:
                        scale_keys(n, p, chain, k)
                for a in range(PAIRS - 1):
                    copy_qT(n, a)

            def drain(n, b, p, cur, nxt, prev):
                denominators(n - 1, NU - 1)
                add_x(n - 1, b - 1)

            def layernorm(n):
                dve.wait_ge(hc_turned.sem, hc_turned.at(n, 1))
                dve.wait_ge(hn_turned.sem, hn_turned.past(n, 1))
                layernorm_steps(dve, linker(ln_link, n), ps[:, 0, :].rearrange("p (t c) -> p t c", c=C), hn[0], stats,
                                mv, rstd, lnsmall)

            def ffn(n, b, nxt):
                if nxt:
                    layernorm(n + 1)
                for i in range(HT):
                    m = HSIZE[i]
                    dve.wait_ge(gelu_ready.sem, gelu_ready.at(n, i + 1))
                    dve.wait_ge(up_done.sem, up_done.at(n, 2 * i + 2))
                    dve.wait_ge(down_done.sem, down_done.past(n, 1))
                    dve.scalar_tensor_tensor(out=mid[0:m, i, :], in0=ps[0:m, 1 + 2 * i, :], scalar=cols[0:m, B1A + i:B1A + i + 1],
                                             in1=gelu[0:m, i, :], op0=ALU.add, op1=ALU.mult).then_inc(mid_ready.sem, 1)
                dve.wait_ge(down_done.sem, down_done.at(n, 1))
                dve.wait_ge(hc_ready.sem, hc_ready.at(n, 1))
                for r in range(2):
                    rows = slice(64 * r, 64 * r + 64)
                    x = xs[rows, b, r:r + S]
                    dve.scalar_tensor_tensor(out=x, in0=ps[rows, 7, :], scalar=cols[rows, B2:B2 + 1], in1=x,
                                             op0=ALU.add, op1=ALU.add).then_inc(x_out.sem, 1)

            with dve.Fori(0, LAYERS) as l:
                dve.wait_ge(tab_ready.sem, tab_ready.at(l, 6))
                dve.sem_inc(passed, 1)
                over_batches(dve, l, head, batch, drain)
                over_ffn(dve, l, lambda n, b: layernorm(n), ffn)
            dve.wait_ge(hn_turned.sem, hn_turned.at(LAYERS * B - 1, 1))
            dve.sem_inc(passed, 1)
            with dve.Fori(0, B // 2) as m:
                for p in range(2):
                    n = m * 2 + p
                    dve.wait_ge(f_turned.sem, f_turned.at(n, 1))
                    dve.wait_ge(f_stored[p].sem, f_stored[p].past(m, 1))
                    link = linker(f_link, n)
                    link(dve.tensor_tensor(hn[p][:], ps[:, p, :].rearrange("p (t c) -> p t c", c=C),
                                           xtok[:, bass.ds(n * TT, TT), :], ALU.add))
                    layernorm_steps(dve, link, hn[p], hn[p], stats, mv, rstd, lnsmall)




def build(nc, io):
    with ExitStack() as ctx:
        ident = ctx.enter_context(nc.sbuf_tensor("ident_sb", [P, P], F32))
        xtok = ctx.enter_context(nc.sbuf_tensor("xtok", [P, B * TT, C], F32))
        xs = ctx.enter_context(nc.sbuf_tensor("xs", [P, B, XW], F32))
        global_attention_block(nc, io, xtok, xs, ident)
        ffn_block(nc, io, xtok, xs, ident)


def shape_constants():
    import numpy as np
    f = np.float32
    inv = (f(1.0) / f(10000.0) ** (np.arange(0, RD, 2, dtype=f) / f(RD))).astype(f)
    fr = np.arange(S, dtype=f)[:, None] * inv[None, :]
    c, s = np.cos(fr), np.sin(fr)
    rope = np.stack([np.concatenate([c, c], 1), np.concatenate([-s, s], 1)], 1).astype(f)
    half = np.arange(0, LD, 2, dtype=f)
    inv = (f(1.0) / f(10000.0) ** (half / f(LD))).astype(f)
    t = np.arange(S, dtype=f)
    fr = t[:, None] * inv[None, :]
    base = (half + f(0.4 * LD)) / f(1.4 * LD)
    power = (t - f(S // 2)) / f(W // 2)
    scale = (base[None, :] ** power[:, None]).astype(f)
    c, s = np.cos(fr), np.sin(fr)
    two = lambda a, b: np.concatenate([a, b], 1)
    q = np.stack([two(c * scale, c * scale), two(-s * scale, s * scale)], 1)
    k = np.stack([two(c / scale, c / scale), two(-s / scale, s / scale)], 1)
    xpos = np.stack([q, k], 1).astype(f)
    i, j = np.arange(P)[:, None], np.arange(KW)[None, :] - W
    seen = (j <= i) & (j >= i - W)
    mask = np.stack([np.where(seen & (j >= 0), 0, MASKED), np.where(seen, 0, MASKED)], 1).astype(f)
    return {"rope": rope, "xpos": xpos, "mask": mask, "ident": np.eye(P, dtype=f)}


def kernel(**inputs):
    import numpy as np
    import concourse.bacc as bacc
    from concourse.bass_utils import run_bass_kernel_spmd

    names = {
        "x": "L0_attn_hidden_states", "wq": "L0_attn_Wq", "wk": "L0_attn_Wk", "wv": "L0_attn_Wv", "wo": "L0_attn_Wo",
        "wqkv": "L0_ffn_wqkv", "qs": "L0_ffn_q_scale", "ks": "L0_ffn_k_scale", "lwo": "L0_ffn_wo",
        "w1": "L0_ffn_w1", "w2": "L0_ffn_w2",
    }
    arrays = {short: np.ascontiguousarray(inputs[name]) for short, name in names.items()}
    cols = np.zeros((LAYERS, P, NCOLS), np.float32)
    b1 = np.asarray(inputs["L0_ffn_b1"])
    for first, offset in ((B1A, 0), (B1G, HID)):
        for i, m in enumerate(HSIZE):
            cols[:, 0:m, first + i] = b1[:, offset + P * i:offset + P * i + m]
    for at, name in ((LNG, "L0_ffn_ln_g"), (LNB, "L0_ffn_ln_b"), (B2, "L0_ffn_b2")):
        cols[:, :, at] = np.asarray(inputs[name])
    arrays["cols"] = cols
    arrays.update(shape_constants())
    nc = bacc.Bacc("TRN2", target_bir_lowering=False, num_devices=1)
    io = {k: nc.dram_tensor("in_" + k, a.shape, mybir.dt.from_np(a.dtype), kind="ExternalInput").ap()
          for k, a in arrays.items()}
    io["out"] = nc.dram_tensor("out_x", (B, S, C), F32, kind="ExternalOutput").ap()
    build(nc, io)
    r = run_bass_kernel_spmd(nc, [{"in_" + k: a for k, a in arrays.items()}], core_ids=[0])
    return r.results[0]["out_x"]
```

```python
from contextlib import ExitStack

import concourse.bass as bass
from concourse import mybir

ALU = mybir.AluOpType
ACT = mybir.ActivationFunctionType
F32 = mybir.dt.float32
F32R = mybir.dt.float32r
BF16 = mybir.dt.bfloat16
I32 = mybir.dt.int32
AX_X = mybir.AxisListType.X

P = 128
B, S, C = 8, 512, 128
TT = S // P
LN_EPS = 1e-5

H, KV, D = 8, 2, 32
G = H // KV
NQK = (H + KV) * D
NQKV = NQK + KV * D
RD = D // 4
SPLIT = 3 * D
SM_SCALE = float(D) ** -0.5

LAYERS, LH, LD, W = 2, 8, 64, 64
INNER = LH * LD
PAIRS = LH // 2
KW = W + P
QK_SCALE = 8.0
MASKED = -1e38
HID = 341
HT = (HID + P - 1) // P
HSIZE = [min(P, HID - P * i) for i in range(HT)]
B1A, B1G, LNG, LNB, B2, NCOLS = 0, HT, 2 * HT, 2 * HT + 1, 2 * HT + 2, 2 * HT + 3
XW = S + 2


class Signal:

    def __init__(self, sem, per, lead=1, unit=1):
        self.sem, self.per, self.lead, self.unit = sem, per, lead, unit

    def at(self, n, k):
        return n * (self.per * self.unit) + (self.lead * self.per + k) * self.unit

    def past(self, n, k, back=1):
        return n * (self.per * self.unit) + ((self.lead - back) * self.per + k) * self.unit


class Chain:

    def __init__(self, engine, sig, n, passed=None):
        self.engine, self.sig, self.n, self.count, self.passed = engine, sig, n, 0, passed

    def add(self, instruction):
        self.count += 1
        instruction.then_inc(self.sig.sem, 1)

    def settle(self):
        self.engine.wait_ge(self.sig.sem, self.sig.at(self.n, self.count))

    def settle_apart(self):
        self.settle()
        self.engine.sem_inc(self.passed, 1)

    def __call__(self, instruction):
        self.add(instruction)
        self.settle()


def rsqrt_step(dve, chain, k, out, x, tmp, least):
    half, y, z = tmp
    chain.settle()
    if k == 0:
        step = dve.tensor_scalar(half, x, least, None, ALU.max)
    elif k == 1:
        step = dve.tensor_scalar(y.bitcast(I32), half.bitcast(I32), 1, None, ALU.logical_shift_right)
    elif k == 2:
        step = dve.tensor_scalar(z.bitcast(I32), y.bitcast(I32), -1.0, 1597463007.0, ALU.mult, ALU.add)
    elif k == 3:
        step = dve.tensor_scalar(half, half, -0.5, None, ALU.mult)
    elif (k - 4) % 3 == 0:
        step = dve.tensor_tensor(y, z, z, ALU.mult)
    elif (k - 4) % 3 == 1:
        step = dve.tensor_tensor(y, y, half, ALU.mult)
    else:
        step = dve.scalar_tensor_tensor(out=out if k == RSQRT_LINKS - 1 else z, in0=y, scalar=1.5, in1=z,
                                        op0=ALU.add, op1=ALU.mult)
    chain.add(step)


RSQRT_LINKS = 4 + 3 * 3


def layernorm_parts(dve, link, src, out, stats, mv, rstd, tmp):
    def statistics():
        for t in range(TT):
            link.add(dve.bn_stats(stats[:, t, :], src[:, t, :]))
        link.settle_apart()
        for t in range(TT):
            link.add(dve.bn_aggr(mv[:, t, :], stats[:, t, :]))

    def deviation(first=0, end=RSQRT_LINKS):
        if first == 0:
            link.settle()
            link.add(dve.tensor_scalar(rstd[:, 0, :], mv[:, :, 1], LN_EPS, None, ALU.add))
        for k in range(first, end):
            rsqrt_step(dve, link, k, rstd[:, 1, :], rstd[:, 0, :], tmp, 1e-30)
        if end == RSQRT_LINKS:
            link.settle()

    def result():
        for t in range(TT):
            link.add(dve.tensor_scalar(out[:, t, :], src[:, t, :], mv[:, t, 0:1], rstd[:, 1, t:t + 1],
                                       ALU.subtract, ALU.mult))
        link.settle_apart()

    return statistics, deviation, result


LAYERNORM_LINKS = 3 * TT + 1 + RSQRT_LINKS


def global_attention_block(nc, io, xtok, xs, ident):
    with ExitStack() as ctx:
        def sb(name, shape, dt=F32):
            return ctx.enter_context(nc.sbuf_tensor(name, shape, dt))

        signals = []

        def signal(name, per, lead=1, unit=1):
            s = Signal(ctx.enter_context(nc.semaphore(name)), per, lead, unit)
            signals.append(s)
            return s

        ps = ctx.enter_context(nc.psum_tensor("ps_a", [P, 8, 512], F32))
        S_BANK, ST_BANK, HEAD_BANK, O_BANK, DEN_BANK, TAIL_BANK = 0, 2, 4, 5, 6, 7
        NST = 2
        FIRST_BANKS = [HEAD_BANK, 0, 1, 2, 3]
        NH = H + KV

        HEAD = [("xT", 0)] + [("qkv", t) for t in range(TT)] + [("gate", 0)]
        HEAD += [("turn", H + g) for g in range(KV)] + [("turn", h) for h in range(3)]
        HEAD += [("gate", 1)] + [("turn", h) for h in range(3, H)]
        NP = len(HEAD)
        PIECE = {piece: k for k, piece in enumerate(HEAD)}
        FIRST_TURN = PIECE["turn", H]
        SLOTS = {
            0: [(0, ("turn", 6)), None, (0, ("turn", 7))],
            1: [(1, ("xT", 0)), (1, ("qkv", 0)), (1, ("qkv", 1))],
            2: [(1, ("qkv", 2)), (1, ("qkv", 3)), (1, ("gate", 0))],
            3: [None, None, None],
            4: [None, (1, ("turn", H)), (1, ("turn", H + 1))],
            5: [(1, ("turn", 0)), (1, ("turn", 1)), (1, ("turn", 2))],
            6: [(1, ("gate", 1)), (1, ("turn", 3)), None],
            7: [(1, ("turn", 4)), (1, ("turn", 5)), None],
        }
        WEIGHTED = {5: (0, 0, [0]), 6: (0, 0, [1]), 7: (0, 0, [2]), 0: (1, 0, [3]),
                    1: (1, 1, [0, 1]), 2: (1, 1, [2]), 3: (1, 1, [3])}
        OUT_COPY = {0: 0, 3: 1}

        wqkv = sb("a_wqkv", [P, NQKV])
        wgate = sb("a_wgate", [P, H * D])
        wo = sb("a_wo", [P, KV, C])
        rope = sb("a_rope", [P, TT, 2, RD])
        ones32 = sb("a_ones32", [P, D])
        xstage = sb("a_xstage", [P, TT, C])
        xT = [sb(f"a_xT{p}", [P, S]) for p in range(2)]
        qkv = [sb(f"a_qkv{p}", [P, TT, NQKV]) for p in range(2)]
        rot = sb("a_rot", [P, 2, TT, NH, RD])
        q3 = sb("a_q3", [P, TT, NH, SPLIT])
        qT = sb("a_qT", [P, H, S], F32R)
        kT = [sb(f"a_kT{p}", [P, KV, S], F32R) for p in range(2)]
        v = sb("a_v", [P, KV, TT, D])
        nmax = sb("a_nmax", [P, H, TT])
        probs = sb("a_probs", [P, KV, G, TT, S])
        gate = [sb(f"a_gate{p}", [P, KV, S]) for p in range(2)]
        tanh = sb("a_tanh", [P, S])
        outs = sb("a_outs", [P, S])
        dens = sb("a_dens", [P, S])
        rden = sb("a_rden", [P, S])
        og = sb("a_og", [P, KV, S])
        y = sb("a_y", [P, TT, C])
        stats = sb("a_stats", [P, TT, 6])
        mv = sb("a_mv", [P, TT, 2])
        rstd = sb("a_rstd", [P, 2, TT])
        small = [sb(f"a_small{i}", [P, TT])[:] for i in range(3)]

        consts_in = ctx.enter_context(nc.semaphore("consts_in"))
        xtok_in = ctx.enter_context(nc.semaphore("xtok_in"))
        consts_set = ctx.enter_context(nc.semaphore("consts_set"))
        passed = ctx.enter_context(nc.semaphore("passed"))
        x_loaded = signal("x_loaded", 1, unit=16)
        head_done = signal("head_done", NP)
        head_read = signal("head_read", NP)
        gate_ready = signal("gate_ready", KV)
        split_link = signal("split_link", 7)
        dup_ready = signal("dup_ready", 2)
        s_done = signal("s_done", 2 * H)
        max_ready = signal("max_ready", 2 * H)
        mrow_done = signal("mrow_done", H)
        mrow_ready = signal("mrow_ready", H)
        st_done = signal("st_done", H * TT)
        exp_ready = signal("exp_ready", H * TT)
        pv_done = signal("pv_done", KV * TT)
        outs_ready = signal("outs_ready", 2 * KV)
        rden_link = signal("rden_link", 3 * KV, lead=2)
        v_ready = signal("v_ready", KV, lead=2)
        og_ready = signal("og_ready", KV)
        wo_done = signal("wo_done", 1)
        norm_link = signal("norm_link", 2 + LAYERNORM_LINKS)
        xn_turned = signal("xn_turned", 1)
        xs_ready = signal("xs_ready", 2)

        def over_batches(engine, head, batch, drain):
            head(0, 0)
            batch(0, 0, cur=True, nxt=True, prev=False)
            with engine.Fori(0, (B - 2) // 2) as m:
                for i in range(2):
                    batch(m * 2 + (i + 1), 1 - i, cur=True, nxt=True, prev=True)
            batch(B - 1, 1, cur=True, nxt=False, prev=True)
            drain(B, 0, cur=False, nxt=False, prev=True)

        def before(n, p, j, cur, prev):
            return (n, p, j - 1, cur) if j else (n - 1, 1 - p, H - 1, prev)

        def slot_piece(n, p, j, slot, cur, nxt):
            if SLOTS[j][slot] is None:
                return None
            ahead, piece = SLOTS[j][slot]
            if not (nxt if ahead else cur):
                return None
            return n + ahead, (p + ahead) % 2, piece

        def first_pieces():
            return [x for x in HEAD if x not in (("turn", 6), ("turn", 7))]

        block = ctx.enter_context(nc.Block())

        @block.sync
        def _(sp):
            for s in signals:
                sp.sem_inc(s.sem, s.lead * s.per * s.unit)
            x_dram = io["x"].rearrange("b (t p) c -> b p t c", p=P)
            sp.dma_start(xstage[:], x_dram[0]).then_inc(x_loaded.sem, 16)
            sp.dma_start(ident[:], io["ident"]).then_inc(consts_in, 16)
            sp.dma_start(wqkv[:, 0:H * D], io["wq"][:, 0:H * D]).then_inc(consts_in, 16)
            sp.dma_start(wqkv[:, H * D:NQK], io["wk"]).then_inc(consts_in, 16)
            sp.dma_start(wqkv[:, NQK:NQKV], io["wv"]).then_inc(consts_in, 16)
            sp.dma_start(wgate[:], io["wq"][:, H * D:2 * H * D]).then_inc(consts_in, 16)
            sp.dma_start(rope[:], io["rope"].rearrange("(t p) a r -> p t a r", p=P)).then_inc(consts_in, 16)
            sp.dma_start(wo[:], io["wo"].rearrange("(g p) c -> p g c", p=P)).then_inc(consts_in, 16)
            sp.dma_start(xtok[:], io["x"].rearrange("b (t p) c -> p (b t) c", p=P)).then_inc(xtok_in, 16)
            with sp.Fori(0, B - 1) as m:
                sp.wait_ge(head_done.sem, head_done.at(m, 1))
                sp.dma_start(xstage[:], x_dram[m + 1]).then_inc(x_loaded.sem, 16)

        CONSTS = 7 * 16
        SETS = 4

        @block.gpsimd
        def _(pool):
            pool.memset(ones32[:], 1.0).then_inc(consts_set, 1)
            for p in range(2):
                pool.wait_ge(consts_set, p + 1)
                pool.memset(kT[p][SPLIT:SPLIT + 1, :, :].bitcast(F32), 1.0).then_inc(consts_set, 1)
            pool.wait_ge(consts_set, SETS - 1)
            pool.memset(xs[:], 0.0).then_inc(consts_set, 1)

            def duplicate(n):
                pool.wait_ge(split_link.sem, split_link.at(n, 5))
                pool.sem_inc(passed, 1)
                pool.tensor_copy(q3[:, :, 0:H, D:2 * D], q3[:, :, 0:H, 0:D]).then_inc(dup_ready.sem, 1)
                pool.tensor_copy(q3[:, :, H:NH, 2 * D:], q3[:, :, H:NH, 0:D]).then_inc(dup_ready.sem, 1)

            def gated(n, g):
                pool.wait_ge(rden_link.sem, rden_link.at(n, 3 * g + 3))
                pool.wait_ge(wo_done.sem, wo_done.past(n, 1))
                pool.tensor_tensor(og[:, g, :], outs[:], rden[:], ALU.mult).then_inc(og_ready.sem, 1)

            def keep_v(n, p, g):
                pool.wait_ge(pv_done.sem, pv_done.past(n, (g + 1) * TT))
                pool.wait_ge(head_read.sem, head_read.at(n, PIECE["qkv", TT - 1] + 1))
                pool.sem_inc(passed, 1)
                pool.tensor_copy(v[:, g], qkv[p][:, :, NQK + g * D:NQK + (g + 1) * D]).then_inc(v_ready.sem, 1)

            def batch(n, p, cur, nxt, prev):
                if prev:
                    gated(n - 1, 0)
                if cur:
                    keep_v(n, p, 0)
                if nxt:
                    duplicate(n + 1)
                if prev:
                    gated(n - 1, 1)
                if cur:
                    keep_v(n, p, 1)

            over_batches(pool, lambda n, p: duplicate(n), batch, batch)

        @block.tensor
        def _(pe):
            pe.wait_ge(consts_in, CONSTS)
            pe.wait_ge(consts_set, SETS)

            def piece(n, p, name, banks=(HEAD_BANK,)):
                kind, i = name
                k = PIECE[name]
                bank = ps[:, banks[k % len(banks)], :]
                last_one = k - len(banks)
                if last_one >= 0:
                    pe.wait_ge(head_read.sem, head_read.at(n, last_one + 1))
                    if HEAD[last_one][0] == "gate":
                        pe.wait_ge(gate_ready.sem, gate_ready.at(n, HEAD[last_one][1] + 1))
                elif k == 0:
                    pe.wait_ge(head_read.sem, head_read.past(n, NP))
                if kind == "xT":
                    pe.wait_ge(x_loaded.sem, x_loaded.at(n, 1))
                    for t in range(TT):
                        last = pe.transpose(bank[:, t * P:(t + 1) * P], xstage[:, t, :], ident[:])
                elif kind == "qkv":
                    if i == 0:
                        pe.wait_ge(head_read.sem, head_read.at(n, 1))
                    last = pe.matmul(bank[:, 0:NQKV], xT[p][:, i * P:(i + 1) * P], wqkv[:], start=True, stop=True)
                elif kind == "gate":
                    last = pe.matmul(bank, wgate[:, i * P:(i + 1) * P], xT[p][:], start=True, stop=True)
                else:
                    if k == FIRST_TURN:
                        pe.wait_ge(split_link.sem, split_link.at(n, split_link.per))
                        pe.wait_ge(dup_ready.sem, dup_ready.at(n, 2))
                    for t in range(TT):
                        last = pe.transpose(bank[0:SPLIT, t * P:(t + 1) * P], q3[:, t, i, :], ident[:])
                last.then_inc(head_done.sem, 1)

            def scores(n, p, h, half):
                if h == 0 and half == 0:
                    pe.wait_ge(head_read.sem, head_read.at(n, PIECE["turn", 5] + 1))
                    pe.wait_ge(max_ready.sem, max_ready.past(n, 2 * H))
                else:
                    pe.wait_ge(max_ready.sem, max_ready.at(n, 2 * h + half))
                if h >= 6 and half == 0:
                    pe.wait_ge(head_read.sem, head_read.at(n, PIECE["turn", h] + 1))
                for t in range(2):
                    q = (2 * half + t) * P
                    last = pe.matmul(ps[:, S_BANK + t, :], qT[0:SPLIT, h, q:q + P], kT[p][0:SPLIT, h // G, :],
                                     start=True, stop=True)
                last.then_inc(s_done.sem, 1)

            def max_row(n, h):
                pe.wait_ge(max_ready.sem, max_ready.at(n, 2 * h + 2))
                pe.wait_ge(mrow_ready.sem, mrow_ready.at(n, h))
                if h == 5:
                    pe.wait_ge(norm_link.sem, norm_link.past(n, 1))
                if h == 7:
                    pe.wait_ge(xs_ready.sem, xs_ready.past(n, 2))
                for t in range(TT):
                    last = pe.transpose(ps[0:1, TAIL_BANK, t * P:(t + 1) * P], nmax[:, h, t:t + 1], ident[:])
                last.then_inc(mrow_done.sem, 1)

            def scores_t(n, p, h, tiles):
                if tiles[0] == 0:
                    pe.wait_ge(mrow_ready.sem, mrow_ready.at(n, h + 1))
                for t in tiles:
                    i = h * TT + t
                    pe.wait_ge(exp_ready.sem, exp_ready.at(n, i - NST + 1))
                    pe.matmul(ps[:, ST_BANK + i % NST, :], kT[p][0:SPLIT + 1, h // G, t * P:(t + 1) * P],
                              qT[0:SPLIT + 1, h, :], start=True, stop=True).then_inc(st_done.sem, 1)

            def weighted(n, p, g, t):
                if t == 0:
                    pe.wait_ge(exp_ready.sem, exp_ready.at(n, (g + 1) * G * TT))
                    pe.wait_ge(outs_ready.sem, outs_ready.at(n, 2 * g))
                    pe.wait_ge(v_ready.sem, v_ready.at(n, g + 1))
                for j in range(G):
                    pe.matmul(ps[D * j:D * (j + 1), O_BANK, :], v[:, g, t, :],
                              probs[:, g, j, t, :], start=(t == 0), stop=(t == TT - 1))
                for j in range(G):
                    last = pe.matmul(ps[D * j:D * (j + 1), DEN_BANK, :], ones32[:],
                                     probs[:, g, j, t, :], start=(t == 0), stop=(t == TT - 1))
                last.then_inc(pv_done.sem, 1)

            def out_project(n):
                pe.wait_ge(og_ready.sem, og_ready.at(n, KV))
                pe.wait_ge(mrow_ready.sem, mrow_ready.at(n + 1, 5) if n_has_next(n) else mrow_ready.at(n, H))
                for t in range(TT):
                    for g in range(KV):
                        last = pe.matmul(ps[:, TAIL_BANK, t * C:(t + 1) * C], og[:, g, t * P:(t + 1) * P], wo[:, g, :],
                                         start=(g == 0), stop=(g == KV - 1))
                last.then_inc(wo_done.sem, 1)

            def n_has_next(n):
                return not (isinstance(n, int) and n == B - 1)

            def turn_result(n):
                pe.wait_ge(norm_link.sem, norm_link.at(n, norm_link.per - 1))
                pe.wait_ge(mrow_ready.sem, mrow_ready.at(n + 1, 7) if n_has_next(n) else mrow_ready.at(n, H))
                for t in range(TT):
                    last = pe.transpose(ps[:, TAIL_BANK, t * P:(t + 1) * P], y[:, t, :], ident[:])
                last.then_inc(xn_turned.sem, 1)

            def batch(n, p, cur, nxt, prev):
                for j in range(H):
                    bn, bp, bh, has_before = before(n, p, j, cur, prev)

                    def slot(i):
                        if x := slot_piece(n, p, j, i, cur, nxt):
                            piece(*x)

                    if cur:
                        scores(n, p, j, 0)
                    if has_before:
                        max_row(bn, bh)
                    slot(0)
                    if j in WEIGHTED:
                        back, g, tiles = WEIGHTED[j]
                        if prev if back else cur:
                            for t in tiles:
                                weighted(n - back, (p + back) % 2, g, t)
                    if has_before:
                        scores_t(bn, bp, bh, [0, 1])
                    if cur:
                        scores(n, p, j, 1)
                    slot(1)
                    if has_before:
                        scores_t(bn, bp, bh, [2, 3])
                    slot(2)
                    if j == 5 and prev:
                        out_project(n - 1)
                    if j == 7 and prev:
                        turn_result(n - 1)

            def head(n, p):
                for name in first_pieces():
                    piece(n, p, name, FIRST_BANKS)
                pe.wait_ge(head_read.sem, head_read.at(n, len(first_pieces())))
                pe.wait_ge(gate_ready.sem, gate_ready.at(n, KV))
                pe.sem_inc(passed, 1)

            over_batches(pe, head, batch, batch)

        @block.scalar
        def _(act):
            def read_piece(n, p, name, banks=(HEAD_BANK,)):
                kind, i = name
                k = PIECE[name]
                act.wait_ge(head_done.sem, head_done.at(n, k + 1))
                bank = ps[:, banks[k % len(banks)], :]
                if kind == "xT":
                    out = act.copy(xT[p][:], bank)
                elif kind == "qkv":
                    act.wait_ge(v_ready.sem, v_ready.past(n, KV, 2))
                    out = act.copy(qkv[p][:, i, :], bank[:, 0:NQKV])
                elif kind == "gate":
                    act.wait_ge(gate_ready.sem, gate_ready.at(n, i))
                    out = act.activation(tanh[:], bank, ACT.Tanh, scale=0.5)
                elif i >= H:
                    out = act.copy(kT[p][0:SPLIT, i - H, :], bank[0:SPLIT, :])
                else:
                    act.wait_ge(st_done.sem, st_done.past(n, (i + 1) * TT))
                    out = act.copy(qT[0:SPLIT, i, :], bank[0:SPLIT, :])
                out.then_inc(head_read.sem, 1)

            def exponentials(n, h, tiles):
                for t in tiles:
                    i = h * TT + t
                    act.wait_ge(st_done.sem, st_done.at(n, i + 1))
                    if h % G == 0 and t == 0:
                        act.wait_ge(pv_done.sem, pv_done.past(n, (h // G + 1) * TT))
                    act.activation(probs[:, h // G, h % G, t, :], ps[:, ST_BANK + i % NST, :], ACT.Exp,
                                   scale=SM_SCALE).then_inc(exp_ready.sem, 1)

            def batch(n, p, cur, nxt, prev):
                for j in range(H):
                    bn, bp, bh, has_before = before(n, p, j, cur, prev)

                    def slot(i):
                        if x := slot_piece(n, p, j, i, cur, nxt):
                            read_piece(*x)

                    if has_before:
                        act.wait_ge(mrow_done.sem, mrow_done.at(bn, bh + 1))
                        act.copy(qT[SPLIT:SPLIT + 1, bh, :], ps[0:1, TAIL_BANK, :]).then_inc(mrow_ready.sem, 1)
                    slot(0)
                    if has_before:
                        exponentials(bn, bh, [0, 1])
                    slot(1)
                    if j in OUT_COPY and prev:
                        g = OUT_COPY[j]
                        act.wait_ge(pv_done.sem, pv_done.at(n - 1, (g + 1) * TT))
                        act.wait_ge(og_ready.sem, og_ready.at(n - 1, g))
                        act.copy(dens[:], ps[:, DEN_BANK, :]).then_inc(outs_ready.sem, 1)
                    if has_before:
                        exponentials(bn, bh, [2, 3])
                    if j in OUT_COPY and prev:
                        act.copy(outs[:], ps[:, O_BANK, :]).then_inc(outs_ready.sem, 1)
                    slot(2)
                    if j == 7 and prev:
                        act.wait_ge(xn_turned.sem, xn_turned.at(n - 1, 1))
                        act.copy(xs[0:64, n - 1, 0:S], ps[0:64, TAIL_BANK, :]).then_inc(xs_ready.sem, 1)
                        act.copy(xs[64:P, n - 1, 1:S + 1], ps[64:P, TAIL_BANK, :]).then_inc(xs_ready.sem, 1)

            def head(n, p):
                for name in first_pieces():
                    read_piece(n, p, name, FIRST_BANKS)

            act.wait_ge(consts_set, SETS)
            over_batches(act, head, batch, batch)

        @block.vector
        def _(dve):
            dve.wait_ge(consts_in, CONSTS)
            dve.wait_ge(xtok_in, 16)
            dve.wait_ge(consts_set, SETS)

            def maxima(n, h, half):
                dve.wait_ge(s_done.sem, s_done.at(n, 2 * h + half + 1))
                if half == 0:
                    dve.wait_ge(mrow_done.sem, mrow_done.past(n, h + 1))
                dve.tensor_reduce(nmax[:, h, 2 * half:2 * half + 2], ps[:, S_BANK:S_BANK + 2, :], AX_X,
                                  ALU.max, negate=True).then_inc(max_ready.sem, 1)

            def rotate(n, p, split):
                dve.wait_ge(head_read.sem, head_read.at(n, PIECE["qkv", TT - 1] + 1))
                heads = qkv[p][:, :, 0:NQK].rearrange("p t (h d) -> p t h d", d=D)
                cos = rope[:, :, 0:1, :].to_broadcast([P, TT, NH, RD])
                sin = rope[:, :, 1:2, :].to_broadcast([P, TT, NH, RD])
                hr = RD // 2
                split.add(dve.tensor_tensor(rot[:, 0], heads[:, :, :, 0:RD], cos, ALU.mult))
                split.add(dve.tensor_tensor(rot[:, 1, :, :, 0:hr], heads[:, :, :, hr:RD], sin[:, :, :, 0:hr], ALU.mult))
                split(dve.tensor_tensor(rot[:, 1, :, :, hr:RD], heads[:, :, :, 0:hr], sin[:, :, :, hr:RD], ALU.mult))
                split.add(dve.tensor_tensor(heads[:, :, :, 0:RD], rot[:, 0], rot[:, 1], ALU.add))

            def high_parts(n, p, split):
                dve.wait_ge(head_done.sem, head_done.past(n, NP))
                split.settle()
                split.add(dve.tensor_copy(q3[:, :, :, 0:D].bitcast(F32R),
                                          qkv[p][:, :, 0:NQK].rearrange("p t (h d) -> p t h d", d=D)))

            def low_parts(n, p, split):
                heads = qkv[p][:, :, 0:NQK].rearrange("p t (h d) -> p t h d", d=D)
                split.settle()
                split.add(dve.tensor_tensor(q3[:, :, H:NH, D:2 * D].bitcast(F32R), heads[:, :, H:NH, :],
                                            q3[:, :, H:NH, 0:D], ALU.subtract))
                split.add(dve.tensor_tensor(q3[:, :, 0:H, 2 * D:].bitcast(F32R), heads[:, :, 0:H, :],
                                            q3[:, :, 0:H, 0:D], ALU.subtract))

            def silu(n, p, g, banks=(HEAD_BANK,)):
                dve.wait_ge(head_read.sem, head_read.at(n, PIECE["gate", g] + 1))
                dve.wait_ge(rden_link.sem, rden_link.past(n, 3 * g + 3, 2))
                dve.scalar_tensor_tensor(out=gate[p][:, g, :], in0=tanh[:], scalar=1.0,
                                         in1=ps[:, banks[PIECE["gate", g] % len(banks)], :], op0=ALU.add, op1=ALU.mult).then_inc(gate_ready.sem, 1)

            def reciprocals(n, chain, g, half):
                cols = slice(half * S // 2, (half + 1) * S // 2)
                if half == 0:
                    dve.wait_ge(outs_ready.sem, outs_ready.at(n, 2 * g + 2))
                    dve.wait_ge(og_ready.sem, og_ready.at(n, g))
                chain.add(dve.reciprocal(rden[:, cols], dens[:, cols]))

            def gates(n, p, chain, g):
                chain.settle()
                chain.add(dve.scalar_tensor_tensor(out=rden[:], in0=rden[:], scalar=0.5, in1=gate[p][:, g, :],
                                                   op0=ALU.mult, op1=ALU.mult))

            def residual(n, norm):
                dve.wait_ge(wo_done.sem, wo_done.at(n, 1))
                dve.wait_ge(xn_turned.sem, xn_turned.past(n, 1))
                dve.wait_ge(norm_link.sem, norm_link.past(n, norm_link.per))
                norm(dve.tensor_tensor(y[:], ps[:, TAIL_BANK, :].rearrange("p (t c) -> p t c", c=C),
                                       xtok[:, bass.ds(n * TT, TT), :], ALU.add))

            def batch(n, p, cur, nxt, prev):
                split = Chain(dve, split_link, n + 1, passed)
                rden_chain = Chain(dve, rden_link, n - 1, passed)
                norm = Chain(dve, norm_link, n - 1, passed)
                statistics, deviation, result = layernorm_parts(dve, norm, y, y, stats, mv, rstd, small)
                for j in range(H):
                    for half in range(2):
                        if cur:
                            maxima(n, j, half)
                        if j in (1, 4) and prev:
                            g = (j - 1) // 3
                            reciprocals(n - 1, rden_chain, g, half)
                            if half:
                                gates(n - 1, 1 - p, rden_chain, g)
                        if nxt:
                            if (j, half) == (2, 1):
                                rotate(n + 1, 1 - p, split)
                            if (j, half) == (3, 0):
                                silu(n + 1, 1 - p, 0)
                                high_parts(n + 1, 1 - p, split)
                            if (j, half) == (3, 1):
                                low_parts(n + 1, 1 - p, split)
                            if (j, half) == (6, 0):
                                silu(n + 1, 1 - p, 1)
                        if prev:
                            if (j, half) == (5, 1):
                                residual(n - 1, norm)
                                statistics()
                            if (j, half) == (6, 0):
                                deviation(0, 6)
                            if (j, half) == (6, 1):
                                deviation(6)
                            if (j, half) == (7, 0):
                                result()
                                norm.add(dve.tensor_copy(xtok[:, bass.ds((n - 1) * TT, TT), :], y[:]))

            def head(n, p):
                split = Chain(dve, split_link, n, passed)
                rotate(n, p, split)
                high_parts(n, p, split)
                low_parts(n, p, split)
                for g in range(KV):
                    silu(n, p, g, FIRST_BANKS)

            over_batches(dve, head, batch, batch)


def ffn_block(nc, io, xtok, xs, ident):
    with ExitStack() as ctx:
        def sb(name, shape, dt=F32):
            return ctx.enter_context(nc.sbuf_tensor(name, shape, dt))

        signals = []

        def signal(name, per, lead=1, unit=1):
            s = Signal(ctx.enter_context(nc.semaphore(name)), per, lead, unit)
            signals.append(s)
            return s

        ps = ctx.enter_context(nc.psum_tensor("ps_b", [P, 8, 512], F32))
        PT_BANK, O_BANK, HEAD_BANK = 4, 6, 7
        FIRST_BANKS = [HEAD_BANK, 0, 1, 2, 3]
        NU = PAIRS * TT

        HEAD = [("proj", t, j) for t in range(TT) for j in range(2)] + [("proj", t, 2) for t in range(TT)]
        HEAD += [("turn", j, a) for a in range(PAIRS) for j in (1, 0)]
        NP = len(HEAD)
        PIECE = {piece: k for k, piece in enumerate(HEAD)}
        FIRST_TURN = PIECE["turn", 1, 0]
        LATE = [("turn", 1, PAIRS - 1), ("turn", 0, PAIRS - 1)]
        SLOTS = {0: [(0, x) for x in LATE]}
        for step, slots in ((1, (0, 1)), (2, (2, 3)), (3, (4, 5)), (4, (6, 7)), (5, (8, None)), (6, (9, None)),
                            (7, (10, None)), (8, (11, None))):
            SLOTS[step] = [None if i is None else (1, HEAD[i]) for i in slots]
        SLOTS |= {13 + a: [(1, ("turn", 1, a)), (1, ("turn", 0, a))] for a in range(PAIRS - 1)}
        OUT_STEP = 5
        T_LAG, O_LAG = 3, 5
        COS_STEP, NORM_STEP, ROT_STEP = 2, 6, 3
        NORMS = 4
        SCALE_STEPS = {9: [0], 10: [1], 11: [2, 3]}
        ROTATED = [3 * (k + 1) for k in range(TT)] + [3 * TT + 4 * (k + 1) for k in range(TT)]

        wqkv = sb("b_wqkv", [P, 3 * INNER])
        wo = sb("b_wo", [P, PAIRS, C])
        w1 = sb("c_w1", [P, 2 * HID])
        w2 = sb("c_w2", [P, HT, C])
        cols = sb("c_cols", [P, NCOLS])
        qs = sb("b_qs", [P, 2, LD])
        xpos = sb("b_xpos", [P, TT, 2, 2, LD])
        tab = sb("b_tab", [P, TT, 2, 2, LD])
        mask = sb("b_mask", [P, 2, KW])
        maskb = sb("b_maskb", [P, 2, KW], BF16)
        identb = sb("b_identb", [P, P], BF16)

        hT = sb("b_hT", [P, S])
        qk = sb("b_qk", [P, TT, 2, INNER])
        rot = sb("b_rot", [P, TT, 2, INNER])
        v = [sb(f"b_v{p}", [P, TT + 1, INNER]) for p in range(2)]
        part = sb("b_part", [P, INNER])
        sq = sb("b_sq", [P, 2, INNER])
        ss = sb("b_ss", [P, TT, 2, LH])
        rn = [sb(f"b_rn{p}", [P, TT, 2, LH]) for p in range(2)]
        small = [sb(f"b_small{i}", [P, TT * 2 * LH])[:] for i in range(3)]
        qT = sb("b_qT", [P, PAIRS, S])
        kT = sb("b_kT", [P, PAIRS, W + S])
        NPB = 4
        nmax = sb("b_nmax", [P, NU, 2])
        bias = sb("b_bias", [P, NU, 2])
        probs = sb("b_probs", [P, NPB, 2, 2 * P])
        den = sb("b_den", [P, NU, 2])
        rden = sb("b_rden", [P, NU, 2])
        pT = sb("b_pT", [P, 2, 2, 2, P])
        oT = sb("b_oT", [P, PAIRS, S])

        hc = sb("c_hT", [P, S])
        hn = sb("c_hn", [P, TT, C])
        hg = sb("c_hg", [P, S])
        gelu = sb("c_gelu", [P, HT, S])
        mid = sb("c_mid", [P, HT, S])
        stats = sb("c_stats", [P, TT, 6])
        mv = sb("c_mv", [P, TT, 2])
        rstd = sb("c_rstd", [P, 2, TT])
        lnsmall = [sb(f"c_small{i}", [P, TT])[:] for i in range(3)]

        GROUPS = 2
        GB = B // GROUPS
        DVE_SHARE = 2
        fstats = sb("f_stats", [P, B * TT, 6])
        fmv = sb("f_mv", [P, B * TT, 2])
        frstd = sb("f_rstd", [P, 3, B * TT])
        fsmall = [sb(f"f_small{i}", [P, GB * TT])[:] for i in range(3)]
        GROUP_LINKS = GB + 2 * GB * TT + 2 + RSQRT_LINKS

        BW, CW = 4, 4
        consts_in = ctx.enter_context(nc.semaphore("b_consts_in"))
        consts_set = ctx.enter_context(nc.semaphore("b_consts_set"))
        consts_cast = ctx.enter_context(nc.semaphore("b_consts_cast"))
        passed = ctx.enter_context(nc.semaphore("b_passed"))
        bw_loaded = signal("bw_loaded", BW, unit=16)
        cw_loaded = signal("cw_loaded", CW, unit=16)
        tab_ready = signal("tab_ready", 6)
        h_ready = signal("h_ready", 1)
        head_done = signal("b_head_done", NP)
        proj_read = signal("b_proj_read", 3 * TT)
        sq_ready = signal("sq_ready", 2 * TT)
        ss_ready = signal("ss_ready", 2 * TT)
        rn_link = signal("rn_link", RSQRT_LINKS + 1)
        cos_ready = signal("cos_ready", 2 * TT)
        rot_link = signal("rot_link", 7 * TT)
        kT_ready = signal("b_kT_ready", PAIRS)
        qT_ready = signal("b_qT_ready", PAIRS)
        s_done = signal("b_s_done", NU)
        max_ready = signal("b_max_ready", NU)
        bias_ready = signal("b_bias_ready", NU)
        exp_ready = signal("b_exp_ready", 2 * NU)
        rden_ready = signal("b_rden_ready", NU)
        norm_ready = signal("b_norm_ready", 2 * NU)
        p_turned = signal("b_p_turned", NU)
        pT_ready = signal("b_pT_ready", NU)
        pv_done = signal("b_pv_done", NU, lead=2)
        oT_ready = signal("b_oT_ready", PAIRS)
        wo_done = signal("b_wo_done", 1)
        x_added = signal("b_x_added", 2, lead=2)
        hc_ready = signal("c_h_ready", 1)
        hc_turned = signal("c_h_turned", 1)
        ln_link = signal("c_ln_link", LAYERNORM_LINKS)
        hn_turned = signal("c_hn_turned", 1)
        hg_ready = signal("c_hg_ready", 1)
        up_done = signal("c_up_done", 2 * HT)
        gelu_ready = signal("c_gelu_ready", HT)
        mid_ready = signal("c_mid_ready", HT)
        down_done = signal("c_down_done", 1)
        x_out = signal("c_x_out", 2, lead=B)
        f_turned = signal("f_turned", B)
        f_link = signal("f_link", GROUPS * GROUP_LINKS)
        f_normed = signal("f_normed", (B - DVE_SHARE) * TT)
        f_normed_too = signal("f_normed_too", DVE_SHARE * TT)
        f_stored = signal("f_stored", B, unit=16)

        def over_batches(engine, l, head, batch, drain):
            n0 = l * B
            head(n0, 0, 0)
            batch(n0, 0, 0, cur=True, nxt=True, prev=False)
            with engine.Fori(0, (B - 2) // 2) as m:
                for i in range(2):
                    b = m * 2 + (i + 1)
                    batch(n0 + b, b, 1 - i, cur=True, nxt=True, prev=True)
            batch(n0 + B - 1, B - 1, 1, cur=True, nxt=False, prev=True)
            drain(n0 + B, B, 0, cur=False, nxt=False, prev=True)

        def lagged(n, p, u, lag, cur, prev):
            return (n, p, u - lag, cur) if u >= lag else (n - 1, 1 - p, u - lag + NU, prev)

        def slot_pieces(n, p, u, cur, nxt):
            return [[(n + x[0], (p + x[0]) % 2, x[1])] if x and (nxt if x[0] else cur) else []
                    for x in SLOTS.get(u, [None, None])]

        early = [x for x in HEAD if x not in LATE]

        def over_ffn(engine, l, first, batch):
            n0 = l * B
            first(n0)
            with engine.Fori(0, B - 2) as b:
                batch(n0 + b, b, left=2)
            for left in (1, 0):
                batch(n0 + (B - 1 - left), B - 1 - left, left)

        block = ctx.enter_context(nc.Block())

        @block.sync
        def _(sp):
            for s in signals:
                sp.sem_inc(s.sem, s.lead * s.per * s.unit)
            sp.dma_start(xpos[:], io["xpos"].rearrange("(t p) a b d -> p t a b d", p=P)).then_inc(consts_in, 16)
            sp.dma_start(mask[:], io["mask"]).then_inc(consts_in, 16)
            with sp.Fori(0, LAYERS) as l:
                sp.wait_ge(wo_done.sem, wo_done.at(l * B - 1, 1))
                sp.wait_ge(tab_ready.sem, tab_ready.past(l, 6))
                sp.dma_start(wqkv[:], io["wqkv"][l]).then_inc(bw_loaded.sem, 16)
                sp.dma_start(wo[:], io["lwo"][l].rearrange("(a p) c -> p a c", p=P)).then_inc(bw_loaded.sem, 16)
                sp.dma_start(qs[:, 0, :], io["qs"][bass.ds(l, 1), :].to_broadcast([P, LD])).then_inc(bw_loaded.sem, 16)
                sp.dma_start(qs[:, 1, :], io["ks"][bass.ds(l, 1), :].to_broadcast([P, LD])).then_inc(bw_loaded.sem, 16)
                sp.wait_ge(x_out.sem, x_out.at(l * B - 1, 2))
                sp.dma_start(w1[:], io["w1"][l]).then_inc(cw_loaded.sem, 16)
                sp.dma_start(w2[:, 0:2, :], io["w2"][l, 0:2 * P].rearrange("(a p) c -> p a c", p=P)).then_inc(cw_loaded.sem, 16)
                sp.dma_start(w2[0:HSIZE[2], 2, :], io["w2"][l, 2 * P:HID]).then_inc(cw_loaded.sem, 16)
                sp.dma_start(cols[:], io["cols"][l]).then_inc(cw_loaded.sem, 16)
            out = io["out"].rearrange("b (t p) c -> b p t c", p=P)
            for n in range(B):
                if n < B - DVE_SHARE:
                    sp.wait_ge(f_normed.sem, f_normed.at(0, (n + 1) * TT))
                else:
                    sp.wait_ge(f_normed_too.sem, f_normed_too.at(0, (n + 1 - (B - DVE_SHARE)) * TT))
                sp.dma_start(out[n], xtok[:, n * TT:(n + 1) * TT, :]).then_inc(f_stored.sem, 16)
            sp.wait_ge(f_stored.sem, f_stored.at(0, B))

        @block.gpsimd
        def _(pool):
            for p in range(2):
                pool.memset(v[p][:, 0, :], 0.0).then_inc(consts_set, 1)
            pool.memset(kT[:, :, 0:W], 0.0).then_inc(consts_set, 1)
            pool.memset(probs[:], 0.0).then_inc(consts_set, 1)
            pool.wait_ge(consts_in, 32)
            pool.tensor_copy(maskb[:], mask[:]).then_inc(consts_cast, 1)
            pool.tensor_copy(identb[:], ident[:]).then_inc(consts_cast, 1)

            def head_start(n, b):
                pool.wait_ge(head_done.sem, head_done.past(n, 3 * TT))
                pool.wait_ge(x_out.sem, x_out.past(n, 2, B))
                pool.sem_inc(passed, 1)
                pool.tensor_copy(hT[:], xs[:, b, 0:S]).then_inc(h_ready.sem, 1)

            def cosines(n, k):
                j, t = k // TT, k % TT
                pool.wait_ge(proj_read.sem, proj_read.at(n, PIECE["proj", t, j] + 1))
                x, r = (a[:, t, j, :].rearrange("p (h d) -> p h d", d=LD) for a in (qk, rot))
                pool.wait_ge(rot_link.sem, rot_link.past(n, ROTATED[k]))
                pool.tensor_tensor(r, x, tab[:, t, j, 0:1, :].to_broadcast([P, LH, LD]),
                                   ALU.mult).then_inc(cos_ready.sem, 1)

            def normalise(n, u):
                pool.wait_ge(rden_ready.sem, rden_ready.at(n, u + 1))
                pool.sem_inc(passed, 1)
                for r in range(2):
                    p_u = probs[:, u % NPB, r, W:W + KW]
                    pool.tensor_scalar(p_u, p_u, rden[:, u, r:r + 1], None, ALU.mult).then_inc(norm_ready.sem, 1)

            def batch(n, b, p, cur, nxt, prev):
                for u in range(NU):
                    if nxt and u == 0:
                        head_start(n + 1, b + 1)
                    if nxt and COS_STEP <= u < COS_STEP + 2 * TT:
                        cosines(n + 1, u - COS_STEP)
                    ln, lp, lu, there = lagged(n, p, u, 1, cur, prev)
                    if there:
                        normalise(ln, lu)

            def head(n, b, p):
                for k in range(2 * TT):
                    cosines(n, k)

            def drain(n, b, p, cur, nxt, prev):
                normalise(n - 1, NU - 1)

            def copy_h(n, b):
                pool.wait_ge(x_added.sem, x_added.at(n, 2))
                pool.wait_ge(hc_turned.sem, hc_turned.past(n, 1))
                pool.sem_inc(passed, 1)
                pool.tensor_copy(hc[:], xs[:, b, 0:S]).then_inc(hc_ready.sem, 1)

            with pool.Fori(0, LAYERS) as l:
                head_start(l * B, 0)
                pool.wait_ge(bw_loaded.sem, bw_loaded.at(l, BW))
                pool.wait_ge(rot_link.sem, rot_link.at(l * B - 1, rot_link.per))
                hd = LD // 2
                for j in range(2):
                    s = qs[:, j:j + 1, :].to_broadcast([P, TT, LD])
                    pool.tensor_tensor(tab[:, :, j, 0, :], xpos[:, :, j, 0, :], s, ALU.mult).then_inc(tab_ready.sem, 1)
                    pool.tensor_tensor(tab[:, :, j, 1, 0:hd], xpos[:, :, j, 1, 0:hd], s[:, :, hd:LD], ALU.mult).then_inc(tab_ready.sem, 1)
                    pool.tensor_tensor(tab[:, :, j, 1, hd:LD], xpos[:, :, j, 1, hd:LD], s[:, :, 0:hd], ALU.mult).then_inc(tab_ready.sem, 1)
                pool.wait_ge(tab_ready.sem, tab_ready.at(l, 6))
                pool.sem_inc(passed, 1)
                over_batches(pool, l, head, batch, drain)
                with pool.Fori(0, B) as b:
                    copy_h(l * B + b, b)

        SETS = 4

        @block.tensor
        def _(pe):
            pe.wait_ge(consts_cast, 2)
            pe.wait_ge(consts_set, SETS)

            def head_bank_free(n, k):
                kind, i, j = HEAD[k - 1]
                if kind == "proj":
                    pe.wait_ge(proj_read.sem, proj_read.at(n, k))
                elif i:
                    pe.wait_ge(kT_ready.sem, kT_ready.at(n, j + 1))
                else:
                    pe.wait_ge(qT_ready.sem, qT_ready.at(n, j + 1))

            def piece(n, p, name, banks=(HEAD_BANK,)):
                kind, i, j = name
                k = PIECE[name]
                bank = ps[:, banks[k % len(banks)], :]
                if k >= len(banks):
                    head_bank_free(n, k + 1 - len(banks))
                if k == 0:
                    pe.wait_ge(h_ready.sem, h_ready.at(n, 1))
                    pe.wait_ge(qT_ready.sem, qT_ready.past(n, PAIRS))
                if kind == "proj":
                    if name in FIRST_AFTER_OUT:
                        pe.wait_ge(x_added.sem, x_added.past(n, 2, 2))
                    last = pe.matmul(bank, hT[:, i * P:(i + 1) * P], wqkv[:, j * INNER:(j + 1) * INNER],
                                     start=True, stop=True)
                else:
                    if k == FIRST_TURN:
                        pe.wait_ge(rot_link.sem, rot_link.at(n, rot_link.per))
                    for t in range(TT):
                        last = pe.transpose(bank[:, t * P:(t + 1) * P], qk[:, t, i, j * P:(j + 1) * P], ident[:])
                last.then_inc(head_done.sem, 1)

            def scores(n, p, u):
                a, t = u // TT, u % TT
                if t == 0:
                    pe.wait_ge(kT_ready.sem, kT_ready.at(n, a + 1))
                    pe.wait_ge(qT_ready.sem, qT_ready.at(n, a + 1))
                if u >= 2:
                    pe.wait_ge(exp_ready.sem, exp_ready.at(n, 2 * (u - 2) + 2))
                else:
                    pe.wait_ge(exp_ready.sem, exp_ready.past(n, 2 * (u - 2 + NU) + 2))
                for r in range(2):
                    rows = slice(LD * r, LD * r + LD)
                    pe.matmul(ps[:, 2 * (u % 2) + r, 0:KW], qT[rows, a, t * P:(t + 1) * P], kT[rows, a, t * P:t * P + KW],
                              start=True, stop=False)
                for r in range(2):
                    last = pe.matmul(ps[:, 2 * (u % 2) + r, 0:KW], identb[:], maskb[:, 0 if t == 0 else 1, :],
                                     start=False, stop=True)
                last.then_inc(s_done.sem, 1)

            def turn_probs(n, u):
                pe.wait_ge(norm_ready.sem, norm_ready.at(n, 2 * u + 2))
                if u >= 2:
                    pe.wait_ge(pT_ready.sem, pT_ready.at(n, u - 1))
                else:
                    pe.wait_ge(pT_ready.sem, pT_ready.past(n, u - 1 + NU))
                for r in range(2):
                    for m in range(2):
                        last = pe.transpose(ps[:, PT_BANK + u % 2, (2 * r + m) * P:(2 * r + m + 1) * P],
                                            probs[:, u % NPB, r, m * P:(m + 1) * P], ident[:])
                last.then_inc(p_turned.sem, 1)

            def weighted(n, p, u):
                a, t = u // TT, u % TT
                pe.wait_ge(pT_ready.sem, pT_ready.at(n, u + 1))
                if t == 0:
                    pe.wait_ge(oT_ready.sem, oT_ready.at(n, a))
                for r in range(2):
                    h = 2 * a + r
                    pe.matmul(ps[LD * r:LD * r + LD, O_BANK, t * P:(t + 1) * P], v[p][:, t + 1, h * LD:(h + 1) * LD],
                              pT[:, u % 2, r, 1, :], start=True, stop=False)
                for r in range(2):
                    h = 2 * a + r
                    last = pe.matmul(ps[LD * r:LD * r + LD, O_BANK, t * P:(t + 1) * P], v[p][W:P, t, h * LD:(h + 1) * LD],
                                     pT[W:P, u % 2, r, 0, :], start=False, stop=True)
                last.then_inc(pv_done.sem, 1)

            def out_project(n, after):
                pe.wait_ge(oT_ready.sem, oT_ready.at(n, PAIRS))
                if after is not None:
                    head_bank_free(n + 2, after)
                else:
                    pe.wait_ge(qT_ready.sem, qT_ready.at(n, PAIRS))
                for a in range(PAIRS):
                    last = pe.matmul(ps[:, HEAD_BANK, :], wo[:, a, :], oT[:, a, :], start=(a == 0), stop=(a == PAIRS - 1))
                last.then_inc(wo_done.sem, 1)

            FIRST_AFTER_OUT = [next(x[1] for x in SLOTS[OUT_STEP + 1] if x)]

            def batch(n, b, p, cur, nxt, prev):
                for u in range(NU):
                    pieces = slot_pieces(n, p, u, cur, nxt)
                    if cur:
                        scores(n, p, u)
                    for x in pieces[0]:
                        piece(*x)
                    ln, lp, lu, there = lagged(n, p, u, T_LAG, cur, prev)
                    if there:
                        turn_probs(ln, lu)
                    ln, lp, lu, there = lagged(n, p, u, O_LAG, cur, prev)
                    if there:
                        weighted(ln, lp, lu)
                    for x in pieces[1]:
                        piece(*x)
                    if u == OUT_STEP and prev:
                        out_project(n - 1, PIECE[[x[1] for x in SLOTS[OUT_STEP] if x][-1]] + 1 if nxt else None)

            def head(n, b, p):
                for x in early:
                    piece(n, p, x, FIRST_BANKS)
                pe.wait_ge(kT_ready.sem, kT_ready.at(n, PAIRS - 1))
                pe.wait_ge(qT_ready.sem, qT_ready.at(n, PAIRS - 1))
                pe.sem_inc(passed, 1)

            def drain(n, b, p, cur, nxt, prev):
                for u in range(OUT_STEP + 1):
                    if u < T_LAG:
                        turn_probs(n - 1, u - T_LAG + NU)
                    if u < O_LAG:
                        weighted(n - 1, 1 - p, u - O_LAG + NU)
                out_project(n - 1, None)

            def turn_h(n):
                pe.wait_ge(hc_ready.sem, hc_ready.at(n, 1))
                pe.wait_ge(hg_ready.sem, hg_ready.past(n, 1))
                for t in range(TT):
                    last = pe.transpose(ps[:, 0, t * P:(t + 1) * P], hc[:, t * P:(t + 1) * P], ident[:])
                last.then_inc(hc_turned.sem, 1)

            def turn_hn(n):
                pe.wait_ge(ln_link.sem, ln_link.at(n, ln_link.per))
                for t in range(TT):
                    last = pe.transpose(ps[:, 0, t * P:(t + 1) * P], hn[:, t, :], ident[:])
                last.then_inc(hn_turned.sem, 1)

            def up(n):
                pe.wait_ge(hg_ready.sem, hg_ready.at(n, 1))
                for i in range(HT):
                    m = HSIZE[i]
                    for a in (1, 0):
                        bank = 1 + 2 * i + a
                        pe.wait_ge(mid_ready.sem, mid_ready.past(n, i + 1))
                        pe.matmul(ps[0:m, bank, :], w1[:, a * HID + i * P:a * HID + i * P + m], hg[:],
                                  start=True, stop=True).then_inc(up_done.sem, 1)

            def down(n, i):
                m = HSIZE[i]
                pe.wait_ge(mid_ready.sem, mid_ready.at(n, i + 1))
                if i == 0:
                    pe.wait_ge(x_out.sem, x_out.past(n, 2))
                last = pe.matmul(ps[:, 7, :], w2[0:m, i, :], mid[0:m, i, :], start=(i == 0), stop=(i == HT - 1))
                if i == HT - 1:
                    last.then_inc(down_done.sem, 1)

            def ffn_first(n):
                turn_h(n)
                turn_hn(n)
                turn_h(n + 1)

            def ffn(n, b, left):
                up(n)
                down(n, 0)
                if left:
                    turn_hn(n + 1)
                down(n, 1)
                if left == 2:
                    turn_h(n + 2)
                down(n, 2)

            with pe.Fori(0, LAYERS) as l:
                pe.wait_ge(bw_loaded.sem, bw_loaded.at(l, BW))
                pe.wait_ge(mid_ready.sem, mid_ready.at(l * B - 1, HT))
                pe.wait_ge(hg_ready.sem, hg_ready.at(l * B - 1, 1))
                pe.wait_ge(x_out.sem, x_out.at(l * B - 1, 2))
                pe.sem_inc(passed, 1)
                over_batches(pe, l, head, batch, drain)
                pe.wait_ge(cw_loaded.sem, cw_loaded.at(l, CW))
                pe.wait_ge(x_added.sem, x_added.at(l * B + B - 1, 2))
                pe.wait_ge(exp_ready.sem, exp_ready.at(l * B + B - 1, 2 * NU))
                pe.wait_ge(pT_ready.sem, pT_ready.at(l * B + B - 1, NU))
                pe.wait_ge(oT_ready.sem, oT_ready.at(l * B + B - 1, PAIRS))
                pe.sem_inc(passed, 1)
                over_ffn(pe, l, ffn_first, ffn)
            pe.wait_ge(mid_ready.sem, mid_ready.at(LAYERS * B - 1, HT))
            pe.wait_ge(hg_ready.sem, hg_ready.at(LAYERS * B - 1, 1))
            pe.wait_ge(x_out.sem, x_out.at(LAYERS * B - 1, 2))
            for n in range(B):
                for t in range(TT):
                    for r in range(2):
                        half = slice(64 * r, 64 * r + 64)
                        last = pe.matmul(ps[:, n, t * C + 64 * r:t * C + 64 * r + 64],
                                         xs[:, n, r + t * P:r + (t + 1) * P], ident[:, half], start=True, stop=True)
                last.then_inc(f_turned.sem, 1)

        @block.scalar
        def _(act):
            act.wait_ge(consts_set, SETS)

            def read_piece(n, p, name, banks=(HEAD_BANK,)):
                kind, i, j = name
                bank = ps[:, banks[PIECE[name] % len(banks)], :]
                if kind == "turn":
                    if i:
                        act.wait_ge(head_done.sem, head_done.at(n, PIECE[name] + 1))
                        act.wait_ge(s_done.sem, s_done.past(n, (j + 1) * TT))
                        act.copy(kT[:, j, W:], bank).then_inc(kT_ready.sem, 1)
                    return
                act.wait_ge(head_done.sem, head_done.at(n, PIECE[name] + 1))
                if j < 2:
                    k = 2 * i + j
                    act.wait_ge(ss_ready.sem, ss_ready.at(n, k - 1))
                    act.copy(qk[:, i, j, :], bank).then_inc(proj_read.sem, 1)
                    act.wait_ge(proj_read.sem, proj_read.at(n, k + 1))
                    act.activation(sq[:, j, :], qk[:, i, j, :], ACT.Square).then_inc(sq_ready.sem, 1)
                else:
                    act.wait_ge(pv_done.sem, pv_done.past(n, NU, 2))
                    act.copy(v[p][:, i + 1, :], bank).then_inc(proj_read.sem, 1)

            def exponentials(n, p, u):
                a, t = u // TT, u % TT
                act.wait_ge(bias_ready.sem, bias_ready.at(n, u + 1))
                if u >= NPB:
                    act.wait_ge(p_turned.sem, p_turned.at(n, u - NPB + 1))
                else:
                    act.wait_ge(p_turned.sem, p_turned.past(n, u - NPB + 1 + NU))
                for r in range(2):
                    h = 2 * a + r
                    act.activation(probs[:, u % NPB, r, W:W + KW], ps[:, 2 * (u % 2) + r, 0:KW],
                                   ACT.Exp, scale=rn[p][:, t, 0, h:h + 1], bias=bias[:, u, r:r + 1],
                                   accum_out=den[:, u, r:r + 1]).then_inc(exp_ready.sem, 1)

            def copy_pT(n, u):
                act.wait_ge(p_turned.sem, p_turned.at(n, u + 1))
                if u >= 2:
                    act.wait_ge(pv_done.sem, pv_done.at(n, u - 1))
                else:
                    act.wait_ge(pv_done.sem, pv_done.past(n, u - 1 + NU))
                act.copy(pT[:, u % 2].rearrange("p r m q -> p (r m q)"), ps[:, PT_BANK + u % 2, :]).then_inc(pT_ready.sem, 1)

            def copy_oT(n, a):
                act.wait_ge(pv_done.sem, pv_done.at(n, (a + 1) * TT))
                act.wait_ge(wo_done.sem, wo_done.past(n, 1))
                act.copy(oT[:, a, :], ps[:, O_BANK, :]).then_inc(oT_ready.sem, 1)

            def step_tail(n, p, u, cur, prev):
                ln, lp, lu, there = lagged(n, p, u, T_LAG, cur, prev)
                if there:
                    copy_pT(ln, lu)
                ln, lp, lu, there = lagged(n, p, u, O_LAG, cur, prev)
                if there and lu % TT == TT - 1:
                    copy_oT(ln, lu // TT)

            def batch(n, b, p, cur, nxt, prev):
                for u in range(NU):
                    pieces = slot_pieces(n, p, u, cur, nxt)
                    for x in pieces[0]:
                        read_piece(*x)
                    if cur:
                        exponentials(n, p, u)
                    for x in pieces[1]:
                        read_piece(*x)
                    step_tail(n, p, u, cur, prev)

            def head(n, b, p):
                for x in early:
                    read_piece(n, p, x, FIRST_BANKS)

            def drain(n, b, p, cur, nxt, prev):
                for u in range(O_LAG):
                    step_tail(n, p, u, cur, prev)

            def scale_h(n):
                act.wait_ge(hn_turned.sem, hn_turned.at(n, 1))
                act.wait_ge(up_done.sem, up_done.past(n, 2 * HT))
                act.activation(hg[:], ps[:, 0, :], ACT.Identity, scale=cols[:, LNG:LNG + 1],
                               bias=cols[:, LNB:LNB + 1]).then_inc(hg_ready.sem, 1)

            def ffn(n, b, left):
                for i in range(HT):
                    m = HSIZE[i]
                    act.wait_ge(up_done.sem, up_done.at(n, 2 * i + 1))
                    act.wait_ge(mid_ready.sem, mid_ready.past(n, i + 1))
                    act.activation(gelu[0:m, i, :], ps[0:m, 2 + 2 * i, :], ACT.Gelu,
                                   bias=cols[0:m, B1G + i:B1G + i + 1]).then_inc(gelu_ready.sem, 1)
                if left:
                    scale_h(n + 1)

            with act.Fori(0, LAYERS) as l:
                over_batches(act, l, head, batch, drain)
                act.wait_ge(cw_loaded.sem, cw_loaded.at(l, CW))
                over_ffn(act, l, scale_h, ffn)
            for g in range(GROUPS):
                act.wait_ge(f_link.sem, f_link.at(0, (g + 1) * GROUP_LINKS))
                for i in range(g * GB * TT, min((g + 1) * GB, B - DVE_SHARE) * TT):
                    act.activation(xtok[:, i, :], xtok[:, i, :], ACT.Identity,
                                   scale=frstd[:, 1, i:i + 1], bias=frstd[:, 2, i:i + 1]).then_inc(f_normed.sem, 1)

        @block.vector
        def _(dve):
            dve.wait_ge(consts_set, SETS)

            def linker(sig, n):
                return Chain(dve, sig, n, passed)

            def squares(n, k):
                t, j = k // 2, k % 2
                dve.wait_ge(sq_ready.sem, sq_ready.at(n, k + 1))
                dve.tensor_reduce(ss[:, t, j, :], sq[:, j, :].rearrange("p (h d) -> p h d", d=LD), AX_X,
                                  ALU.add).then_inc(ss_ready.sem, 1)

            def norms(n, p, link, k):
                if k == 0:
                    dve.wait_ge(ss_ready.sem, ss_ready.at(n, 2 * TT))
                if k < RSQRT_LINKS:
                    rsqrt_step(dve, link, k, rn[p][:].rearrange("p t j h -> p (t j h)"),
                               ss[:].rearrange("p t j h -> p (t j h)"), small, 1e-24)
                elif k == RSQRT_LINKS:
                    link.settle()
                    link.add(dve.tensor_scalar(rn[p][:, :, 0, :], rn[p][:, :, 0, :], QK_SCALE, None, ALU.mult))

            def rotate(n, link, k, between):
                j, t = k // TT, k % TT
                x, r, a = (z.rearrange("p (h d) -> p h d", d=LD) for z in (qk[:, t, j, :], rot[:, t, j, :], part[:]))
                hd = LD // 2
                sin = tab[:, t, j, 1:2, :].to_broadcast([P, LH, LD])
                link.settle()
                dve.wait_ge(proj_read.sem, proj_read.at(n, PIECE["proj", t, j] + 1))
                link.add(dve.tensor_tensor(a[:, :, 0:hd], x[:, :, hd:LD], sin[:, :, 0:hd], ALU.mult))
                link.add(dve.tensor_tensor(a[:, :, hd:LD], x[:, :, 0:hd], sin[:, :, hd:LD], ALU.mult))
                between()
                link.settle()
                dve.wait_ge(cos_ready.sem, cos_ready.at(n, k + 1))
                link.add(dve.tensor_tensor(x, r, a, ALU.add))

            def scale_keys(n, p, link, k):
                t = k - TT
                x = qk[:, t, 1, :].rearrange("p (h d) -> p h d", d=LD)
                nrm = rn[p][:, t, 1, :].rearrange("p (h o) -> p h o", o=1).to_broadcast([P, LH, LD])
                dve.wait_ge(rn_link.sem, rn_link.at(n, RSQRT_LINKS))
                link.settle()
                link.add(dve.tensor_tensor(x, x, nrm, ALU.mult))

            def maxima(n, u):
                dve.wait_ge(s_done.sem, s_done.at(n, u + 1))
                b2 = 2 * (u % 2)
                dve.tensor_reduce(nmax[:, u, :], ps[:, b2:b2 + 2, 0:KW], AX_X, ALU.max, negate=True).then_inc(max_ready.sem, 1)

            def biases(n, p, u):
                a, t = u // TT, u % TT
                dve.wait_ge(max_ready.sem, max_ready.at(n, u + 1))
                dve.wait_ge(rn_link.sem, rn_link.at(n, rn_link.per))
                dve.tensor_tensor(bias[:, u, :], nmax[:, u, :], rn[p][:, t, 0, 2 * a:2 * a + 2], ALU.mult).then_inc(bias_ready.sem, 1)

            def denominators(n, u):
                dve.wait_ge(exp_ready.sem, exp_ready.at(n, 2 * u + 2))
                dve.wait_ge(norm_ready.sem, norm_ready.past(n, 2 * u + 2))
                dve.reciprocal(rden[:, u, :], den[:, u, :]).then_inc(rden_ready.sem, 1)

            def copy_qT(n, a, banks=(HEAD_BANK,)):
                dve.wait_ge(head_done.sem, head_done.at(n, PIECE["turn", 0, a] + 1))
                dve.wait_ge(s_done.sem, s_done.past(n, (a + 1) * TT))
                dve.tensor_copy(qT[:, a, :], ps[:, banks[PIECE["turn", 0, a] % len(banks)], :]).then_inc(qT_ready.sem, 1)

            def add_x(n, b):
                dve.wait_ge(wo_done.sem, wo_done.at(n, 1))
                for r in range(2):
                    x = xs[64 * r:64 * r + 64, b, r:r + S]
                    dve.tensor_tensor(x, ps[64 * r:64 * r + 64, HEAD_BANK, :], x, ALU.add).then_inc(x_added.sem, 1)

            def batch(n, b, p, cur, nxt, prev):
                rn_chain, rot_chain = linker(rn_link, n + 1), linker(rot_link, n + 1)
                for u in range(NU):
                    def norm_step(i):
                        k = (u - NORM_STEP) * NORMS + i
                        if nxt and 0 <= k <= RSQRT_LINKS:
                            norms(n + 1, 1 - p, rn_chain, k)

                    if cur:
                        maxima(n, u)
                    norm_step(0)
                    if cur:
                        biases(n, p, u)
                    norm_step(1)
                    ln, lp, lu, there = lagged(n, p, u, 1, cur, prev)
                    if there:
                        denominators(ln, lu)
                    k = u - ROT_STEP
                    if nxt:
                        for t in SCALE_STEPS.get(u, []):
                            scale_keys(n + 1, 1 - p, rot_chain, TT + t)
                    for xn, xp, (kind, i, j) in sum(slot_pieces(n, p, u, cur, nxt), []):
                        if kind == "proj" and j < 2:
                            squares(xn, 2 * i + j)
                        if kind == "turn" and not i:
                            copy_qT(xn, j)
                    if u == OUT_STEP and prev:
                        add_x(n - 1, b - 1)
                    if nxt and 0 <= k < 2 * TT:
                        rotate(n + 1, rot_chain, k, lambda: norm_step(2))
                    else:
                        norm_step(2)
                    norm_step(3)

            def head(n, b, p):
                rn_chain, rot_chain = linker(rn_link, n), linker(rot_link, n)
                for t in range(TT):
                    squares(n, 2 * t)
                    squares(n, 2 * t + 1)
                    rotate(n, rot_chain, t, lambda: None)
                for k in range(RSQRT_LINKS + 1):
                    norms(n, p, rn_chain, k)
                for t in range(TT):
                    rotate(n, rot_chain, TT + t, lambda: None)
                    scale_keys(n, p, rot_chain, TT + t)
                for a in range(PAIRS - 1):
                    copy_qT(n, a, FIRST_BANKS)

            def drain(n, b, p, cur, nxt, prev):
                denominators(n - 1, NU - 1)
                add_x(n - 1, b - 1)

            def begin_layernorm(n):
                link = linker(ln_link, n)
                statistics, _, _ = layernorm_parts(*layernorm_args(link))
                dve.wait_ge(hc_turned.sem, hc_turned.at(n, 1))
                statistics()

            def end_layernorm(n):
                link = linker(ln_link, n)
                link.count = 2 * TT
                return layernorm_parts(*layernorm_args(link))[1:]

            def layernorm_args(link):
                return (dve, link, ps[:, 0, :].rearrange("p (t c) -> p t c", c=C), hn, stats, mv, rstd, lnsmall)

            def ffn_first(n):
                begin_layernorm(n)
                deviation, result = end_layernorm(n)
                deviation()
                dve.wait_ge(hn_turned.sem, hn_turned.past(n, 1))
                result()
                begin_layernorm(n + 1)

            def gated(n, i):
                m = HSIZE[i]
                dve.wait_ge(gelu_ready.sem, gelu_ready.at(n, i + 1))
                dve.wait_ge(up_done.sem, up_done.at(n, 2 * i + 2))
                dve.wait_ge(down_done.sem, down_done.past(n, 1))
                dve.scalar_tensor_tensor(out=mid[0:m, i, :], in0=ps[0:m, 1 + 2 * i, :], scalar=cols[0:m, B1A + i:B1A + i + 1],
                                         in1=gelu[0:m, i, :], op0=ALU.add, op1=ALU.mult).then_inc(mid_ready.sem, 1)

            def ffn(n, b, left):
                if left:
                    deviation, result = end_layernorm(n + 1)
                    deviation(0, 10)
                gated(n, 0)
                if left:
                    deviation(10)
                    dve.wait_ge(hn_turned.sem, hn_turned.past(n + 1, 1))
                    result()
                for i in range(1, HT):
                    gated(n, i)
                if left == 2:
                    begin_layernorm(n + 2)
                dve.wait_ge(down_done.sem, down_done.at(n, 1))
                dve.wait_ge(hc_ready.sem, hc_ready.at(n, 1))
                for r in range(2):
                    rows = slice(64 * r, 64 * r + 64)
                    x = xs[rows, b, r:r + S]
                    dve.scalar_tensor_tensor(out=x, in0=ps[rows, 7, :], scalar=cols[rows, B2:B2 + 1], in1=x,
                                             op0=ALU.add, op1=ALU.add).then_inc(x_out.sem, 1)

            with dve.Fori(0, LAYERS) as l:
                dve.wait_ge(tab_ready.sem, tab_ready.at(l, 6))
                dve.sem_inc(passed, 1)
                over_batches(dve, l, head, batch, drain)
                over_ffn(dve, l, ffn_first, ffn)
            link = linker(f_link, 0)
            for g in range(GROUPS):
                tiles = range(g * GB * TT, (g + 1) * GB * TT)
                span = slice(tiles[0], tiles[-1] + 1)
                for n in range(g * GB, (g + 1) * GB):
                    x = xtok[:, n * TT:(n + 1) * TT, :]
                    dve.wait_ge(f_turned.sem, f_turned.at(0, n + 1))
                    link(dve.tensor_tensor(x, ps[:, n, :].rearrange("p (t c) -> p t c", c=C), x, ALU.add))
                    for i in range(n * TT, (n + 1) * TT):
                        link.add(dve.bn_stats(fstats[:, i, :], xtok[:, i, :]))
                link.settle_apart()
                for i in tiles:
                    link.add(dve.bn_aggr(fmv[:, i, :], fstats[:, i, :]))
                link.settle()
                link.add(dve.tensor_scalar(frstd[:, 0, span], fmv[:, span, 1], LN_EPS, None, ALU.add))
                for k in range(RSQRT_LINKS):
                    rsqrt_step(dve, link, k, frstd[:, 1, span], frstd[:, 0, span], fsmall, 1e-30)
                link.settle()
                link.add(dve.scalar_tensor_tensor(out=frstd[:, 2, span], in0=fmv[:, span, 0], scalar=-1.0,
                                                  in1=frstd[:, 1, span], op0=ALU.mult, op1=ALU.mult))
            for i in range((B - DVE_SHARE) * TT, B * TT):
                dve.tensor_scalar(xtok[:, i, :], xtok[:, i, :], fmv[:, i, 0:1], frstd[:, 1, i:i + 1],
                                  ALU.subtract, ALU.mult).then_inc(f_normed_too.sem, 1)


def build(nc, io):
    with ExitStack() as ctx:
        ident = ctx.enter_context(nc.sbuf_tensor("ident_sb", [P, P], F32))
        xtok = ctx.enter_context(nc.sbuf_tensor("xtok", [P, B * TT, C], F32))
        xs = ctx.enter_context(nc.sbuf_tensor("xs", [P, B, XW], F32))
        global_attention_block(nc, io, xtok, xs, ident)
        ffn_block(nc, io, xtok, xs, ident)


def shape_constants():
    import numpy as np
    f = np.float32
    inv = (f(1.0) / f(10000.0) ** (np.arange(0, RD, 2, dtype=f) / f(RD))).astype(f)
    fr = np.arange(S, dtype=f)[:, None] * inv[None, :]
    c, s = np.cos(fr), np.sin(fr)
    rope = np.stack([np.concatenate([c, c], 1), np.concatenate([-s, s], 1)], 1).astype(f)
    half = np.arange(0, LD, 2, dtype=f)
    inv = (f(1.0) / f(10000.0) ** (half / f(LD))).astype(f)
    t = np.arange(S, dtype=f)
    fr = t[:, None] * inv[None, :]
    base = (half + f(0.4 * LD)) / f(1.4 * LD)
    power = (t - f(S // 2)) / f(W // 2)
    scale = (base[None, :] ** power[:, None]).astype(f)
    c, s = np.cos(fr), np.sin(fr)
    two = lambda a, b: np.concatenate([a, b], 1)
    q = np.stack([two(c * scale, c * scale), two(-s * scale, s * scale)], 1)
    k = np.stack([two(c / scale, c / scale), two(-s / scale, s / scale)], 1)
    xpos = np.stack([q, k], 1).astype(f)
    i, j = np.arange(P)[:, None], np.arange(KW)[None, :] - W
    seen = (j <= i) & (j >= i - W)
    mask = np.stack([np.where(seen & (j >= 0), 0, MASKED), np.where(seen, 0, MASKED)], 1).astype(f)
    return {"rope": rope, "xpos": xpos, "mask": mask, "ident": np.eye(P, dtype=f)}


def kernel(**inputs):
    import numpy as np
    import concourse.bacc as bacc
    from concourse.bass_utils import run_bass_kernel_spmd

    names = {
        "x": "L0_attn_hidden_states", "wq": "L0_attn_Wq", "wk": "L0_attn_Wk", "wv": "L0_attn_Wv", "wo": "L0_attn_Wo",
        "wqkv": "L0_ffn_wqkv", "qs": "L0_ffn_q_scale", "ks": "L0_ffn_k_scale", "lwo": "L0_ffn_wo",
        "w1": "L0_ffn_w1", "w2": "L0_ffn_w2",
    }
    arrays = {short: np.ascontiguousarray(inputs[name]) for short, name in names.items()}
    cols = np.zeros((LAYERS, P, NCOLS), np.float32)
    b1 = np.asarray(inputs["L0_ffn_b1"])
    for first, offset in ((B1A, 0), (B1G, HID)):
        for i, m in enumerate(HSIZE):
            cols[:, 0:m, first + i] = b1[:, offset + P * i:offset + P * i + m]
    for at, name in ((LNG, "L0_ffn_ln_g"), (LNB, "L0_ffn_ln_b"), (B2, "L0_ffn_b2")):
        cols[:, :, at] = np.asarray(inputs[name])
    arrays["cols"] = cols
    arrays.update(shape_constants())
    nc = bacc.Bacc("TRN2", target_bir_lowering=False, num_devices=1)
    io = {k: nc.dram_tensor("in_" + k, a.shape, mybir.dt.from_np(a.dtype), kind="ExternalInput").ap()
          for k, a in arrays.items()}
    io["out"] = nc.dram_tensor("out_x", (B, S, C), F32, kind="ExternalOutput").ap()
    build(nc, io)
    r = run_bass_kernel_spmd(nc, [{"in_" + k: a for k, a in arrays.items()}], core_ids=[0])
    return r.results[0]["out_x"]
```
